# Optimizing a Trainium2 kernel written in Bass

```python
import numpy as np
import jax
import jax.numpy as jnp

def _softmax(x, axis=-1):
    return jax.nn.softmax(x, axis=axis)

def _gelu(x):
    return jax.nn.gelu(x, approximate=True)

def _silu(x):
    return jax.nn.silu(x)

def _sigmoid(x):
    return jax.nn.sigmoid(x)

def _layernorm(x, axis=-1, eps=1e-05):
    m = jnp.mean(x, axis=axis, keepdims=True)
    v = jnp.var(x, axis=axis, keepdims=True)
    return (x - m) / jnp.sqrt(v + eps)

def _scatter_add(tgt, idx, src, axis=0):
    return tgt.at[idx].add(src)

def _segment_sum(src, seg, n):
    return jax.ops.segment_sum(src, seg, n)
kernel_name = 'mk_seq_postln_d4_jaxref_r8_74a21b'

def setup_inputs(seed: int=0):
    np.random.seed(seed)
    _w = jnp.asarray

    def _L0_attn_setup():
        import math
        import jax, jax.numpy as jnp
        import numpy as np
        EXP_SCALING = 10.0
        KEY_SCALE_MAX = math.log(2 ** 16 - 1)
        key = jax.random.key(seed)
        ks = jax.random.split(key, 5)
        B, T, C, nh = (2, 256, 128, 16)
        x = jax.random.normal(ks[0], (B, T, C), dtype=jnp.float32)
        W_k = jax.random.normal(ks[1], (C, C), dtype=jnp.float32) * 0.02
        W_v = jax.random.normal(ks[2], (C, C), dtype=jnp.float32) * 0.02
        W_c = jax.random.normal(ks[3], (C, C), dtype=jnp.float32) * 0.02
        leaky_key_beta = (jnp.linspace(0.5, 5.0, nh).reshape(1, nh, 1, 1) / EXP_SCALING).astype(jnp.float32)
        key_scale = jnp.ones((1, nh, 1, 1), jnp.float32) / EXP_SCALING
        v_coef = jax.random.uniform(ks[4], (1, nh, 1, 1), dtype=jnp.float32)
        val_scale = jnp.full((1, nh, 1, 1), -0.5 / EXP_SCALING, jnp.float32)
        return dict(x=x, W_k=W_k, W_v=W_v, W_c=W_c, leaky_key_beta=leaky_key_beta, key_scale=key_scale, v_coef=v_coef, val_scale=val_scale)
    _L0_attn_in = _L0_attn_setup()

    def _L0_ffn_setup():
        import jax, jax.numpy as jnp
        import numpy as np
        CAPACITY_FACTOR = 1.0
        key = jax.random.key(seed)
        ks = jax.random.split(key, 5)
        B, S, D, E, F = (2, 256, 128, 8, 512)
        x = jax.random.normal(ks[0], (B, S, D), dtype=jnp.float32)
        Ws = jax.random.normal(ks[1], (D, E), dtype=jnp.float32) * (1.0 / np.sqrt(D))
        bs = jnp.zeros((E,), dtype=jnp.float32)
        W1 = jax.random.normal(ks[2], (E, D, F), dtype=jnp.float32) * (1.0 / np.sqrt(D))
        b1 = jnp.zeros((E, F), dtype=jnp.float32)
        W2 = jax.random.normal(ks[3], (E, F, D), dtype=jnp.float32) * (1.0 / np.sqrt(F))
        b2 = jnp.zeros((E, D), dtype=jnp.float32)
        return {'x': x, 'Ws': Ws, 'bs': bs, 'W1': W1, 'b1': b1, 'W2': W2, 'b2': b2}
    _L0_ffn_in = _L0_ffn_setup()

    def _L1_attn_setup():
        import jax, jax.numpy as jnp
        import numpy as np
        DIM = 128
        HEADS = 16
        DIM_HEAD = 64
        INNER = HEADS * DIM_HEAD
        HALF = DIM_HEAD // 2
        SCALE = DIM_HEAD ** (-0.5)

        def _apply_rope(x):
            n = x.shape[-2]
            theta = 1.0 / 10000.0 ** (jnp.arange(HALF, dtype=jnp.float32) / HALF)
            angles = jnp.arange(n, dtype=x.dtype)[:, None] * theta[None, :]
            cos = jnp.cos(angles)[None, None]
            sin = jnp.sin(angles)[None, None]
            x1, x2 = (x[..., :HALF], x[..., HALF:])
            return jnp.concatenate([x1 * cos - x2 * sin, x1 * sin + x2 * cos], axis=-1)
        key = jax.random.key(seed)
        k1, k2, k3, k4 = jax.random.split(key, 4)
        x = jax.random.normal(k1, (2, 256, DIM), dtype=jnp.float32)
        w_qkv = jax.random.normal(k2, (DIM, 3 * INNER), dtype=jnp.float32) * DIM ** (-0.5)
        w_out = jax.random.normal(k3, (INNER, DIM), dtype=jnp.float32) * INNER ** (-0.5)
        b_out = jax.random.normal(k4, (DIM,), dtype=jnp.float32) * 0.02
        return {'x': x, 'w_qkv': w_qkv, 'w_out': w_out, 'b_out': b_out}
    _L1_attn_in = _L1_attn_setup()

    def _L1_ffn_setup():
        import jax, jax.numpy as jnp
        import numpy as np
        DIM = 128
        DEPTH = 6
        HEADS = 16
        DIM_HEAD = 64
        WINDOW = 32
        INNER = HEADS * DIM_HEAD
        DIM_INNER = int(DIM * 4 * 2 / 3)
        QK_SCALE = 8.0

        def shift_tokens(t):
            a, s = jnp.split(t, 2, -1)
            s = jnp.pad(s, ((0, 0), (1, 0), (0, 0)))[:, :-1]
            return jnp.concatenate([a, s], -1)

        def l2norm(t):
            return t / jnp.maximum(jnp.linalg.norm(t, axis=-1, keepdims=True), 1e-12)

        def rotate_half(x):
            x1, x2 = jnp.split(x, 2, -1)
            return jnp.concatenate([-x2, x1], -1)

        def rotary_tables(n):
            half = jnp.arange(0, DIM_HEAD, 2, dtype=jnp.float32)
            inv_freq = 1.0 / 10000.0 ** (half / DIM_HEAD)
            t = jnp.arange(n, dtype=jnp.float32)
            freqs = t[:, None] * inv_freq[None, :]
            freqs = jnp.concatenate([freqs, freqs], -1)
            base_scale = (half + 0.4 * DIM_HEAD) / (1.4 * DIM_HEAD)
            power = (t - n // 2) / (WINDOW // 2)
            scale = base_scale[None, :] ** power[:, None]
            scale = jnp.concatenate([scale, scale], -1)
            return (freqs, scale)

        def local_attention(q, k, v):
            b, h, n, d = q.shape
            w = WINDOW
            nw = n // w
            bq = q.reshape(b, h, nw, w, d)
            bk = k.reshape(b, h, nw, w, d)
            bv = v.reshape(b, h, nw, w, d)

            def look(t):
                p = jnp.pad(t, ((0, 0), (0, 0), (1, 0), (0, 0), (0, 0)))
                return jnp.concatenate([p[:, :, :nw], p[:, :, 1:]], axis=3)
            bk2, bv2 = (look(bk), look(bv))
            seq = jnp.arange(n).reshape(nw, w)
            seq_p = jnp.pad(seq, ((1, 0), (0, 0)), constant_values=-1)
            jt = jnp.concatenate([seq_p[:nw], seq_p[1:]], axis=1)
            it = seq[:, :, None]
            jb = jt[:, None, :]
            mask = (it < jb) | (it > jb + w) | (jb == -1)
            sim = jnp.einsum('bhwie,bhwje->bhwij', bq, bk2) * QK_SCALE
            sim = jnp.where(mask, -jnp.finfo(sim.dtype).max, sim)
            attn = jax.nn.softmax(sim, -1)
            out = jnp.einsum('bhwij,bhwje->bhwie', attn, bv2)
            return out.reshape(b, h, n, d)

        def attn_layer(x, Wqkv, qs, ksc, Wo):
            b, n, _ = x.shape
            qkv = x @ Wqkv
            q, k, v = jnp.split(qkv, 3, -1)
            sh = lambda t: t.reshape(b, n, HEADS, DIM_HEAD).transpose(0, 2, 1, 3)
            q, k, v = (sh(q), sh(k), sh(v))
            q = l2norm(q) * qs
            k = l2norm(k) * ksc
            freqs, scale = rotary_tables(n)
            cos, sin = (jnp.cos(freqs), jnp.sin(freqs))
            q = q * cos * scale + rotate_half(q) * sin * scale
            inv = 1.0 / scale
            k = k * cos * inv + rotate_half(k) * sin * inv
            out = local_attention(q, k, v)
            out = out.transpose(0, 2, 1, 3).reshape(b, n, INNER)
            return out @ Wo

        def ffn_layer(x, g, bln, W1, b1, W2, b2):
            mu = x.mean(-1, keepdims=True)
            var = ((x - mu) ** 2).mean(-1, keepdims=True)
            xn = (x - mu) / jnp.sqrt(var + 1e-05) * g + bln
            hg = xn @ W1 + b1
            a, gate = jnp.split(hg, 2, -1)
            return a * jax.nn.gelu(gate, approximate=False) @ W2 + b2
        key = jax.random.key(seed)
        ks = jax.random.split(key, 8)
        B, N = (2, 256)
        init = lambda k, shape: jax.random.normal(k, shape, jnp.float32) * 0.02
        return {'x': jax.random.normal(ks[0], (B, N, DIM), jnp.float32), 'Wqkv': init(ks[1], (DEPTH, DIM, 3 * INNER)), 'q_scale': jnp.ones((DEPTH, DIM_HEAD), jnp.float32), 'k_scale': jnp.ones((DEPTH, DIM_HEAD), jnp.float32), 'Wo': init(ks[2], (DEPTH, INNER, DIM)), 'ln_g': jnp.ones((DEPTH, DIM), jnp.float32), 'ln_b': jnp.zeros((DEPTH, DIM), jnp.float32), 'W1': init(ks[3], (DEPTH, DIM, 2 * DIM_INNER)), 'b1': jnp.zeros((DEPTH, 2 * DIM_INNER), jnp.float32), 'W2': init(ks[4], (DEPTH, DIM_INNER, DIM)), 'b2': jnp.zeros((DEPTH, DIM), jnp.float32)}
    _L1_ffn_in = _L1_ffn_setup()

    def _L2_attn_setup():
        import jax, jax.numpy as jnp
        import numpy as np
        import math
        D_MODEL = 128
        D_STATE = 16
        D_CONV = 4
        EXPAND = 2
        D_INNER = EXPAND * D_MODEL
        DT_RANK = math.ceil(D_MODEL / 16)
        BATCH, SEQ = (4, 128)
        DT_MIN, DT_MAX = (0.001, 0.1)

        def _forward(x, W_in, W_conv, b_conv, W_xproj, W_dt, b_dt, A_log, D, W_out):
            b, l, _ = x.shape
            d_inner = W_in.shape[1] // 2
            d_conv = W_conv.shape[-1]
            n = A_log.shape[1]
            r = W_dt.shape[0]
            xz = x @ W_in
            xi, z = jnp.split(xz, 2, axis=-1)
            xi_t = jnp.moveaxis(xi, 1, 2)
            xi_pad = jnp.pad(xi_t, ((0, 0), (0, 0), (d_conv - 1, 0)))
            conv = jax.lax.conv_general_dilated(xi_pad, W_conv, window_strides=(1,), padding='VALID', feature_group_count=d_inner)
            xc = jax.nn.silu(jnp.moveaxis(conv + b_conv[None, :, None], 2, 1))
            dbc = xc @ W_xproj
            delta_lr, B, C = jnp.split(dbc, [r, r + n], axis=-1)
            delta = jax.nn.softplus(delta_lr @ W_dt + b_dt)
            A = -jnp.exp(A_log)
            dA = jnp.exp(delta[..., None] * A)
            dBx = delta[..., None] * B[:, :, None, :] * xc[..., None]

            def step(h, inp):
                dA_t, dBx_t, C_t, x_t = inp
                h = dA_t * h + dBx_t
                y = jnp.einsum('bdn,bn->bd', h, C_t) + D * x_t
                return (h, y)
            h0 = jnp.zeros((b, d_inner, n), x.dtype)
            _, ys = jax.lax.scan(step, h0, (jnp.moveaxis(dA, 1, 0), jnp.moveaxis(dBx, 1, 0), jnp.moveaxis(C, 1, 0), jnp.moveaxis(xc, 1, 0)))
            y = jnp.moveaxis(ys, 0, 1)
            return y * jax.nn.silu(z) @ W_out
        key = jax.random.key(seed)
        ks = jax.random.split(key, 8)
        x = jax.random.normal(ks[0], (BATCH, SEQ, D_MODEL), dtype=jnp.float32)
        W_in = jax.random.normal(ks[1], (D_MODEL, 2 * D_INNER), jnp.float32) * 0.02
        W_conv = jax.random.normal(ks[2], (D_INNER, 1, D_CONV), jnp.float32) * 0.2
        b_conv = jnp.zeros((D_INNER,), jnp.float32)
        W_xproj = jax.random.normal(ks[3], (D_INNER, DT_RANK + 2 * D_STATE), jnp.float32) * 0.02
        dt_init_std = DT_RANK ** (-0.5)
        W_dt = jax.random.uniform(ks[4], (DT_RANK, D_INNER), jnp.float32, -dt_init_std, dt_init_std)
        u = jax.random.uniform(ks[5], (D_INNER,), jnp.float32)
        dt = jnp.clip(jnp.exp(u * (math.log(DT_MAX) - math.log(DT_MIN)) + math.log(DT_MIN)), DT_MIN, None)
        b_dt = dt + jnp.log(-jnp.expm1(-dt))
        A_log = jnp.log(jnp.tile(jnp.arange(1, D_STATE + 1, dtype=jnp.float32)[None, :], (D_INNER, 1)))
        D = jnp.ones((D_INNER,), jnp.float32)
        W_out = jax.random.normal(ks[6], (D_INNER, D_MODEL), jnp.float32) * 0.02
        return {'x': x, 'W_in': W_in, 'W_conv': W_conv, 'b_conv': b_conv, 'W_xproj': W_xproj, 'W_dt': W_dt, 'b_dt': b_dt, 'A_log': A_log, 'D': D, 'W_out': W_out}
    _L2_attn_in = _L2_attn_setup()

    def _L2_ffn_setup():
        import jax, jax.numpy as jnp
        import numpy as np
        DIM = 128

        def _reference_tuple_inner(x, W_r, W_k, W_v, mu_r, mu_k):
            B, T, C = x.shape
            x_prev = jnp.concatenate([jnp.zeros((B, 1, C), x.dtype), x[:, :-1, :]], axis=1)
            xr = mu_r * x + (1.0 - mu_r) * x_prev
            xk = mu_k * x + (1.0 - mu_k) * x_prev
            r = jax.nn.sigmoid(jnp.einsum('btc,dc->btd', xr, W_r))
            k = jnp.einsum('btc,dc->btd', xk, W_k)
            k_act = jnp.square(jax.nn.relu(k))
            out = r * jnp.einsum('btc,dc->btd', k_act, W_v)
            new_state = x[:, -1, :]
            return (out, new_state)
        key = jax.random.key(seed)
        ks = jax.random.split(key, 6)
        B, T, C = (8, 256, DIM)
        x = jax.random.normal(ks[0], (B, T, C), dtype=jnp.float32)
        s = 1.0 / np.sqrt(C)
        W_r = jax.random.uniform(ks[1], (C, C), jnp.float32, -s, s)
        W_k = jax.random.uniform(ks[2], (C, C), jnp.float32, -s, s)
        W_v = jax.random.uniform(ks[3], (C, C), jnp.float32, -s, s)
        mu_r = jax.random.uniform(ks[4], (C,), jnp.float32)
        mu_k = jax.random.uniform(ks[5], (C,), jnp.float32)
        return {'x': x, 'W_r': W_r, 'W_k': W_k, 'W_v': W_v, 'mu_r': mu_r, 'mu_k': mu_k}
    _L2_ffn_in = _L2_ffn_setup()

    def _L3_attn_setup():
        import jax, jax.numpy as jnp
        import numpy as np
        B, S, D = (4, 256, 128)

        def _xavier(key, shape):
            bound = float(np.sqrt(6.0 / (shape[0] + shape[1])))
            return jax.random.uniform(key, shape, dtype=jnp.float32, minval=-bound, maxval=bound)
        key = jax.random.key(seed)
        k0, k1, k2, k3 = jax.random.split(key, 4)
        return {'embeddings': jax.random.normal(k0, (B, S, D), dtype=jnp.float32), 'W_Q': _xavier(k1, (D, D)), 'W_K': _xavier(k2, (D, D)), 'W_V': _xavier(k3, (D, D))}
    _L3_attn_in = _L3_attn_setup()

    def _L3_ffn_setup():
        import jax, jax.numpy as jnp
        import numpy as np
        BLOCK = 16
        _GRID = jnp.array([0.0, 0.5, 1.0, 1.5, 2.0, 3.0, 4.0, 6.0], dtype=jnp.float32)
        _MID = jnp.array([0.25, 0.75, 1.25, 1.75, 2.5, 3.5, 5.0], dtype=jnp.float32)

        def fp4_quant_dequant(x):
            shape = x.shape
            xb = x.reshape(shape[:-1] + (shape[-1] // BLOCK, BLOCK))
            scale = jnp.max(jnp.abs(xb), axis=-1, keepdims=True) / 6.0
            scale = jnp.maximum(scale, jnp.float32(1e-12))
            xn = xb / scale
            idx = jnp.searchsorted(_MID, jnp.abs(xn))
            q = _GRID[idx] * jnp.sign(xn) * scale
            return q.reshape(shape)

        def fp4_linear(x, w):
            xq = fp4_quant_dequant(x)
            wq = fp4_quant_dequant(w)
            return jnp.einsum('bsk,nk->bsn', xq, wq)
        key = jax.random.key(seed)
        k1, k2, k3, k4 = jax.random.split(key, 4)
        H, I = (128, 352)
        x = jax.random.normal(k1, (4, 512, H), dtype=jnp.float32)
        w_gate = jax.random.normal(k2, (I, H), dtype=jnp.float32) * 0.02
        w_up = jax.random.normal(k3, (I, H), dtype=jnp.float32) * 0.02
        w_down = jax.random.normal(k4, (H, I), dtype=jnp.float32) * 0.02
        return {'x': x, 'w_gate': w_gate, 'w_up': w_up, 'w_down': w_down}
    _L3_ffn_in = _L3_ffn_setup()
    _d = {'L0_attn_x': _L0_attn_in['x'], 'L0_attn_W_k': _L0_attn_in['W_k'], 'L0_attn_W_v': _L0_attn_in['W_v'], 'L0_attn_W_c': _L0_attn_in['W_c'], 'L0_attn_leaky_key_beta': _L0_attn_in['leaky_key_beta'], 'L0_attn_key_scale': _L0_attn_in['key_scale'], 'L0_attn_v_coef': _L0_attn_in['v_coef'], 'L0_attn_val_scale': _L0_attn_in['val_scale'], 'L0_ffn_Ws': _L0_ffn_in['Ws'], 'L0_ffn_bs': _L0_ffn_in['bs'], 'L0_ffn_W1': _L0_ffn_in['W1'], 'L0_ffn_b1': _L0_ffn_in['b1'], 'L0_ffn_W2': _L0_ffn_in['W2'], 'L0_ffn_b2': _L0_ffn_in['b2'], 'L1_attn_w_qkv': _L1_attn_in['w_qkv'], 'L1_attn_w_out': _L1_attn_in['w_out'], 'L1_attn_b_out': _L1_attn_in['b_out'], 'L1_ffn_Wqkv': _L1_ffn_in['Wqkv'], 'L1_ffn_q_scale': _L1_ffn_in['q_scale'], 'L1_ffn_k_scale': _L1_ffn_in['k_scale'], 'L1_ffn_Wo': _L1_ffn_in['Wo'], 'L1_ffn_ln_g': _L1_ffn_in['ln_g'], 'L1_ffn_ln_b': _L1_ffn_in['ln_b'], 'L1_ffn_W1': _L1_ffn_in['W1'], 'L1_ffn_b1': _L1_ffn_in['b1'], 'L1_ffn_W2': _L1_ffn_in['W2'], 'L1_ffn_b2': _L1_ffn_in['b2'], 'L2_attn_W_in': _L2_attn_in['W_in'], 'L2_attn_W_conv': _L2_attn_in['W_conv'], 'L2_attn_b_conv': _L2_attn_in['b_conv'], 'L2_attn_W_xproj': _L2_attn_in['W_xproj'], 'L2_attn_W_dt': _L2_attn_in['W_dt'], 'L2_attn_b_dt': _L2_attn_in['b_dt'], 'L2_attn_A_log': _L2_attn_in['A_log'], 'L2_attn_D': _L2_attn_in['D'], 'L2_attn_W_out': _L2_attn_in['W_out'], 'L2_ffn_W_r': _L2_ffn_in['W_r'], 'L2_ffn_W_k': _L2_ffn_in['W_k'], 'L2_ffn_W_v': _L2_ffn_in['W_v'], 'L2_ffn_mu_r': _L2_ffn_in['mu_r'], 'L2_ffn_mu_k': _L2_ffn_in['mu_k'], 'L3_attn_W_Q': _L3_attn_in['W_Q'], 'L3_attn_W_K': _L3_attn_in['W_K'], 'L3_attn_W_V': _L3_attn_in['W_V'], 'L3_ffn_w_gate': _L3_ffn_in['w_gate'], 'L3_ffn_w_up': _L3_ffn_in['w_up'], 'L3_ffn_w_down': _L3_ffn_in['w_down']}
    _x0 = _d['L0_attn_x']
    _d['L0_attn_x'] = jax.random.normal(jax.random.fold_in(jax.random.key(seed), 1), (1, 2048, 128), dtype=_x0.dtype)
    del _x0
    return _d

def reference(L0_attn_x, L0_attn_W_k, L0_attn_W_v, L0_attn_W_c, L0_attn_leaky_key_beta, L0_attn_key_scale, L0_attn_v_coef, L0_attn_val_scale, L0_ffn_Ws, L0_ffn_bs, L0_ffn_W1, L0_ffn_b1, L0_ffn_W2, L0_ffn_b2, L1_attn_w_qkv, L1_attn_w_out, L1_attn_b_out, L1_ffn_Wqkv, L1_ffn_q_scale, L1_ffn_k_scale, L1_ffn_Wo, L1_ffn_ln_g, L1_ffn_ln_b, L1_ffn_W1, L1_ffn_b1, L1_ffn_W2, L1_ffn_b2, L2_attn_W_in, L2_attn_W_conv, L2_attn_b_conv, L2_attn_W_xproj, L2_attn_W_dt, L2_attn_b_dt, L2_attn_A_log, L2_attn_D, L2_attn_W_out, L2_ffn_W_r, L2_ffn_W_k, L2_ffn_W_v, L2_ffn_mu_r, L2_ffn_mu_k, L3_attn_W_Q, L3_attn_W_K, L3_attn_W_V, L3_ffn_w_gate, L3_ffn_w_up, L3_ffn_w_down):

    def _L0_attn_ref(x, W_k, W_v, W_c, leaky_key_beta, key_scale, v_coef, val_scale):
        import math
        import jax, jax.numpy as jnp
        import numpy as np
        EXP_SCALING = 10.0
        KEY_SCALE_MAX = math.log(2 ** 16 - 1)
        B, T, C = x.shape
        nh = leaky_key_beta.shape[1]
        hs = C // nh
        k = (x @ W_k.T).reshape(B, T, nh, hs).transpose(0, 2, 1, 3)
        t = jnp.arange(T)
        dec = t[:, None] - t[None, :]
        causal = dec >= 0
        dec_f = jnp.where(causal, dec, 0).astype(x.dtype)
        beta = jnp.abs(leaky_key_beta).reshape(nh, 1, 1) * EXP_SCALING
        coef = jnp.where(causal[None], jnp.exp(-dec_f[None] * beta), 0.0)
        k = jnp.einsum('hij,bhjd->bhid', coef, k)
        k = k / (jnp.linalg.norm(k, axis=-1, keepdims=True) + 1e-10)
        k = k * jnp.exp(jnp.minimum(EXP_SCALING * key_scale, KEY_SCALE_MAX))
        v = (x @ W_v.T).reshape(B, T, nh, hs).transpose(0, 2, 1, 3)
        v_shift = jnp.concatenate([v[:, :, 1:], jnp.zeros_like(v[:, :, :1])], axis=2)
        v = (1.0 - v_coef) * v_shift + v_coef * v
        v = v / (jnp.linalg.norm(v, axis=-1, keepdims=True) + 1e-10)
        v = v * jnp.exp(EXP_SCALING * val_scale)
        q = k[:, :, 1:]
        att = jnp.einsum('bhqd,bhkd->bhqk', q, k)
        mask = t[None, :] <= t[:T - 1, None]
        att = jnp.where(mask[None, None], att, -jnp.inf)
        att = jax.nn.softmax(att, axis=-1)
        y1 = jnp.einsum('bhqk,bhkd->bhqd', att, v)
        y = jnp.concatenate([jnp.zeros_like(y1[:, :, :1]), y1], axis=2)
        y = y.transpose(0, 2, 1, 3).reshape(B, T, C)
        return y @ W_c.T

    def _L0_ffn_ref(x, Ws, bs, W1, b1, W2, b2):
        import jax, jax.numpy as jnp
        import numpy as np
        CAPACITY_FACTOR = 1.0
        B, S, D = x.shape
        E = Ws.shape[1]
        N = B * S
        k = int(CAPACITY_FACTOR * N / E)
        xf = x.reshape(N, D)
        route_prob = jax.nn.softmax(xf @ Ws + bs, axis=-1).T
        route_vals, routes = jax.lax.top_k(route_prob, k)
        xin = xf[routes]
        h = jax.nn.gelu(jnp.einsum('ekd,edf->ekf', xin, W1) + b1[:, None, :])
        out = jnp.einsum('ekf,efd->ekd', h, W2) + b2[:, None, :]
        out = out * route_vals[..., None]
        final = jnp.zeros((N, D), dtype=x.dtype).at[routes.reshape(-1)].add(out.reshape(-1, D))
        return final.reshape(B, S, D)

    def _L1_attn_ref(x, w_qkv, w_out, b_out):
        import jax, jax.numpy as jnp
        import numpy as np
        DIM = 128
        HEADS = 16
        DIM_HEAD = 64
        INNER = HEADS * DIM_HEAD
        HALF = DIM_HEAD // 2
        SCALE = DIM_HEAD ** (-0.5)

        def _apply_rope(x):
            n = x.shape[-2]
            theta = 1.0 / 10000.0 ** (jnp.arange(HALF, dtype=jnp.float32) / HALF)
            angles = jnp.arange(n, dtype=x.dtype)[:, None] * theta[None, :]
            cos = jnp.cos(angles)[None, None]
            sin = jnp.sin(angles)[None, None]
            x1, x2 = (x[..., :HALF], x[..., HALF:])
            return jnp.concatenate([x1 * cos - x2 * sin, x1 * sin + x2 * cos], axis=-1)
        b, n, _ = x.shape
        qkv = x @ w_qkv
        qkv = qkv.reshape(b, n, 3, HEADS, DIM_HEAD)
        qkv = jnp.transpose(qkv, (2, 0, 3, 1, 4))
        q, k, v = (qkv[0], qkv[1], qkv[2])
        q = _apply_rope(q)
        k = _apply_rope(k)
        scores = jnp.einsum('bhnd,bhmd->bhnm', q, k) * SCALE
        attn = jax.nn.softmax(scores, axis=-1)
        out = jnp.einsum('bhnm,bhmd->bhnd', attn, v)
        out = jnp.transpose(out, (0, 2, 1, 3)).reshape(b, n, INNER)
        return out @ w_out + b_out

    def _L1_ffn_ref(x, Wqkv, q_scale, k_scale, Wo, ln_g, ln_b, W1, b1, W2, b2):
        import jax, jax.numpy as jnp
        import numpy as np
        DIM = 128
        DEPTH = 6
        HEADS = 16
        DIM_HEAD = 64
        WINDOW = 32
        INNER = HEADS * DIM_HEAD
        DIM_INNER = int(DIM * 4 * 2 / 3)
        QK_SCALE = 8.0

        def shift_tokens(t):
            a, s = jnp.split(t, 2, -1)
            s = jnp.pad(s, ((0, 0), (1, 0), (0, 0)))[:, :-1]
            return jnp.concatenate([a, s], -1)

        def l2norm(t):
            return t / jnp.maximum(jnp.linalg.norm(t, axis=-1, keepdims=True), 1e-12)

        def rotate_half(x):
            x1, x2 = jnp.split(x, 2, -1)
            return jnp.concatenate([-x2, x1], -1)

        def rotary_tables(n):
            half = jnp.arange(0, DIM_HEAD, 2, dtype=jnp.float32)
            inv_freq = 1.0 / 10000.0 ** (half / DIM_HEAD)
            t = jnp.arange(n, dtype=jnp.float32)
            freqs = t[:, None] * inv_freq[None, :]
            freqs = jnp.concatenate([freqs, freqs], -1)
            base_scale = (half + 0.4 * DIM_HEAD) / (1.4 * DIM_HEAD)
            power = (t - n // 2) / (WINDOW // 2)
            scale = base_scale[None, :] ** power[:, None]
            scale = jnp.concatenate([scale, scale], -1)
            return (freqs, scale)

        def local_attention(q, k, v):
            b, h, n, d = q.shape
            w = WINDOW
            nw = n // w
            bq = q.reshape(b, h, nw, w, d)
            bk = k.reshape(b, h, nw, w, d)
            bv = v.reshape(b, h, nw, w, d)

            def look(t):
                p = jnp.pad(t, ((0, 0), (0, 0), (1, 0), (0, 0), (0, 0)))
                return jnp.concatenate([p[:, :, :nw], p[:, :, 1:]], axis=3)
            bk2, bv2 = (look(bk), look(bv))
            seq = jnp.arange(n).reshape(nw, w)
            seq_p = jnp.pad(seq, ((1, 0), (0, 0)), constant_values=-1)
            jt = jnp.concatenate([seq_p[:nw], seq_p[1:]], axis=1)
            it = seq[:, :, None]
            jb = jt[:, None, :]
            mask = (it < jb) | (it > jb + w) | (jb == -1)
            sim = jnp.einsum('bhwie,bhwje->bhwij', bq, bk2) * QK_SCALE
            sim = jnp.where(mask, -jnp.finfo(sim.dtype).max, sim)
            attn = jax.nn.softmax(sim, -1)
            out = jnp.einsum('bhwij,bhwje->bhwie', attn, bv2)
            return out.reshape(b, h, n, d)

        def attn_layer(x, Wqkv, qs, ksc, Wo):
            b, n, _ = x.shape
            qkv = x @ Wqkv
            q, k, v = jnp.split(qkv, 3, -1)
            sh = lambda t: t.reshape(b, n, HEADS, DIM_HEAD).transpose(0, 2, 1, 3)
            q, k, v = (sh(q), sh(k), sh(v))
            q = l2norm(q) * qs
            k = l2norm(k) * ksc
            freqs, scale = rotary_tables(n)
            cos, sin = (jnp.cos(freqs), jnp.sin(freqs))
            q = q * cos * scale + rotate_half(q) * sin * scale
            inv = 1.0 / scale
            k = k * cos * inv + rotate_half(k) * sin * inv
            out = local_attention(q, k, v)
            out = out.transpose(0, 2, 1, 3).reshape(b, n, INNER)
            return out @ Wo

        def ffn_layer(x, g, bln, W1, b1, W2, b2):
            mu = x.mean(-1, keepdims=True)
            var = ((x - mu) ** 2).mean(-1, keepdims=True)
            xn = (x - mu) / jnp.sqrt(var + 1e-05) * g + bln
            hg = xn @ W1 + b1
            a, gate = jnp.split(hg, 2, -1)
            return a * jax.nn.gelu(gate, approximate=False) @ W2 + b2
        for i in range(DEPTH):
            x = attn_layer(shift_tokens(x), Wqkv[i], q_scale[i], k_scale[i], Wo[i]) + x
            x = ffn_layer(shift_tokens(x), ln_g[i], ln_b[i], W1[i], b1[i], W2[i], b2[i]) + x
        return x

    def _L2_attn_ref(x, W_in, W_conv, b_conv, W_xproj, W_dt, b_dt, A_log, D, W_out):
        import jax, jax.numpy as jnp
        import numpy as np
        import math
        D_MODEL = 128
        D_STATE = 16
        D_CONV = 4
        EXPAND = 2
        D_INNER = EXPAND * D_MODEL
        DT_RANK = math.ceil(D_MODEL / 16)
        BATCH, SEQ = (4, 128)
        DT_MIN, DT_MAX = (0.001, 0.1)

        def _forward(x, W_in, W_conv, b_conv, W_xproj, W_dt, b_dt, A_log, D, W_out):
            b, l, _ = x.shape
            d_inner = W_in.shape[1] // 2
            d_conv = W_conv.shape[-1]
            n = A_log.shape[1]
            r = W_dt.shape[0]
            xz = x @ W_in
            xi, z = jnp.split(xz, 2, axis=-1)
            xi_t = jnp.moveaxis(xi, 1, 2)
            xi_pad = jnp.pad(xi_t, ((0, 0), (0, 0), (d_conv - 1, 0)))
            conv = jax.lax.conv_general_dilated(xi_pad, W_conv, window_strides=(1,), padding='VALID', feature_group_count=d_inner)
            xc = jax.nn.silu(jnp.moveaxis(conv + b_conv[None, :, None], 2, 1))
            dbc = xc @ W_xproj
            delta_lr, B, C = jnp.split(dbc, [r, r + n], axis=-1)
            delta = jax.nn.softplus(delta_lr @ W_dt + b_dt)
            A = -jnp.exp(A_log)
            dA = jnp.exp(delta[..., None] * A)
            dBx = delta[..., None] * B[:, :, None, :] * xc[..., None]

            def step(h, inp):
                dA_t, dBx_t, C_t, x_t = inp
                h = dA_t * h + dBx_t
                y = jnp.einsum('bdn,bn->bd', h, C_t) + D * x_t
                return (h, y)
            h0 = jnp.zeros((b, d_inner, n), x.dtype)
            _, ys = jax.lax.scan(step, h0, (jnp.moveaxis(dA, 1, 0), jnp.moveaxis(dBx, 1, 0), jnp.moveaxis(C, 1, 0), jnp.moveaxis(xc, 1, 0)))
            y = jnp.moveaxis(ys, 0, 1)
            return y * jax.nn.silu(z) @ W_out
        return _forward(x, W_in, W_conv, b_conv, W_xproj, W_dt, b_dt, A_log, D, W_out)

    def _L2_ffn_ref(x, W_r, W_k, W_v, mu_r, mu_k):
        import jax, jax.numpy as jnp
        import numpy as np
        DIM = 128

        def _reference_tuple_inner(x, W_r, W_k, W_v, mu_r, mu_k):
            B, T, C = x.shape
            x_prev = jnp.concatenate([jnp.zeros((B, 1, C), x.dtype), x[:, :-1, :]], axis=1)
            xr = mu_r * x + (1.0 - mu_r) * x_prev
            xk = mu_k * x + (1.0 - mu_k) * x_prev
            r = jax.nn.sigmoid(jnp.einsum('btc,dc->btd', xr, W_r))
            k = jnp.einsum('btc,dc->btd', xk, W_k)
            k_act = jnp.square(jax.nn.relu(k))
            out = r * jnp.einsum('btc,dc->btd', k_act, W_v)
            new_state = x[:, -1, :]
            return (out, new_state)
        return _reference_tuple_inner(x, W_r, W_k, W_v, mu_r, mu_k)[0]

    def _L3_attn_ref(embeddings, W_Q, W_K, W_V):
        import jax, jax.numpy as jnp
        import numpy as np
        B, S, D = (4, 256, 128)

        def _xavier(key, shape):
            bound = float(np.sqrt(6.0 / (shape[0] + shape[1])))
            return jax.random.uniform(key, shape, dtype=jnp.float32, minval=-bound, maxval=bound)
        _, seq_len, d = embeddings.shape
        Q = embeddings @ W_Q
        K = embeddings @ W_K
        V = embeddings @ W_V
        scale = 1.0 / jnp.sqrt(jnp.float32(d))
        scores = jnp.einsum('bqd,bkd->bqk', Q, K) * scale
        causal = jnp.tril(jnp.ones((seq_len, seq_len), dtype=bool))
        scores = jnp.where(causal[None, :, :], scores, -jnp.inf)
        probs = jax.nn.softmax(scores, axis=-1)
        return jnp.einsum('bqk,bkd->bqd', probs, V)

    def _L3_ffn_ref(x, w_gate, w_up, w_down):
        import jax, jax.numpy as jnp
        import numpy as np
        BLOCK = 16
        _GRID = jnp.array([0.0, 0.5, 1.0, 1.5, 2.0, 3.0, 4.0, 6.0], dtype=jnp.float32)
        _MID = jnp.array([0.25, 0.75, 1.25, 1.75, 2.5, 3.5, 5.0], dtype=jnp.float32)

        def fp4_quant_dequant(x):
            shape = x.shape
            xb = x.reshape(shape[:-1] + (shape[-1] // BLOCK, BLOCK))
            scale = jnp.max(jnp.abs(xb), axis=-1, keepdims=True) / 6.0
            scale = jnp.maximum(scale, jnp.float32(1e-12))
            xn = xb / scale
            idx = jnp.searchsorted(_MID, jnp.abs(xn))
            q = _GRID[idx] * jnp.sign(xn) * scale
            return q.reshape(shape)

        def fp4_linear(x, w):
            xq = fp4_quant_dequant(x)
            wq = fp4_quant_dequant(w)
            return jnp.einsum('bsk,nk->bsn', xq, wq)
        gate = fp4_linear(x, w_gate)
        y = fp4_linear(x, w_up)
        h = jax.nn.silu(gate) * y
        return fp4_linear(h, w_down)
    x = L0_attn_x
    x = _layernorm(x + _L0_attn_ref(x, L0_attn_W_k, L0_attn_W_v, L0_attn_W_c, L0_attn_leaky_key_beta, L0_attn_key_scale, L0_attn_v_coef, L0_attn_val_scale), axis=-1)
    x = _layernorm(x + _L0_ffn_ref(x, L0_ffn_Ws, L0_ffn_bs, L0_ffn_W1, L0_ffn_b1, L0_ffn_W2, L0_ffn_b2), axis=-1)
    x = _layernorm(x + _L1_attn_ref(x, L1_attn_w_qkv, L1_attn_w_out, L1_attn_b_out), axis=-1)
    x = _layernorm(x + _L1_ffn_ref(x, L1_ffn_Wqkv, L1_ffn_q_scale, L1_ffn_k_scale, L1_ffn_Wo, L1_ffn_ln_g, L1_ffn_ln_b, L1_ffn_W1, L1_ffn_b1, L1_ffn_W2, L1_ffn_b2), axis=-1)
    x = _layernorm(x + _L2_attn_ref(x, L2_attn_W_in, L2_attn_W_conv, L2_attn_b_conv, L2_attn_W_xproj, L2_attn_W_dt, L2_attn_b_dt, L2_attn_A_log, L2_attn_D, L2_attn_W_out), axis=-1)
    x = _layernorm(x + _L2_ffn_ref(x, L2_ffn_W_r, L2_ffn_W_k, L2_ffn_W_v, L2_ffn_mu_r, L2_ffn_mu_k), axis=-1)
    x = _layernorm(x + _L3_attn_ref(x, L3_attn_W_Q, L3_attn_W_K, L3_attn_W_V), axis=-1)
    x = _layernorm(x + _L3_ffn_ref(x, L3_ffn_w_gate, L3_ffn_w_up, L3_ffn_w_down), axis=-1)
    return x

_drawn_inputs = setup_inputs


def setup_inputs(seed=0):
    import zlib

    import numpy as np

    out = dict(_drawn_inputs(seed))
    spreads = {'L0_attn_key_scale': (0.10000000149011612, 0.6),
     'L0_attn_val_scale': (-0.05000000074505806, 0.6),
     'L0_ffn_bs': (0.0, 0.1),
     'L0_ffn_b1': (0.0, 0.292),
     'L0_ffn_b2': (0.0, 0.1),
     'L1_ffn_q_scale': (1.0, 0.6),
     'L1_ffn_k_scale': (1.0, 0.6),
     'L1_ffn_ln_g': (1.0, 0.6),
     'L1_ffn_ln_b': (0.0, 0.8),
     'L1_ffn_b1': (0.0, 0.8),
     'L1_ffn_b2': (0.0, 0.1),
     'L2_attn_b_conv': (0.0, 0.8),
     'L2_attn_D': (1.0, 0.6)}
    factors = {'L0_attn_W_k': 2.768,
     'L0_attn_W_v': 2.866,
     'L0_attn_W_c': 2.669,
     'L0_attn_leaky_key_beta': 4.411,
     'L0_attn_v_coef': 3.707,
     'L1_ffn_W1': 3.619,
     'L1_ffn_W2': 3.529,
     'L2_attn_W_in': 8.0,
     'L2_attn_W_conv': 8.0,
     'L2_attn_W_xproj': 8.0,
     'L2_attn_W_dt': 8.0,
     'L2_attn_b_dt': 8.0,
     'L2_attn_A_log': 8.0,
     'L2_attn_W_out': 8.0,
     'L2_ffn_W_r': 3.094,
     'L2_ffn_mu_r': 6.2,
     'L3_ffn_w_gate': 5.619,
     'L3_ffn_w_up': 5.351,
     'L3_ffn_w_down': 5.385}
    for name, (base, spread) in spreads.items():
        noise = np.random.default_rng([zlib.crc32(name.encode()), seed]).standard_normal(out[name].shape)
        drawn = base * np.exp(spread * noise) if base else spread * noise
        out[name] = jnp.asarray(drawn.astype(out[name].dtype))
    for name, factor in factors.items():
        out[name] = (out[name] * factor).astype(out[name].dtype)
    return out
```

```python
import numpy as np
import concourse.bass as bass
from concourse import mybir
from contextlib import ExitStack, contextmanager

fp32 = mybir.dt.float32
bf16 = mybir.dt.bfloat16
ALU = mybir.AluOpType
ACT = mybir.ActivationFunctionType
AX = mybir.AxisListType

T = 2048
C = 128
P = 128
NT = T // P
QB = 512
NB = T // QB
LN_EPS = 1e-5
MASKED = -1e30


class Lane:

    def __init__(self, eng, own, base=None):
        self.eng, self.own = eng, own
        self.seen, self.base = {}, dict(base or {})

    def wait(self, sem, by=1):
        self.seen[sem] = self.seen.get(sem, 0) + by
        self.eng.wait_ge(sem, self.base.get(sem, 0) + self.seen[sem])

    def skip(self, sem, by):
        self.seen[sem] = self.seen.get(sem, 0) + by

    def ahead(self, sem, by):
        self.eng.wait_ge(sem, self.base.get(sem, 0) + self.seen.get(sem, 0) + by)

    def post(self, ins):
        ins.then_inc(self.own, 1)
        self.seen[self.own] = self.seen.get(self.own, 0) + 1

    def settle(self):
        self.eng.wait_ge(self.own, self.base.get(self.own, 0) + self.seen[self.own])

    def seq(self, ins):
        self.post(ins)
        self.settle()

    @contextmanager
    def loop(self, count, per):
        before, outer = dict(self.seen), dict(self.base)
        with self.eng.Fori(0, count) as i:
            for sem, by in per.items():
                self.base[sem] = outer.get(sem, 0) + i * by
            yield i
            added = {s: n - before.get(s, 0) for s, n in self.seen.items() if n != before.get(s, 0)}
            assert added == {s: per.get(s, 0) for s in added}, \
                ("per pass", {s.name: n for s, n in added.items()}, {s.name: n for s, n in per.items()})
        self.base = outer
        self.seen = {s: before.get(s, 0) + count * per.get(s, 0) for s in self.seen}


class Ring:

    def __init__(self, nc, ctx, banks, name):
        self.buf = ctx.enter_context(nc.psum_tensor(f"{name}_bank", [P, banks, QB], fp32))
        self.filled = nc.alloc_semaphore(f"{name}_filled")
        self.freed = nc.alloc_semaphore(f"{name}_freed")
        self.banks = banks

    def writer(self, lane):
        return RingEnd(self, lane, self.freed)

    def reader(self, lane):
        lane.eng.sem_inc(self.freed, self.banks)
        lane.seen[self.freed] = self.banks
        return RingEnd(self, lane, self.filled)


class RingEnd:
    def __init__(self, ring, lane, sem):
        self.ring, self.lane, self.sem, self.turn = ring, lane, sem, 0

    def take(self):
        self.lane.wait(self.sem)
        bank = self.ring.buf[:, self.turn % self.ring.banks, :]
        self.turn += 1
        return bank

    def filled(self, ins):
        ins.then_inc(self.ring.filled, 1)

    def free(self, ins):
        ins.then_inc(self.ring.freed, 1)
        self.lane.seen[self.ring.freed] += 1

    def settle(self):
        self.lane.eng.wait_ge(self.ring.freed, self.lane.base.get(self.ring.freed, 0) + self.lane.seen[self.ring.freed])


def layernorm(nc, g, name, feature=None, token=None, out_dram=None):
    with ExitStack() as ctx:
        def sb(n, shape, dt=fp32):
            return ctx.enter_context(nc.sbuf_tensor(f"{name}_{n}", shape, dt))

        def sem(n):
            return nc.alloc_semaphore(f"{name}_{n}")

        z = sb("z", [P, NT, C])
        stats = sb("stats", [P, NT, 6])
        meanvar = sb("meanvar", [P, NT, 2])
        std = sb("std", [P, NT])
        rstd = sb("rstd", [P, NT])
        eps = sb("eps", [P, 1])
        up = ctx.enter_context(nc.psum_tensor(f"{name}_up", [P, NT, C], fp32))
        down = ctx.enter_context(nc.psum_tensor(f"{name}_down", [P, NT, C], fp32))
        turned = sem("turned")
        z_ready = sem("z_ready")
        std_ready = sem("std_ready")
        x_ready = sem("x_ready")
        back = sem("back")
        xT_ready = sem("xT_ready")
        stored = sem("stored")
        own = sem("dve_steps")
        G = 4
        block = ctx.enter_context(nc.Block())

        @block.tensor
        def _(pe):
            if feature is not None:
                for t in range(NT):
                    last = nc.tensor.transpose(up[:, t, :], feature[:, t * P:(t + 1) * P], g.ident[:])
                    if t % G == G - 1:
                        last.then_inc(turned, 1)
            if out_dram is None:
                for k in range(NT // G):
                    pe.wait_ge(x_ready, k + 1)
                    for t in range(k * G, (k + 1) * G):
                        last = nc.tensor.transpose(down[:, t, :], g.x[:, t, :], g.ident[:])
                    last.then_inc(back, 1)

        @block.vector
        def _(dve):
            lane = Lane(dve, own)
            lane.seq(nc.vector.memset(eps[:], LN_EPS))
            for k in range(NT // G):
                s = slice(k * G, (k + 1) * G)
                if feature is not None:
                    dve.wait_ge(turned, k + 1)
                delta = up[:, s, :] if feature is not None else token[:, s, :]
                lane.seq(nc.vector.tensor_tensor(z[:, s, :], delta, g.x[:, s, :], ALU.add))
                for t in range(k * G, (k + 1) * G):
                    lane.post(nc.vector.bn_stats(stats[:, t, :], z[:, t, :]))
                lane.settle()
                for t in range(k * G, (k + 1) * G):
                    last = nc.vector.bn_aggr(meanvar[:, t, :], stats[:, t, :])
                last.then_inc(z_ready, 1)
            for k in range(NT // G):
                s = slice(k * G, (k + 1) * G)
                dve.wait_ge(std_ready, k + 1)
                lane.seq(nc.vector.reciprocal(rstd[:, s], std[:, s]))
                for t in range(k * G, (k + 1) * G):
                    last = nc.vector.tensor_scalar(g.x[:, t, :], z[:, t, :], meanvar[:, t, 0:1],
                                                   rstd[:, t:t + 1], ALU.subtract, ALU.mult)
                last.then_inc(x_ready, 1)

        @block.scalar
        def _(act):
            for k in range(NT // G):
                s = slice(k * G, (k + 1) * G)
                act.wait_ge(z_ready, k + 1)
                nc.scalar.activation(std[:, s], meanvar[:, s, 1], ACT.Sqrt, bias=eps[:]).then_inc(std_ready, 1)
            if out_dram is None:
                for k in range(NT // G):
                    act.wait_ge(back, k + 1)
                    nc.scalar.copy(g.xT[:, k * QB:(k + 1) * QB], down[:, k * G:(k + 1) * G, :]).then_inc(xT_ready, 1)

        @block.sync
        def _(sp):
            if out_dram is not None:
                for k in range(NT // G):
                    sp.wait_ge(x_ready, k + 1)
                    sp.dma_start(out_dram[k * QB:(k + 1) * QB, :].rearrange("(t p) c -> p t c", p=P),
                                 g.x[:, k * G:(k + 1) * G, :]).then_inc(stored, 16)
                sp.wait_ge(stored, 16 * (NT // G))


def attention(nc, g, name, heads, D, k_src, v_src, w_all, wo_all, scale, yT,
              causal=None, rope=None, separate_q=True, bias=None):
    one = D < P
    R = D + 1 if one else D
    DV = R
    pieces = (["q", "qr"] if rope else ["q"]) if separate_q else []
    pieces += ["k", "kr"] if rope else ["k"]
    NW = len(pieces) * R + DV
    with ExitStack() as ctx:
        def sb(n, shape, dt=fp32):
            return ctx.enter_context(nc.sbuf_tensor(f"{name}_{n}", shape, dt))

        def sem(n):
            return nc.alloc_semaphore(f"{name}_{n}")

        wh = sb("w_head", [P, NW])
        woh = sb("wo_head", [R, C])
        qT = sb("qT", [R, T])
        kT = sb("kT", [R, T])
        v = sb("v", [P, NT, DV])
        probs = sb("probs", [P, 4, QB])
        rotated = sb("rotated", [R, QB])
        chunk_max = sb("chunk_max", [P, 4, NB])
        row_max = sb("row_max", [P, 4])
        rsum = sb("rsum", [1, QB])
        rsum_all = sb("rsum_all", [R, QB])
        oT = sb("oT", [R, QB])
        negmax = sb("negmax", [1, T]) if not one else qT
        ring = Ring(nc, ctx, 4, name)
        scoresT = ctx.enter_context(nc.psum_tensor(f"{name}_scoresT", [P, 2, QB], fp32))
        out = ctx.enter_context(nc.psum_tensor(f"{name}_out", [P, 2, QB], fp32))

        w_ready = sem("w_ready")
        prepared = sem("prepared")
        w_used = sem("w_used")
        max_ready = sem("max_ready")
        negmax_ready = sem("negmax_ready")
        scores_ready = sem("scores_ready")
        probs_ready = sem("probs_ready")
        out_ready = sem("out_ready")
        rsum_ready = sem("rsum_ready")
        oT_ready = sem("oT_ready")
        projected = sem("projected")
        own = sem("dve_steps")
        pool_own = sem("pool_steps")
        block = ctx.enter_context(nc.Block())

        def chunks(b, qt):
            if causal is None:
                return [(c * QB, QB) for c in range(NB)]
            return [(c * QB, QB) for c in range(b)] + [(b * QB, P * (qt + 1))]

        def key_tiles(b):
            if causal is None:
                return [(k, 0) for k in range(NT)]
            return [(k, max(0, (k - 4 * b) * P)) for k in range(4 * (b + 1))]

        n_keys = sum(len(key_tiles(b)) for b in range(NB))
        n_chunks = sum(len(chunks(b, q)) for b in range(NB) for q in range(4))
        n_ring = NB * (len(pieces) + 1) + n_chunks + NB + NB + (NB if one else 0)
        assert n_ring % 4 == 0 or heads == 1
        wcols = {p: wh[:, i * R:(i + 1) * R] for i, p in enumerate(pieces)}
        wv = wh[:, len(pieces) * R:NW]
        diag_q, diag_k = (g.mask_strict_q, g.mask_strict_k) if causal == "strict" else (g.mask_q, g.mask_k)

        def maybe_loop(lane, per):
            return lane.loop(heads, per) if heads > 1 else once()

        @block.gpsimd
        def _(pool):
            lane = Lane(pool, pool_own)
            with maybe_loop(lane, {w_used: 1, projected: 1, pool_own: 1 if one else 0}) as h:
                lane.wait(w_used)
                copied = nc.gpsimd.tensor_copy(wh[:], w_all[:, h, :])
                if one:
                    lane.post(copied)
                    lane.wait(projected)
                    copied = nc.gpsimd.tensor_copy(woh[:], wo_all[:, h, :])
                    lane.settle()
                else:
                    lane.wait(projected)
                copied.then_inc(w_ready, 1)

        @block.tensor
        def _(pe):
            lane = Lane(pe, None)
            to_dve = ring.writer(lane)
            with maybe_loop(lane, {ring.freed: n_ring, w_ready: 1, prepared: 1, max_ready: NB,
                                   negmax_ready: NB, probs_ready: n_keys,
                                   rsum_ready: NB, oT_ready: NB if one else 0}) as h:
                lane.wait(w_ready)
                for b in range(NB):
                    for p in pieces:
                        bank = to_dve.take()
                        to_dve.filled(nc.tensor.matmul(bank[0:R, :], wcols[p], k_src[:, b * QB:(b + 1) * QB],
                                                       start=True, stop=True))
                    bank = to_dve.take()
                    for t in range(4):
                        tok = (4 * b + t) * P
                        last = nc.tensor.matmul(bank[:, t * DV:(t + 1) * DV] if 4 * DV <= QB else None,
                                                v_src[:, tok:tok + P], wv, start=True, stop=True)
                    to_dve.filled(last)
                lane.wait(prepared)

                def find_max(b):
                    for qt in range(4):
                        q0 = b * QB + qt * P
                        row0 = 1 if one else 0
                        for first, n in chunks(b, qt):
                            bank = to_dve.take()
                            diag = causal is not None and first == b * QB
                            last = nc.tensor.matmul(bank[:, 0:n], qT[:, q0:q0 + P], kT[:, first:first + n],
                                                    start=True, stop=not diag)
                            if diag:
                                last = nc.tensor.matmul(bank[:, n - P:n], g.ident[:], diag_q[:],
                                                        start=False, stop=True)
                            to_dve.filled(last)
                    lane.wait(max_ready)
                    bank = to_dve.take()
                    for qt in range(4):
                        last = nc.tensor.matmul(bank[0:1, qt * P:(qt + 1) * P], row_max[:, qt:qt + 1], g.ident[:],
                                                start=True, stop=True)
                    to_dve.filled(last)

                def weigh(b):
                    lane.wait(negmax_ready)
                    tiles = key_tiles(b)
                    acc = out[:, b % 2, :]

                    def values(j):
                        k, off = tiles[j]
                        lane.wait(probs_ready)
                        last = nc.tensor.matmul(acc[0:R, off:QB], v[:, k, :], probs[:, j % 4, off:QB],
                                                start=j == 0, stop=j == len(tiles) - 1)
                        if not one:
                            last = nc.tensor.matmul(sums[0:1, off:QB], g.ones[:, 0:1], probs[:, j % 4, off:QB],
                                                    start=j == 0, stop=j == len(tiles) - 1)
                        return last

                    sums = out[:, 1 - b % 2, :]
                    for j, (k, off) in enumerate(tiles):
                        bank = scoresT[:, j % 2, off:QB]
                        diag = causal is not None and k >= 4 * b
                        last = nc.tensor.matmul(bank, kT[:, k * P:(k + 1) * P], qT[:, b * QB + off:(b + 1) * QB],
                                                start=True, stop=one and not diag)
                        if not one:
                            last = nc.tensor.matmul(bank, g.ones[0:1, :], negmax[0:1, b * QB + off:(b + 1) * QB],
                                                    start=False, stop=not diag)
                        if diag:
                            last = nc.tensor.matmul(scoresT[:, j % 2, off:off + P], g.ident[:], diag_k[:],
                                                    start=False, stop=True)
                        last.then_inc(scores_ready, 1)
                        if j > 0:
                            values(j - 1)
                    values(len(tiles) - 1).then_inc(out_ready, 1)
                    lane.wait(rsum_ready)
                    bank = to_dve.take()
                    to_dve.filled(nc.tensor.matmul(bank[:, :], g.ones[0:1, :], rsum[:], start=True, stop=True))
                    if one:
                        lane.wait(oT_ready)
                        bank = to_dve.take()
                        to_dve.filled(nc.tensor.matmul(bank[:, :], woh[:], oT[:], start=True, stop=True))

                find_max(0)
                for b in range(NB):
                    if b + 1 < NB and one:
                        find_max(b + 1)
                    weigh(b)
                    if b + 1 < NB and not one:
                        find_max(b + 1)

        @block.scalar
        def _(act):
            lane = Lane(act, None)
            with maybe_loop(lane, {scores_ready: n_keys}) as h:
                for b in range(NB):
                    for j, (k, off) in enumerate(key_tiles(b)):
                        lane.wait(scores_ready)
                        nc.scalar.activation(probs[:, j % 4, off:QB], scoresT[:, j % 2, off:QB], ACT.Exp,
                                             scale=scale).then_inc(probs_ready, 1)

        @block.vector
        def _(dve):
            lane = Lane(dve, own)
            from_pe = ring.reader(lane)
            dve.sem_inc(projected, 1)
            dve.sem_inc(w_used, 1)
            per = {ring.filled: n_ring, ring.freed: n_ring, out_ready: NB, w_ready: 0,
                   own: PER_OWN[name]}
            if one:
                lane.seq(nc.vector.memset(v[:, :, 0:1], 1.0))
            with maybe_loop(lane, per) as h:
                for b in range(NB):
                    s = slice(b * QB, (b + 1) * QB)
                    for dst, names in ((qT, ["q", "qr"]), (kT, ["k", "kr"])):
                        if names[0] not in pieces:
                            continue
                        bank = from_pe.take()
                        if not rope:
                            if dst is kT and one:
                                if not separate_q:
                                    lane.post(nc.vector.tensor_copy(qT[:, s], bank[0:R, :]))
                                from_pe.free(nc.vector.tensor_scalar(kT[:, s], bank[0:R, :], g.e0[0:R, :], None, ALU.add))
                            else:
                                from_pe.free(nc.vector.tensor_copy(dst[:, s], bank[0:R, :]))
                            continue
                        cos, sin = rope
                        from_pe.free(nc.vector.tensor_tensor(dst[:, s], bank[0:R, :], cos[:, s], ALU.mult))
                        bank = from_pe.take()
                        from_pe.free(nc.vector.tensor_tensor(rotated[:], bank[0:R, :], sin[:, s], ALU.mult))
                        from_pe.settle()
                        if dst is kT:
                            lane.seq(nc.vector.scalar_tensor_tensor(kT[:, s], rotated[:], g.e0[0:R, :], kT[:, s],
                                                                    ALU.add, ALU.add))
                        else:
                            lane.seq(nc.vector.tensor_tensor(qT[:, s], rotated[:], qT[:, s], ALU.add))
                    bank = from_pe.take()
                    row0 = 1 if one else 0
                    src = bank[:, 0:4 * DV].rearrange("p (t d) -> p t d", t=4)
                    from_pe.free(nc.vector.tensor_copy(v[:, 4 * b:4 * b + 4, row0:DV], src[:, :, row0:DV]))
                from_pe.settle()
                dve.sem_inc(prepared, 1)
                dve.sem_inc(w_used, 1)

                def find_max(b):
                    for qt in range(4):
                        for c, (first, n) in enumerate(chunks(b, qt)):
                            bank = from_pe.take()
                            from_pe.free(nc.vector.reduce_max(chunk_max[:, qt, c:c + 1], bank[:, 0:n], axis=AX.X))
                    from_pe.settle()
                    n = len(chunks(b, 0))
                    nc.vector.reduce_max(row_max[:], chunk_max[:, :, 0:n], axis=AX.X).then_inc(max_ready, 1)
                    bank = from_pe.take()
                    from_pe.free(nc.vector.tensor_scalar(negmax[0:1, b * QB:(b + 1) * QB], bank[0:1, :], -1.0, None, ALU.mult))
                    from_pe.settle()
                    dve.sem_inc(negmax_ready, 1)

                def finish(b):
                    acc = out[:, b % 2, :]
                    sums = acc[0:1, :] if one else out[0:1, 1 - b % 2, :]
                    lane.wait(out_ready)
                    nc.vector.reciprocal(rsum[:], sums).then_inc(rsum_ready, 1)
                    bank = from_pe.take()
                    from_pe.free(nc.vector.tensor_copy(rsum_all[:], bank[0:R, :]))
                    from_pe.settle()
                    s = slice(b * QB, (b + 1) * QB)
                    if not one:
                        lane.post(nc.vector.tensor_tensor(yT[:, s], acc[0:R, :], rsum_all[:], ALU.mult))
                        return
                    ins = nc.vector.tensor_tensor(oT[:], acc[0:R, :], rsum_all[:], ALU.mult)
                    if causal == "strict" and b == 0:
                        lane.seq(ins)
                        ins = nc.vector.memset(oT[:, 0:1], 0.0)
                    ins.then_inc(oT_ready, 1)
                    bank = from_pe.take()
                    from_pe.free(nc.vector.tensor_tensor(yT[:, s], bank[:, :], yT[:, s], ALU.add))

                find_max(0)
                for b in range(NB):
                    if b + 1 < NB and one:
                        find_max(b + 1)
                    finish(b)
                    if b + 1 < NB and not one:
                        find_max(b + 1)
                from_pe.settle()
                dve.sem_inc(projected, 1)


@contextmanager
def once():
    yield 0


def decayed_keys(nc, g, w, kT_out, vT_out):
    with ExitStack() as ctx:
        def sb(n, shape, dt=fp32):
            return ctx.enter_context(nc.sbuf_tensor(f"dk_{n}", shape, dt))

        def sem(n):
            return nc.alloc_semaphore(f"dk_{n}")

        square = sb("square", [P, T])
        norm = sb("norm", [P, T])
        col = sb("col", [P, 8])
        acc = [ctx.enter_context(nc.psum_tensor(f"dk_acc{i}", [P, NB, QB], fp32)) for i in range(2)]
        projected = sem("projected")
        squared = sem("squared")
        summed = sem("summed")
        normed = sem("normed")
        cols_ready = sem("cols_ready")
        raw_ready = sem("raw_ready")
        clipped = sem("clipped")
        done = sem("done")
        own = sem("dve_steps")
        act_own = sem("act_steps")
        block = ctx.enter_context(nc.Block())
        outs = (kT_out, vT_out)

        @block.tensor
        def _(pe):
            for i, wt in enumerate((w["kT"], w["vT"])):
                for b in range(NB):
                    last = nc.tensor.matmul(acc[i][:, b, :], wt[:], g.xT[:, b * QB:(b + 1) * QB], start=True, stop=True)
                last.then_inc(projected, 1)
            for i in range(2):
                pe.wait_ge(squared, i + 1)
                for b in range(NB):
                    last = nc.tensor.matmul(acc[i][:, b, :], g.head_ones[:], square[:, b * QB:(b + 1) * QB],
                                            start=True, stop=True)
                last.then_inc(summed, 1)

        @block.scalar
        def _(act):
            nc.scalar.activation(col[:, 0:1], w["beta"], ACT.Abs).then_inc(act_own, 1)
            act.wait_ge(act_own, 1)
            nc.scalar.activation(col[:, 1:2], col[:, 0:1], ACT.Exp, scale=-10.0)
            nc.scalar.activation(col[:, 3:4], w["val_scale"], ACT.Exp, scale=10.0)
            act.wait_ge(clipped, 1)
            nc.scalar.activation(col[:, 2:3], col[:, 5:6], ACT.Exp).then_inc(cols_ready, 1)
            for i in range(2):
                act.wait_ge(raw_ready, i + 1)
                if i:
                    act.wait_ge(summed, i)
                nc.scalar.activation(square[:], outs[i][:], ACT.Square).then_inc(squared, 1)
                act.wait_ge(summed, i + 1)
                if i:
                    act.wait_ge(done, 1)
                nc.scalar.activation(norm[:], acc[i][:, :, :].rearrange("p b q -> p (b q)"), ACT.Sqrt).then_inc(normed, 1)

        @block.vector
        def _(dve):
            lane = Lane(dve, own)
            nc.vector.tensor_scalar(col[:, 5:6], w["key_scale"], 10.0, KEY_SCALE_MAX, ALU.mult, ALU.min).then_inc(clipped, 1)
            lane.post(nc.vector.tensor_scalar(col[:, 4:5], w["v_coef"], -1.0, 1.0, ALU.mult, ALU.add))
            dve.wait_ge(cols_ready, 1)
            dve.wait_ge(projected, 1)
            k_raw = acc[0][:, :, :].rearrange("p b q -> p (b q)")
            v_raw = acc[1][:, :, :].rearrange("p b q -> p (b q)")
            nc.vector.tensor_tensor_scan(kT_out[:], col[:, 1:2].to_broadcast([P, T]), k_raw, 0.0,
                                         ALU.mult, ALU.add).then_inc(raw_ready, 1)
            dve.wait_ge(projected, 2)
            lane.seq(nc.vector.tensor_scalar(vT_out[:], v_raw, w["v_coef"], None, ALU.mult))
            nc.vector.scalar_tensor_tensor(vT_out[:, 0:T - 1], v_raw[:, 1:T], col[:, 4:5], vT_out[:, 0:T - 1],
                                           ALU.mult, ALU.add).then_inc(raw_ready, 1)
            dve.wait_ge(raw_ready, 2)
            for i, factor in enumerate((col[:, 2:3], col[:, 3:4])):
                dve.wait_ge(normed, i + 1)
                lane.seq(nc.vector.tensor_scalar(norm[:], norm[:], 1e-10, None, ALU.add))
                lane.seq(nc.vector.reciprocal(norm[:], norm[:]))
                nc.vector.scalar_tensor_tensor(outs[i][:], outs[i][:], factor, norm[:],
                                               ALU.mult, ALU.mult).then_inc(done, 1)


E_ = 8
F_ = 512
FT = F_ // P
TOPK = T // E_
EXPERT_COLS = F_ + FT * C + FT + 1


def stage_l0_ffn(nc, g, d, y):
    with ExitStack() as ctx:
        def sb(n, shape, dt=fp32):
            return ctx.enter_context(nc.sbuf_tensor(f"l0f_{n}", shape, dt))
        ws, bs = sb("ws", [P, E_]), sb("bs", [P, NT, E_])
        probsT = sb("probsT", [E_, T])
        left = sb("left", [E_, T])
        gates = sb("gates", [E_, T])
        expert_out = sb("expert_out", [C, E_, T])
        select = sb("select", [E_, E_, P])
        load(nc, "l0f", [(ws[:], d["L0_ffn_Ws"]), (bs[:], d["h_l0_bs"]), (select[:], d["c_select8"])])
        route(nc, g, ws, bs, probsT, left)
        experts(nc, g, d, probsT, left, gates, expert_out)
        combine(nc, g, select, gates, expert_out)
    layernorm(nc, g, "ln1", feature=g.delta)


def route(nc, g, ws, bs, probsT, left):
    with ExitStack() as ctx:
        def sb(n, shape, dt=fp32):
            return ctx.enter_context(nc.sbuf_tensor(f"rt_{n}", shape, dt))

        def sem(n):
            return nc.alloc_semaphore(f"rt_{n}")
        p = sb("p", [P, NT, E_])
        row = sb("row", [P, NT])
        logits = ctx.enter_context(nc.psum_tensor("rt_logits", [P, NT, E_], fp32))
        turned = ctx.enter_context(nc.psum_tensor("rt_turned", [E_, T], fp32))
        logits_ready, shifted = sem("logits_ready"), sem("shifted")
        exp_ready, p_ready, turned_ready = sem("exp_ready"), sem("p_ready"), sem("turned_ready")
        own = sem("dve_steps")
        block = ctx.enter_context(nc.Block())

        @block.tensor
        def _(pe):
            for t in range(NT):
                last = nc.tensor.matmul(logits[:, t, :], g.xT[:, t * P:(t + 1) * P], ws[:], start=True, stop=True)
            last.then_inc(logits_ready, 1)
            pe.wait_ge(p_ready, 1)
            for t in range(NT):
                last = nc.tensor.transpose(turned[:, t * P:(t + 1) * P], p[:, t, :], g.ident[:])
            last.then_inc(turned_ready, 1)

        @block.vector
        def _(dve):
            lane = Lane(dve, own)
            dve.wait_ge(logits_ready, 1)
            lane.seq(nc.vector.tensor_tensor(p[:], logits[:], bs[:], ALU.add))
            lane.seq(nc.vector.reduce_max(row[:], p[:], axis=AX.X))
            nc.vector.tensor_tensor(p[:], p[:], spread(row[:], E_), ALU.subtract).then_inc(shifted, 1)
            dve.wait_ge(exp_ready, 1)
            lane.seq(nc.vector.reduce_sum(row[:], p[:], axis=AX.X))
            lane.seq(nc.vector.reciprocal(row[:], row[:]))
            nc.vector.tensor_tensor(p[:], p[:], spread(row[:], E_), ALU.mult).then_inc(p_ready, 1)
            dve.wait_ge(turned_ready, 1)
            nc.vector.tensor_copy(probsT[:], turned[:])
            nc.vector.tensor_copy(left[:], turned[:])

        @block.scalar
        def _(act):
            act.wait_ge(shifted, 1)
            nc.scalar.activation(p[:], p[:], ACT.Exp).then_inc(exp_ready, 1)


def spread(ap, n):
    return ap.unsqueeze(2).to_broadcast([ap.shape[0], ap.shape[1], n])


def experts(nc, g, d, probsT, left, gates, expert_out):
    with ExitStack() as ctx:
        def sb(n, shape, dt=fp32):
            return ctx.enter_context(nc.sbuf_tensor(f"ex_{n}", shape, dt))

        def sem(n):
            return nc.alloc_semaphore(f"ex_{n}")
        w = sb("w", [P, 2, EXPERT_COLS])
        hidden = sb("hidden", [P, 2, FT, QB])
        best = sb("best", [E_, 8])
        up = ctx.enter_context(nc.psum_tensor("ex_up", [P, FT, QB], fp32))
        down = ctx.enter_context(nc.psum_tensor("ex_down", [P, 2, QB], fp32))
        loaded = [sem(f"loaded{s}") for s in range(2)]
        w_free = sem("w_free")
        up_ready = sem("up_ready")
        up_done = sem("up_done")
        down_ready = sem("down_ready")
        down_done = sem("down_done")
        own = sem("dve_steps")
        block = ctx.enter_context(nc.Block())
        b1_at, b2_at = F_ + FT * C, F_ + FT * C + FT

        @block.sync
        def _(sp):
            lane = Lane(sp, None)
            with lane.loop(E_ // 2, {w_free: 2}) as i:
                for s in range(2):
                    lane.wait(w_free)
                    sp.dma_start(w[:, s, :], d["h_l0_experts"][2 * i + s]).then_inc(loaded[s], 16)

        @block.tensor
        def _(pe):
            lane = Lane(pe, None)
            with lane.loop(E_ // 2, {loaded[0]: 16, loaded[1]: 16, up_done: 2 * NB * FT,
                                     down_done: 2 * NB}) as i:
                for s in range(2):
                    lane.wait(loaded[s], 16)

                    def make_up(b):
                        for f in range(FT):
                            lane.wait(up_done)
                            nc.tensor.matmul(up[:, f, :], w[:, s, f * P:(f + 1) * P], g.xT[:, b * QB:(b + 1) * QB],
                                             start=True, stop=True).then_inc(up_ready, 1)

                    def make_down(b):
                        lane.wait(down_done)
                        for f in range(FT):
                            last = nc.tensor.matmul(down[:, b % 2, :], w[:, s, F_ + f * C:F_ + (f + 1) * C],
                                                    hidden[:, b % 2, f, :], start=f == 0, stop=f == FT - 1)
                        last.then_inc(down_ready, 1)
                    make_up(0)
                    for b in range(1, NB):
                        make_up(b)
                        make_down(b - 1)
                    pe.wait_ge(up_done, lane.base[up_done] + lane.seen[up_done] + FT)
                    make_down(NB - 1)

        @block.scalar
        def _(act):
            lane = Lane(act, None)
            act.sem_inc(up_done, FT)
            act.sem_inc(down_done, 2)
            act.sem_inc(w_free, 2)
            with lane.loop(E_ // 2, {up_ready: 2 * NB * FT, down_ready: 2 * NB}) as i:
                for s in range(2):
                    def gelu(b):
                        for f in range(FT):
                            lane.wait(up_ready)
                            nc.scalar.activation(hidden[:, b % 2, f, :], up[:, f, :], ACT.Gelu_apprx_tanh,
                                                 bias=w[:, s, b1_at + f:b1_at + f + 1]).then_inc(up_done, 1)

                    def store(b):
                        lane.wait(down_ready)
                        nc.scalar.activation(expert_out[:, 2 * i + s, b * QB:(b + 1) * QB], down[:, b % 2, :],
                                             ACT.Identity, bias=w[:, s, b2_at:b2_at + 1]).then_inc(down_done, 1)
                    gelu(0)
                    for b in range(1, NB):
                        gelu(b)
                        store(b - 1)
                    store(NB - 1)
                    act.wait_ge(down_done, 2 + NB * (2 * i + s + 1))
                    act.sem_inc(w_free, 1)

        @block.vector
        def _(dve):
            lane = Lane(dve, own)
            for _ in range(TOPK // 8):
                lane.seq(nc.vector.max(best[:], left[:]))
                lane.seq(nc.vector.match_replace(left[:], best[:], left[:], -1.0))
            nc.vector.scalar_tensor_tensor(gates[:], left[:], 0.0, probsT[:], ALU.is_lt, ALU.mult)


def combine(nc, g, select, gates, expert_out):
    with ExitStack() as ctx:
        def sem(n):
            return nc.alloc_semaphore(f"cb_{n}")
        part = ctx.enter_context(nc.sbuf_tensor("cb_part", [P, 2, T // 2], fp32))
        spread_gate = ctx.enter_context(nc.psum_tensor("cb_gate", [P, 2, 2, QB], fp32))
        gate_ready, gate_used = sem("gate_ready"), sem("gate_used")
        own = sem("dve_steps")
        block = ctx.enter_context(nc.Block())
        H = T // 2

        @block.tensor
        def _(pe):
            n = 0
            for e in range(E_):
                for half in range(2):
                    if n >= 2:
                        pe.wait_ge(gate_used, n - 1)
                    for b in range(2):
                        at = half * H + b * QB
                        last = nc.tensor.matmul(spread_gate[:, half, b, :], select[:, e, :], gates[:, at:at + QB],
                                                start=True, stop=True)
                    last.then_inc(gate_ready, 1)
                    n += 1

        @block.vector
        def _(dve):
            lane = Lane(dve, own)
            n = 0
            for e in range(E_):
                for half in range(2):
                    n += 1
                    s = slice(half * H, (half + 1) * H)
                    dve.wait_ge(gate_ready, n)
                    weight = spread_gate[:, half].rearrange("p b q -> p (b q)")
                    dst = g.delta[:, s] if e == 0 else part[:, half, :]
                    nc.vector.tensor_tensor(dst, weight, expert_out[:, e, s], ALU.mult).then_inc(gate_used, 1)
                    dve.wait_ge(gate_used, n)
                    if e:
                        lane.seq(nc.vector.tensor_tensor(g.delta[:, s], part[:, half, :], g.delta[:, s], ALU.add))


DEPTH = 6
LH = 16
LD = 64
INNER = LH * LD
WIN = 32
SPAN = WIN + P
GROUP = 3
GROUPS = [list(range(a, min(a + 2 * GROUP, LH), 2)) for b in range(0, LH, 2 * GROUP) for a in (b, b + 1)]
FI = int(C * 4 * 2 / 3)
FCH = [(a, min(P, FI - a)) for a in range(0, FI, P)]
LEFT = 64
QK_SCALE = 8.0
PIECES = 6
A_RING, B_RING = PIECES + 2 + 4, 2


def hold(eng, sem):
    eng.sem_inc(sem, 1)


def shift_copy(nc, lane, held, dst, src, first, count, ready):
    hold(lane.eng, held)
    lane.seq(nc.gpsimd.tensor_copy(dst[0:C // 2, :], src[0:C // 2, bass.ds(first + LEFT, count)]))
    hold(lane.eng, held)
    nc.gpsimd.tensor_copy(dst[C // 2:C, :], src[C // 2:C, bass.ds(first + LEFT - 1, count)]).then_inc(ready, 1)


def stage_l1_ffn(nc, g, d, y):
    with ExitStack() as ctx:
        def sb(n, shape, dt=fp32):
            return ctx.enter_context(nc.sbuf_tensor(f"lw_{n}", shape, dt))

        def sem(n):
            return nc.alloc_semaphore(f"lw_{n}")
        L = Shared()
        L.sb = sb
        L.xa, L.xb = sb("xa", [C, LEFT + T + P]), sb("xb", [C, LEFT + T + P])
        L.wqkv, L.wo = sb("wqkv", [C, 3 * INNER]), sb("wo", [P, INNER // P, C])
        L.w1, L.w2 = sb("w1", [C, 2 * FI]), sb("w2", [P, len(FCH), C])
        L.scales = sb("scales", [P, 4, LD])
        L.cols = sb("cols", [P, 3 + 2 * len(FCH)])
        L.rope = sb("rope", [P, NT, 4, LD])
        L.band = sb("band", [P, 2, SPAN], bf16)
        L.ident16 = sb("ident16", [P, P], bf16)
        L.halo_scale = sb("halo_scale", [P, 1])
        L.minus_half = sb("minus_half", [P, 2 * LH])
        L.bank = ctx.enter_context(nc.psum_tensor("lw_bank", [P, 8, QB], fp32))
        band32 = sb("band32", [P, 2, SPAN])
        cleared = sem("cleared")
        L.held, L.held_sp = sem("held"), sem("held_sp")
        load(nc, "lw", [(L.rope[:], d["c_rope"]), (band32[:], d["c_band"]), (L.halo_scale[:], d["c_halo_scale"])])
        with nc.Block() as block:
            @block.vector
            def _(dve):
                nc.vector.memset(L.xa[:], 0.0).then_inc(cleared, 1)
                nc.vector.memset(L.xb[:], 0.0)
                nc.vector.tensor_copy(L.band[:], band32[:])
                nc.vector.tensor_copy(L.ident16[:], g.ident[:])
                dve.wait_ge(cleared, 1)
                nc.vector.tensor_copy(L.xa[:, LEFT:LEFT + T], g.xT[:])

            @block.gpsimd
            def _(pool):
                nc.gpsimd.memset(L.minus_half[:], -0.5)
        A = LocalAttention(nc, g, L, ctx)
        with nc.Block() as block:
            @block.scalar
            def _(act):
                act.sem_inc(A.ring_freed, 2)
        F = LocalFfn(nc, g, L, ctx)
        w_loaded = sem("w_loaded")
        with nc.Fori(0, DEPTH) as layer:
            with nc.Block() as block:
                @block.sync
                def _(sp):
                    for dst, src in ((L.wqkv[:], "L1_ffn_Wqkv"), (L.wo[:], "h_lw_wo"), (L.w1[:], "L1_ffn_W1"),
                                     (L.w2[:], "h_lw_w2"), (L.scales[:], "h_lw_scales"), (L.cols[:], "h_lw_cols")):
                        sp.dma_start(dst, d[src][layer]).then_inc(w_loaded, 16)
                    sp.wait_ge(w_loaded, 16 * 6 * (layer + 1))
                    hold(sp, L.held_sp)
            A.run(layer)
            F.run(layer)
        with nc.Block() as block:
            @block.vector
            def _(dve):
                nc.vector.tensor_copy(g.delta[:], L.xa[:, LEFT:LEFT + T])
    layernorm(nc, g, "ln3", feature=g.delta)


class LocalAttention:

    def __init__(self, nc, g, L, ctx):
        self.nc, self.g, self.L = nc, g, L

        def sem(n):
            return nc.alloc_semaphore(f"la_{n}")

        def sb(n, shape, dt=fp32):
            return ctx.enter_context(nc.sbuf_tensor(f"la_{n}", shape, dt))
        self.xs = sb("xs", [C, 2, SPAN])
        self.raw = sb("raw", [P, 2 * LH, LD])
        self.square = sb("square", [P, 2 * LH, LD])
        self.roped = sb("roped", [P, 2 * LH, LD])
        self.turn = sb("turn", [P, 2 * LH, LD])
        self.tab = sb("tab", [P, 4, LD])
        self.sumsq = sb("sumsq", [P, 2 * LH])
        self.rnorm = sb("rnorm", [P, 2, 2 * LH])
        self.qfac = sb("qfac", [P, 2, 2, LH])
        self.v = sb("v", [P, 2, INNER])
        self.vh = sb("vh", [WIN, 2, INNER])
        self.qT = sb("qT", [P, 2, LH // 2, P])
        self.kT = sb("kT", [P, 2, LH // 2, SPAN])
        self.rowmax = sb("rowmax", [P, LH])
        self.bias = sb("bias", [P, LH])
        self.rowsum = sb("rowsum", [P, LH])
        self.rrow = sb("rrow", [P, LH])
        self.p = sb("p", [P, 3, GROUP, SPAN])
        self.pT = sb("pT", [P, 2, GROUP, P])
        self.pTh = sb("pTh", [WIN, 2, GROUP, WIN])
        self.o = sb("o", [P, INNER])
        self.oT = sb("oT", [P, INNER // P, C])
        self.ring_filled = sem("ring_filled")
        self.ring_freed = sem("ring_freed")
        self.scores_ready = sem("scores_ready")
        self.bias_ready = sem("bias_ready")
        self.probs_ready = sem("probs_ready")
        self.pT_ready = sem("pT_ready")
        self.pT_copied = sem("pT_copied")
        self.out_ready = sem("out_ready")
        self.o_ready = sem("o_ready")
        self.y_ready = sem("y_ready")
        self.y_added = sem("y_added")
        self.xs_ready = sem("xs_ready")
        self.tab_ready = sem("tab_ready")
        self.squares_ready = sem("squares_ready")
        self.sums_ready = sem("sums_ready")
        self.rot_ready = sem("rot_ready")
        self.rope_done = sem("rope_done")
        self.halo_ready = sem("halo_ready")
        self.dve_steps = sem("dve_steps")
        self.act_steps = sem("act_steps")
        self.pool_steps = sem("pool_steps")
        groups = len(GROUPS)
        self.per_tile = {
            self.ring_filled: A_RING + B_RING, self.ring_freed: A_RING + B_RING,
            self.scores_ready: groups, self.bias_ready: groups, self.probs_ready: groups,
            self.pT_ready: groups, self.pT_copied: groups, self.out_ready: 1, self.o_ready: 1,
            self.y_ready: 1, self.y_added: 1, self.xs_ready: 1, self.tab_ready: 1,
            self.squares_ready: 2, self.sums_ready: 1, self.rot_ready: 2, self.rope_done: 1,
            self.halo_ready: 1, self.dve_steps: groups + 1, self.pool_steps: 7}

    def steps(self, lane, body):
        body(0, None, 0, False)
        body(1, 0, 1, True)
        with lane.loop((NT - 2) // 2, {sem: 2 * by for sem, by in self.per_tile.items()}) as i:
            body(2 * i + 2, 2 * i + 1, 0, False)
            body(2 * i + 3, 2 * i + 2, 1, False)
        body(None, NT - 1, 0, False)

    def base(self, layer, given=0):
        base = {sem: layer * by * NT for sem, by in self.per_tile.items()}
        base[self.ring_freed] = layer * (A_RING + B_RING) * NT + given
        base[self.xs_ready] = layer * (NT + 1)
        base[self.pool_steps] = layer * (7 * NT + 1)
        return base

    def check(self, lane):
        for sem, by in self.per_tile.items():
            assert lane.seen.get(sem, 0) <= by * NT + 1, (sem.name, lane.seen[sem], by * NT)

    def run(self, layer):
        nc, g, L = self.nc, self.g, self.L
        S = self
        bank = L.bank
        RING, SCORES, PT, OUT = 0, 2, 5, 6
        out = bank[:, OUT:OUT + 2, :].rearrange("p b q -> p (b q)")

        def scores_of(k):
            return bank[:, SCORES + k % 3, 0:GROUP * SPAN].rearrange("p (h s) -> p h s", s=SPAN)
        with nc.Block() as block:
            @block.gpsimd
            def _(pool):
                lane = Lane(pool, S.pool_steps, S.base(layer, given=2))
                one = nc.gpsimd

                def shifted(t, slot):
                    shift_copy(nc, lane, L.held, S.xs[:, slot, :], L.xa, t * P - WIN, SPAN, S.xs_ready)
                    lane.wait(S.xs_ready)
                    hold(pool, L.held)

                def body(a, b, s, first):
                    if a is None:
                        return
                    one.tensor_tensor(S.tab[:], L.rope[:, a, :, :], L.scales[:], ALU.mult).then_inc(S.tab_ready, 1)
                    for half in range(2):
                        hs = slice(half * LH, (half + 1) * LH)
                        lane.wait(S.ring_freed, 2)
                        one.tensor_tensor(S.square[:, hs, :], S.raw[:, hs, :], S.raw[:, hs, :],
                                          ALU.mult).then_inc(S.squares_ready, 1)
                    lane.skip(S.ring_freed, A_RING - 4 + (B_RING if b is not None else 0))
                    lane.wait(S.rot_ready, 2)
                    lane.post(one.tensor_tensor(S.roped[:, 0:LH, :], S.roped[:, 0:LH, :], S.turn[:, 0:LH, :], ALU.add))
                    lane.post(one.tensor_tensor(S.roped[:, LH:, :], S.roped[:, LH:, :], S.turn[:, LH:, :], ALU.add))
                    lane.wait(S.sums_ready)
                    lane.settle()
                    hold(pool, L.held)
                    lane.seq(one.tensor_scalar(S.sumsq[:], S.sumsq[:], 1e-24, None, ALU.max))
                    lane.seq(one.tensor_tensor(S.rnorm[:, s, :], S.sumsq[:], L.minus_half[:], ALU.pow))
                    hold(pool, L.held)
                    lane.post(one.tensor_scalar(S.qfac[:, s, 0, :], S.rnorm[:, s, 0:LH], QK_SCALE, None, ALU.mult))
                    lane.post(one.tensor_scalar(S.qfac[:, s, 1, :], S.rnorm[:, s, 0:LH], -QK_SCALE, None, ALU.mult))
                    one.tensor_tensor(S.roped[:, LH:, :], S.roped[:, LH:, :], spread(S.rnorm[:, s, LH:], LD),
                                      ALU.mult).then_inc(S.rope_done, 1)
                    lane.wait(S.rope_done)
                    shifted(a + 1, 1 - s)
                shifted(0, 0)
                S.steps(lane, body)
                S.check(lane)

            @block.tensor
            def _(pe):
                lane = Lane(pe, None, S.base(layer))
                place = [0]

                def ring():
                    lane.wait(S.ring_freed)
                    place[0] += 1
                    return bank[:, RING + (place[0] - 1) % 2, :]

                def body(a, b, s, first):
                    o = 1 - s

                    def scores(k):
                        dst = scores_of(k)
                        for i, h in enumerate(GROUPS[k]):
                            at = (h % 2) * LD
                            nc.tensor.matmul(dst[:, i, :], S.qT[at:at + LD, o, h // 2, :], S.kT[at:at + LD, o, h // 2, :],
                                             start=True, stop=False)
                            last = nc.tensor.matmul(dst[:, i, :], L.ident16[:], L.band[:, 1 if first else 0, :],
                                                    start=False, stop=True)
                        last.then_inc(S.scores_ready, 1)

                    def transpose_probs(k):
                        lane.wait(S.probs_ready)
                        for i, h in enumerate(GROUPS[k]):
                            nc.tensor.transpose(bank[:, PT, i * P:(i + 1) * P], S.p[:, k % 3, i, WIN:SPAN], g.ident[:])
                        for i, h in enumerate(GROUPS[k]):
                            at = GROUP * P + i * WIN
                            last = nc.tensor.transpose(bank[0:WIN, PT, at:at + WIN], S.p[0:WIN, k % 3, i, 0:WIN],
                                                       g.ident[0:WIN, 0:WIN])
                        last.then_inc(S.pT_ready, 1)

                    def values(k):
                        lane.wait(S.pT_copied)
                        for i, h in enumerate(GROUPS[k]):
                            cols = slice(h * LD, (h + 1) * LD)
                            nc.tensor.matmul(out[:, cols], S.pT[:, k % 2, i, :], S.v[:, o, cols], start=True, stop=True)
                            last = nc.tensor.matmul(out[0:WIN, cols], S.pTh[:, k % 2, i, :], S.vh[:, o, cols],
                                                    start=False, stop=True, skip_group_check=True)
                        return last

                    def project(j):
                        dst = ring()
                        nc.tensor.matmul(dst, S.xs[:, s, WIN:SPAN], L.wqkv[:, j * QB:(j + 1) * QB],
                                         start=True, stop=True).then_inc(S.ring_filled, 1)
                    if b is not None:
                        lane.ahead(S.ring_freed, 2)
                        lane.wait(S.halo_ready)
                        if not first:
                            lane.wait(S.y_added)
                        for k in range(3):
                            scores(k)
                    if a is not None:
                        lane.wait(S.xs_ready)
                    for k in range(PIECES):
                        if b is not None:
                            transpose_probs(k)
                            if k + 3 < PIECES:
                                scores(k + 3)
                        if a is not None:
                            project(k)
                        if b is not None:
                            last = values(k)
                    if b is not None:
                        last.then_inc(S.out_ready, 1)
                    if a is not None:
                        for j in range(2):
                            dst = ring()
                            nc.tensor.matmul(dst[0:WIN, :], S.xs[:, s, 0:WIN], L.wqkv[:, (4 + j) * QB:(5 + j) * QB],
                                             start=True, stop=True).then_inc(S.ring_filled, 1)
                    if b is not None:
                        lane.wait(S.o_ready)
                        for j in range(2):
                            dst = ring()
                            for i in range(4):
                                c = 4 * j + i
                                last = nc.tensor.transpose(dst[:, i * P:(i + 1) * P], S.o[:, c * P:(c + 1) * P], g.ident[:])
                            last.then_inc(S.ring_filled, 1)
                    if a is not None:
                        lane.wait(S.rope_done)
                        flat = S.roped[:].rearrange("p h d -> p (h d)")
                        for j in range(4):
                            dst = ring()
                            for i in range(4):
                                c = 4 * j + i
                                last = nc.tensor.transpose(dst[:, i * P:(i + 1) * P], flat[:, c * P:(c + 1) * P], g.ident[:])
                            last.then_inc(S.ring_filled, 1)
                    if b is not None:
                        if a is None:
                            lane.ahead(S.ring_freed, 2)
                        for c in range(INNER // P):
                            last = nc.tensor.matmul(out[:, 0:P], L.wo[:, c, :], S.oT[:, c, :],
                                                    start=c == 0, stop=c == INNER // P - 1)
                        last.then_inc(S.y_ready, 1)
                S.steps(lane, body)
                lane.wait(S.y_added)
                S.check(lane)

            @block.scalar
            def _(act):
                lane = Lane(act, S.act_steps, S.base(layer))
                place = [0]

                def copy(dst, rows=P, shape=None):
                    lane.wait(S.ring_filled)
                    src = bank[0:rows, RING + place[0] % 2, :]
                    place[0] += 1
                    if shape:
                        src = src.rearrange("p (a b) -> p a b", b=shape)
                    nc.scalar.copy(dst, src).then_inc(S.ring_freed, 1)

                def body(a, b, s, first):
                    o = 1 - s
                    for k in range(PIECES):
                        if b is not None:
                            lane.wait(S.bias_ready)
                            src = scores_of(k)
                            for i, h in enumerate(GROUPS[k]):
                                last = nc.scalar.activation(S.p[:, k % 3, i, :], src[:, i, :], ACT.Exp,
                                                            bias=S.bias[:, h:h + 1], scale=S.qfac[:, o, 0, h:h + 1],
                                                            accum_out=S.rowsum[:, h:h + 1])
                            last.then_inc(S.probs_ready, 1)
                        if a is not None:
                            if k < 4:
                                copy(S.raw[:, 8 * k:8 * k + 8, :], shape=LD)
                            else:
                                copy(S.v[:, s, (k - 4) * QB:(k - 3) * QB])
                    if a is not None:
                        for j in range(2):
                            copy(S.vh[:, s, j * QB:(j + 1) * QB], rows=WIN)
                    if b is not None:
                        for j in range(2):
                            copy(S.oT[:, 4 * j:4 * j + 4, :], shape=C)
                    if a is not None:
                        for j in range(2):
                            copy(S.qT[:, s, 4 * j:4 * j + 4, :], shape=P)
                        for j in range(2):
                            copy(S.kT[:, s, 4 * j:4 * j + 4, WIN:SPAN], shape=P)
                S.steps(lane, body)
                S.check(lane)

            @block.vector
            def _(dve):
                lane = Lane(dve, S.dve_steps, S.base(layer, given=2))

                def body(a, b, s, first):
                    o = 1 - s

                    def find_bias(k):
                        lane.wait(S.scores_ready)
                        src = scores_of(k)
                        h0, n = GROUPS[k][0], len(GROUPS[k])
                        hs = slice(h0, GROUPS[k][-1] + 1, 2)
                        lane.seq(nc.vector.reduce_max(S.rowmax[:, hs], src[:, 0:n, :], axis=AX.X))
                        nc.vector.tensor_tensor(S.bias[:, hs], S.rowmax[:, hs], S.qfac[:, o, 1, hs],
                                                ALU.mult).then_inc(S.bias_ready, 1)

                    def copy_probs(k):
                        lane.wait(S.pT_ready)
                        n = len(GROUPS[k])
                        nc.vector.tensor_copy(S.pT[:, k % 2, 0:n, :],
                                              bank[:, PT, 0:n * P].rearrange("p (h q) -> p h q", q=P))
                        at = GROUP * P
                        nc.vector.tensor_copy(S.pTh[:, k % 2, 0:n, :],
                                              bank[0:WIN, PT, at:at + n * WIN].rearrange("p (h q) -> p h q", q=WIN)
                                              ).then_inc(S.pT_copied, 1)

                    def rotate(half):
                        hs = slice(half * LH, (half + 1) * LH)
                        lane.wait(S.ring_freed, 2)
                        if half == 0:
                            lane.wait(S.tab_ready)
                        tab = S.tab[:, 2 * half:2 * half + 2, :]

                        def heads_of(x):
                            return x.unsqueeze(1).to_broadcast([P, LH, x.shape[-1]])
                        H2 = LD // 2
                        nc.vector.tensor_tensor(S.roped[:, hs, :], S.raw[:, hs, :], heads_of(tab[:, 0, :]), ALU.mult)
                        nc.vector.tensor_tensor(S.turn[:, hs, 0:H2], S.raw[:, hs, H2:LD], heads_of(tab[:, 1, 0:H2]), ALU.mult)
                        nc.vector.tensor_tensor(S.turn[:, hs, H2:LD], S.raw[:, hs, 0:H2], heads_of(tab[:, 1, H2:LD]),
                                                ALU.mult).then_inc(S.rot_ready, 1)
                    if b is not None:
                        lane.wait(S.rope_done)
                        if first:
                            nc.vector.memset(S.kT[:, o, :, 0:WIN], 0.0).then_inc(S.halo_ready, 1)
                        else:
                            nc.vector.tensor_scalar(S.kT[:, o, :, 0:WIN], S.kT[:, s, :, P:SPAN], L.halo_scale[:], None,
                                                    ALU.mult).then_inc(S.halo_ready, 1)
                        for k in range(3):
                            find_bias(k)
                    for k in range(PIECES):
                        if b is not None:
                            copy_probs(k)
                            if k + 3 < PIECES:
                                find_bias(k + 3)
                        if a is not None and k in (1, 3):
                            rotate(k // 2)
                    if a is not None:
                        lane.wait(S.squares_ready, 2)
                        nc.vector.reduce_sum(S.sumsq[:], S.square[:], axis=AX.X).then_inc(S.sums_ready, 1)
                    if b is not None:
                        lane.seq(nc.vector.reciprocal(S.rrow[:], S.rowsum[:]))
                        lane.wait(S.out_ready)
                        nc.vector.tensor_tensor(S.o[:].rearrange("p (h d) -> p h d", d=LD),
                                                out.rearrange("p (h d) -> p h d", d=LD), spread(S.rrow[:], LD),
                                                ALU.mult).then_inc(S.o_ready, 1)
                    lane.skip(S.ring_freed, (A_RING - 4 if a is not None else 0) + (B_RING if b is not None else 0))
                    if b is not None:
                        lane.wait(S.y_ready)
                        nc.vector.tensor_tensor(L.xb[:, bass.ds(b * P + LEFT, P)], out[:, 0:P],
                                                L.xa[:, bass.ds(b * P + LEFT, P)], ALU.add).then_inc(S.y_added, 1)
                S.steps(lane, body)
                S.check(lane)


class LocalFfn:

    def __init__(self, nc, g, L, ctx):
        self.nc, self.g, self.L = nc, g, L

        def sb(n, shape, dt=fp32):
            return ctx.enter_context(nc.sbuf_tensor(f"lf_{n}", shape, dt))
        self.xs = sb("xs", [C, 2, QB])
        self.stats = sb("stats", [P, 4, 6])
        self.meanvar = sb("meanvar", [P, 2, 4, 2])
        self.rstd = sb("rstd", [P, 2, 4])
        self.xn = sb("xn", [P, 2, 4, C])
        self.xnT = sb("xnT", [C, QB])
        self.gelu = sb("gelu", [P, 2, QB])
        self.h = sb("h", [P, len(FCH), QB])
        self.xs_ready = nc.alloc_semaphore("lf_xs_ready")
        self.turned = nc.alloc_semaphore("lf_turned")
        self.stats_ready = nc.alloc_semaphore("lf_stats_ready")
        self.rstd_ready = nc.alloc_semaphore("lf_rstd_ready")
        self.xn_ready = nc.alloc_semaphore("lf_xn_ready")
        self.xn_turned = nc.alloc_semaphore("lf_xn_turned")
        self.xnT_ready = nc.alloc_semaphore("lf_xnT_ready")
        self.gate_ready = nc.alloc_semaphore("lf_gate_ready")
        self.gelu_ready = nc.alloc_semaphore("lf_gelu_ready")
        self.a_ready = nc.alloc_semaphore("lf_a_ready")
        self.h_ready = nc.alloc_semaphore("lf_h_ready")
        self.y_ready = nc.alloc_semaphore("lf_y_ready")
        self.y_added = nc.alloc_semaphore("lf_y_added")
        self.dve_steps = nc.alloc_semaphore("lf_dve_steps")
        self.pool_steps = nc.alloc_semaphore("lf_pool_steps")

    def run(self, layer):
        nc, g, L, S = self.nc, self.g, self.L, self
        bank = L.bank
        TURN, BACK, GATE, AFACT, Y = 0, 2, 3, 5, 7
        NCH = len(FCH)

        def upto(sem, per_block, n):
            return layer * (per_block * NB) + n

        def tokens(b):
            return slice(LEFT + b * QB, LEFT + (b + 1) * QB)
        with nc.Block() as block:
            @block.gpsimd
            def _(pool):
                lane = Lane(pool, S.pool_steps, {S.pool_steps: layer * 2 * NB})

                def shifted(b):
                    if b >= 2:
                        pool.wait_ge(S.turned, upto(S.turned, 1, b - 1))
                    shift_copy(nc, lane, L.held, S.xs[:, b % 2, :], L.xb, b * QB, QB, S.xs_ready)
                    pool.wait_ge(S.xs_ready, upto(S.xs_ready, 1, b + 1))
                shifted(0)
                for b in range(NB):
                    if b + 1 < NB:
                        shifted(b + 1)
                    pool.wait_ge(S.stats_ready, upto(S.stats_ready, 1, b + 1))
                    hold(pool, L.held)
                    lane.seq(nc.gpsimd.tensor_scalar(S.rstd[:, b % 2, :], S.meanvar[:, b % 2, :, 1], LN_EPS, None, ALU.add))
                    nc.gpsimd.tensor_tensor(S.rstd[:, b % 2, :], S.rstd[:, b % 2, :], L.minus_half[:, 0:4],
                                            ALU.pow).then_inc(S.rstd_ready, 1)
                    pool.wait_ge(S.rstd_ready, upto(S.rstd_ready, 1, b + 1))

            @block.tensor
            def _(pe):
                def turn(b):
                    pe.wait_ge(S.xs_ready, upto(S.xs_ready, 1, b + 1))
                    if b >= 2:
                        pe.wait_ge(S.xn_ready, upto(S.xn_ready, 1, b - 1))
                    for t in range(4):
                        last = nc.tensor.transpose(bank[:, TURN + b % 2, t * P:(t + 1) * P],
                                                   S.xs[:, b % 2, t * P:(t + 1) * P], g.ident[:])
                    last.then_inc(S.turned, 1)
                turn(0)
                for b in range(NB):
                    if b + 1 < NB:
                        turn(b + 1)
                    pe.wait_ge(S.xn_ready, upto(S.xn_ready, 1, b + 1))
                    for t in range(4):
                        last = nc.tensor.transpose(bank[:, BACK, t * P:(t + 1) * P], S.xn[:, b % 2, t, :], g.ident[:])
                    last.then_inc(S.xn_turned, 1)
                    pe.wait_ge(S.xnT_ready, upto(S.xnT_ready, 1, b + 1))
                    for j, (at, n) in enumerate(FCH):
                        c = NCH * b + j
                        if c >= 2:
                            pe.wait_ge(S.gelu_ready, upto(S.gelu_ready, NCH, c - 1))
                        nc.tensor.matmul(bank[0:n, GATE + c % 2, :], L.w1[:, FI + at:FI + at + n], S.xnT[:],
                                         start=True, stop=True).then_inc(S.gate_ready, 1)
                        if c >= 2:
                            pe.wait_ge(S.h_ready, upto(S.h_ready, NCH, c - 1))
                        nc.tensor.matmul(bank[0:n, AFACT + c % 2, :], L.w1[:, at:at + n], S.xnT[:],
                                         start=True, stop=True).then_inc(S.a_ready, 1)
                    if b:
                        pe.wait_ge(S.y_added, upto(S.y_added, 1, b))
                    for j, (at, n) in enumerate(FCH):
                        pe.wait_ge(S.h_ready, upto(S.h_ready, NCH, NCH * b + j + 1))
                        last = nc.tensor.matmul(bank[:, Y, :], L.w2[0:n, j, :], S.h[0:n, j, :],
                                                start=j == 0, stop=j == NCH - 1)
                    last.then_inc(S.y_ready, 1)

            @block.scalar
            def _(act):
                for b in range(NB):
                    act.wait_ge(S.xn_turned, upto(S.xn_turned, 1, b + 1))
                    if b:
                        act.wait_ge(S.a_ready, upto(S.a_ready, NCH, NCH * b))
                    nc.scalar.activation(S.xnT[:], bank[:, BACK, :], ACT.Identity, bias=L.cols[:, 1:2],
                                         scale=L.cols[:, 0:1]).then_inc(S.xnT_ready, 1)
                    for j, (at, n) in enumerate(FCH):
                        c = NCH * b + j
                        act.wait_ge(S.gate_ready, upto(S.gate_ready, NCH, c + 1))
                        if c >= 2:
                            act.wait_ge(S.h_ready, upto(S.h_ready, NCH, c - 1))
                        nc.scalar.activation(S.gelu[0:n, c % 2, :], bank[0:n, GATE + c % 2, :], ACT.Gelu,
                                             bias=L.cols[0:n, 3 + NCH + j:4 + NCH + j]).then_inc(S.gelu_ready, 1)

            @block.vector
            def _(dve):
                lane = Lane(dve, S.dve_steps, {S.dve_steps: layer * 4 * NB})

                def normalise(b):
                    dve.wait_ge(S.turned, upto(S.turned, 1, b + 1))
                    src = bank[:, TURN + b % 2, :].rearrange("p (t c) -> p t c", c=C)
                    for t in range(4):
                        lane.post(nc.vector.bn_stats(S.stats[:, t, :], src[:, t, :]))
                    lane.settle()
                    hold(dve, L.held)
                    for t in range(4):
                        last = nc.vector.bn_aggr(S.meanvar[:, b % 2, t, :], S.stats[:, t, :])
                    last.then_inc(S.stats_ready, 1)
                    dve.wait_ge(S.stats_ready, upto(S.stats_ready, 1, b + 1))
                    dve.wait_ge(S.rstd_ready, upto(S.rstd_ready, 1, b + 1))
                    if b >= 2:
                        dve.wait_ge(S.xn_turned, upto(S.xn_turned, 1, b - 1))
                    for t in range(4):
                        last = nc.vector.tensor_scalar(S.xn[:, b % 2, t, :], src[:, t, :], S.meanvar[:, b % 2, t, 0:1],
                                                       S.rstd[:, b % 2, t:t + 1], ALU.subtract, ALU.mult)
                    last.then_inc(S.xn_ready, 1)
                normalise(0)
                for b in range(NB):
                    if b + 1 < NB:
                        normalise(b + 1)
                    for j, (at, n) in enumerate(FCH):
                        c = NCH * b + j
                        dve.wait_ge(S.a_ready, upto(S.a_ready, NCH, c + 1))
                        dve.wait_ge(S.gelu_ready, upto(S.gelu_ready, NCH, c + 1))
                        nc.vector.scalar_tensor_tensor(S.h[0:n, j, :], bank[0:n, AFACT + c % 2, :], L.cols[0:n, 3 + j:4 + j],
                                                       S.gelu[0:n, c % 2, :], ALU.add, ALU.mult).then_inc(S.h_ready, 1)
                    dve.wait_ge(S.y_ready, upto(S.y_ready, 1, b + 1))
                    nc.vector.scalar_tensor_tensor(L.xa[:, tokens(b)], bank[:, Y, :], L.cols[:, 2:3], L.xb[:, tokens(b)],
                                                   ALU.add, ALU.add).then_inc(S.y_added, 1)


DI = 256
DT = DI // P
NS = 16
RANK = 8
TAPS = 4
SERIES_BELOW = 0.01


def stage_l2_attn(nc, g, d, y):
    with ExitStack() as ctx:
        def sb(n, shape, dt=fp32):
            return ctx.enter_context(nc.sbuf_tensor(f"l2a_{n}", shape, dt))
        shapes = {"w_in": [C, 4 * P], "w_out": [P, DT, C], "xproj": [P, DT, RANK + 2 * NS], "w_dt": [RANK, DI],
                  "cols": [P, DT, TAPS + 3], "a_log": [P, DT, NS]}
        w = {n: sb(n, s) for n, s in shapes.items()}
        select = sb("select", [NS, NS, P])
        load(nc, "l2a", [(t[:], d["h_l2_" + n]) for n, t in w.items()] + [(select[:], d["c_select16"])])
        xc, zs = sb("xc", [P, DT, T]), sb("zs", [P, DT, T])
        step, dx = sb("step", [P, DT, T]), sb("dx", [P, DT, T])
        bT, cT = sb("bT", [NS, T]), sb("cT", [NS, T])
        ysum = sb("ysum", [P, DT, T])
        scan_inputs(nc, g, w, xc, zs)
        scan_steps(nc, g, w, xc, step, dx, bT, cT)
        scan_states(nc, g, w, select, xc, zs, step, dx, bT, cT, ysum)
    layernorm(nc, g, "ln4", feature=g.delta)


def scan_inputs(nc, g, w, xc, zs):
    with ExitStack() as ctx:
        def sb(n, shape, dt=fp32):
            return ctx.enter_context(nc.sbuf_tensor(f"si_{n}", shape, dt))

        def sem(n):
            return nc.alloc_semaphore(f"si_{n}")
        padded = sb("padded", [P, DT, TAPS - 1 + T])
        conv = sb("conv", [P, DT, T])
        acc = [ctx.enter_context(nc.psum_tensor(f"si_acc{i}", [P, NB, QB], fp32)) for i in range(2)]
        made, taken = sem("made"), sem("taken")
        conv_ready = sem("conv_ready")
        z_taken = sem("z_taken")
        own = sem("dve_steps")
        block = ctx.enter_context(nc.Block())

        def flat(i):
            return acc[i][:, :, :].rearrange("p b q -> p (b q)")

        @block.tensor
        def _(pe):
            for m in range(2 * DT):
                if m >= 2:
                    pe.wait_ge(taken, m - 1)
                for b in range(NB):
                    last = nc.tensor.matmul(acc[m % 2][:, b, :], w["w_in"][:, m * P:(m + 1) * P],
                                            g.xT[:, b * QB:(b + 1) * QB], start=True, stop=True)
                last.then_inc(made, 1)

        @block.vector
        def _(dve):
            lane = Lane(dve, own)
            lane.post(nc.vector.memset(padded[:, :, 0:TAPS - 1], 0.0))
            for m in range(DT):
                dve.wait_ge(made, m + 1)
                nc.vector.tensor_copy(padded[:, m, TAPS - 1:], flat(m)).then_inc(taken, 1)
            dve.wait_ge(taken, DT)
            lane.settle()
            for m in range(DT):
                lane.seq(nc.vector.tensor_scalar(conv[:, m, :], padded[:, m, 0:T], w["cols"][:, m, 0:1], None, ALU.mult))
                for j in range(1, TAPS):
                    ins = nc.vector.scalar_tensor_tensor(conv[:, m, :], padded[:, m, j:j + T], w["cols"][:, m, j:j + 1],
                                                         conv[:, m, :], ALU.mult, ALU.add)
                    if j < TAPS - 1:
                        lane.seq(ins)
                ins.then_inc(conv_ready, 1)

        @block.scalar
        def _(act):
            for m in range(DT):
                act.wait_ge(made, DT + m + 1)
                nc.scalar.activation(zs[:, m, :], flat(m), ACT.Silu)
            for m in range(DT):
                act.wait_ge(conv_ready, m + 1)
                nc.scalar.activation(xc[:, m, :], conv[:, m, :], ACT.Silu, bias=w["cols"][:, m, TAPS:TAPS + 1])


def scan_steps(nc, g, w, xc, step, dx, bT, cT):
    with ExitStack() as ctx:
        def sb(n, shape, dt=fp32):
            return ctx.enter_context(nc.sbuf_tensor(f"ss_{n}", shape, dt))

        def sem(n):
            return nc.alloc_semaphore(f"ss_{n}")
        low = sb("low", [RANK, T])
        raw, ex, one_ex = (sb(n, [P, DT, T]) for n in ("raw", "ex", "one_ex"))
        ps = [ctx.enter_context(nc.psum_tensor(f"ss_ps{i}", [P, NB, QB], fp32)) for i in range(2)]
        made, taken = sem("made"), sem("taken")
        low_ready = sem("low_ready")
        raw_ready, abs_ready, ex_ready, one_ready, ln_ready = (sem(n) for n in ("raw_ready", "abs_ready", "ex_ready", "one_ready", "ln_ready"))
        own = sem("dve_steps")
        block = ctx.enter_context(nc.Block())

        def flat(i, rows=P):
            return ps[i][0:rows, :, :].rearrange("p b q -> p (b q)")

        @block.tensor
        def _(pe):
            for n, (at, rows) in enumerate(((0, RANK), (RANK, NS), (RANK + NS, NS))):
                if n >= 2:
                    pe.wait_ge(taken, n - 1)
                for b in range(NB):
                    for m in range(DT):
                        last = nc.tensor.matmul(ps[n % 2][0:rows, b, :], w["xproj"][:, m, at:at + rows],
                                                xc[:, m, b * QB:(b + 1) * QB], start=m == 0, stop=m == DT - 1)
                last.then_inc(made, 1)
            for m in range(DT):
                pe.wait_ge(taken, 2 + m)
                for b in range(NB):
                    last = nc.tensor.matmul(ps[(m + 1) % 2][:, b, :], w["w_dt"][:, m * P:(m + 1) * P],
                                            low[:, b * QB:(b + 1) * QB], start=True, stop=True)
                last.then_inc(made, 1)

        @block.vector
        def _(dve):
            lane = Lane(dve, own)
            for n, (dst, rows) in enumerate(((low, RANK), (bT, NS), (cT, NS))):
                dve.wait_ge(made, n + 1)
                nc.vector.tensor_copy(dst[:], flat(n % 2, rows)).then_inc(taken, 1)
            for m in range(DT):
                dve.wait_ge(made, 4 + m)
                nc.vector.tensor_scalar(raw[:, m, :], flat((m + 1) % 2), w["cols"][:, m, TAPS + 1:TAPS + 2], None,
                                        ALU.add).then_inc(raw_ready, 1)
            dve.wait_ge(ex_ready, 1)
            lane.post(nc.vector.tensor_scalar(dx[:], ex[:], -0.25, 1.0 / 3.0, ALU.mult, ALU.add))
            nc.vector.tensor_scalar(one_ex[:], ex[:], 1.0, None, ALU.add).then_inc(one_ready, 1)
            lane.settle()
            lane.seq(nc.vector.tensor_tensor(dx[:], dx[:], ex[:], ALU.mult))
            lane.seq(nc.vector.scalar_tensor_tensor(dx[:], dx[:], -0.5, ex[:], ALU.add, ALU.mult))
            lane.seq(nc.vector.scalar_tensor_tensor(dx[:], dx[:], 1.0, ex[:], ALU.add, ALU.mult))
            dve.wait_ge(ln_ready, 1)
            lane.seq(nc.vector.tensor_tensor(dx[:], dx[:], step[:], ALU.subtract))
            lane.seq(nc.vector.scalar_tensor_tensor(dx[:], ex[:], SERIES_BELOW, dx[:], ALU.is_lt, ALU.mult))
            lane.seq(nc.vector.scalar_tensor_tensor(step[:], raw[:], 0.0, step[:], ALU.max, ALU.add))
            lane.seq(nc.vector.tensor_tensor(step[:], step[:], dx[:], ALU.add))
            nc.vector.tensor_tensor(dx[:], step[:], xc[:], ALU.mult)

        @block.scalar
        def _(act):
            act.wait_ge(raw_ready, DT)
            nc.scalar.activation(ex[:], raw[:], ACT.Abs).then_inc(abs_ready, 1)
            act.wait_ge(abs_ready, 1)
            nc.scalar.activation(ex[:], ex[:], ACT.Exp, scale=-1.0).then_inc(ex_ready, 1)
            act.wait_ge(one_ready, 1)
            nc.scalar.activation(step[:], one_ex[:], ACT.Ln).then_inc(ln_ready, 1)


def scan_states(nc, g, w, select, xc, zs, step, dx, bT, cT, ysum):
    with ExitStack() as ctx:
        def sb(n, shape, dt=fp32):
            return ctx.enter_context(nc.sbuf_tensor(f"st_{n}", shape, dt))

        def sem(n):
            return nc.alloc_semaphore(f"st_{n}")
        a = sb("a", [P, DT, NS])
        bn, cn = sb("bn", [P, 2, T]), sb("cn", [P, 2, T])
        decay = sb("decay", [P, 2, T])
        h = g.delta
        hc = sb("hc", [P, 2, T])
        bps = ctx.enter_context(nc.psum_tensor("st_bps", [P, NB, QB], fp32))
        cps = ctx.enter_context(nc.psum_tensor("st_cps", [P, NB, QB], fp32))
        a_exp, a_ready = sem("a_exp"), sem("a_ready")
        spread_ready = sem("spread_ready")
        spread_copied = sem("spread_copied")
        decay_ready = sem("decay_ready")
        scanned = sem("scanned")
        hc_ready = sem("hc_ready")
        added = sem("added")
        y_ready = sem("y_ready")
        out_ready = sem("out_ready")
        own = sem("dve_steps")
        block = ctx.enter_context(nc.Block())

        @block.tensor
        def _(pe):
            for n in range(NS):
                for i, (ps, src) in enumerate(((bps, bT), (cps, cT))):
                    if n:
                        pe.wait_ge(spread_copied, 2 * n - 1 + i)
                    for b in range(NB):
                        last = nc.tensor.matmul(ps[:, b, :], select[:, n, :], src[:, b * QB:(b + 1) * QB],
                                                start=True, stop=True)
                    last.then_inc(spread_ready, 1)
            pe.wait_ge(y_ready, DT)
            pe.wait_ge(spread_copied, 2 * NS)
            for b in range(NB):
                for m in range(DT):
                    last = nc.tensor.matmul(bps[:, b, :], w["w_out"][:, m, :], ysum[:, m, b * QB:(b + 1) * QB],
                                            start=m == 0, stop=m == DT - 1)
            last.then_inc(out_ready, 1)

        @block.scalar
        def _(act):
            nc.scalar.activation(a[:], w["a_log"][:], ACT.Exp).then_inc(a_exp, 1)
            act.wait_ge(a_ready, 1)
            for n in range(NS):
                for i, (ps, dst) in enumerate(((bps, bn), (cps, cn))):
                    act.wait_ge(spread_ready, 2 * n + i + 1)
                    if n >= 2:
                        act.wait_ge(hc_ready, DT * (n - 1))
                    nc.scalar.copy(dst[:, n % 2, :], ps[:, :, :].rearrange("p b q -> p (b q)")).then_inc(spread_copied, 1)
                for m in range(DT):
                    k = DT * n + m
                    if k >= 2:
                        act.wait_ge(scanned, k - 1)
                    nc.scalar.activation(decay[:, k % 2, :], step[:, m, :], ACT.Exp,
                                         scale=a[:, m, n:n + 1]).then_inc(decay_ready, 1)

        @block.vector
        def _(dve):
            lane = Lane(dve, own)
            dve.wait_ge(a_exp, 1)
            nc.vector.tensor_scalar(a[:], a[:], -1.0, None, ALU.mult).then_inc(a_ready, 1)
            for n in range(NS):
                dve.wait_ge(spread_copied, 2 * n + 2)
                for m in range(DT):
                    k = DT * n + m
                    if k >= 2:
                        dve.wait_ge(added, k - 1)
                    lane.seq(nc.vector.tensor_tensor(hc[:, k % 2, :], dx[:, m, :], bn[:, n % 2, :], ALU.mult))
                    dve.wait_ge(decay_ready, k + 1)
                    if k:
                        dve.wait_ge(hc_ready, k)
                    nc.vector.tensor_tensor_scan(h[:], decay[:, k % 2, :], hc[:, k % 2, :], 0.0,
                                                 ALU.mult, ALU.add).then_inc(scanned, 1)
                    dve.wait_ge(scanned, k + 1)
                    nc.vector.tensor_tensor(hc[:, k % 2, :], h[:], cn[:, n % 2, :], ALU.mult).then_inc(hc_ready, 1)
            dve.wait_ge(added, DT * NS)
            for m in range(DT):
                lane.seq(nc.vector.scalar_tensor_tensor(ysum[:, m, :], xc[:, m, :], w["cols"][:, m, TAPS + 2:TAPS + 3],
                                                        ysum[:, m, :], ALU.mult, ALU.add))
                nc.vector.tensor_tensor(ysum[:, m, :], ysum[:, m, :], zs[:, m, :], ALU.mult).then_inc(y_ready, 1)
            dve.wait_ge(out_ready, 1)
            nc.vector.tensor_copy(g.delta[:], bps[:, :, :].rearrange("p b q -> p (b q)"))

        @block.gpsimd
        def _(pool):
            for k in range(DT * NS):
                m = k % DT
                pool.wait_ge(hc_ready, k + 1)
                if k < DT:
                    nc.gpsimd.tensor_copy(ysum[:, m, :], hc[:, k % 2, :]).then_inc(added, 1)
                else:
                    pool.wait_ge(added, k - 1)
                    nc.gpsimd.tensor_tensor(ysum[:, m, :], hc[:, k % 2, :], ysum[:, m, :], ALU.add).then_inc(added, 1)


def stage_l2_ffn(nc, g, d, y):
    with ExitStack() as ctx:
        def sb(n, shape, dt=fp32):
            return ctx.enter_context(nc.sbuf_tensor(f"l2f_{n}", shape, dt))

        def sem(n):
            return nc.alloc_semaphore(f"l2f_{n}")
        w = {n: sb(n, [P, P]) for n in ("rT", "kT", "vT")}
        mu = sb("mu", [P, 4])
        load(nc, "l2f", [(t[:], d["h_l2f_" + n]) for n, t in w.items()] + [(mu[:, 0:2], d["h_l2f_mu"])])
        mixed = sb("mixed", [P, 2, T])
        r = sb("r", [P, T])
        k = sb("k", [P, NB, QB])
        ps = ctx.enter_context(nc.psum_tensor("l2f_ps", [P, 2, NB, QB], fp32))
        mixed_ready = sem("mixed_ready")
        made, v_made = sem("made"), sem("v_made")
        sig, k_sq = sem("sig"), sem("k_sq")
        own, act_own = sem("dve_steps"), sem("act_steps")
        with nc.Block() as block:
            @block.vector
            def _(dve):
                lane = Lane(dve, own)
                lane.seq(nc.vector.tensor_scalar(mu[:, 2:4], mu[:, 0:2], -1.0, 1.0, ALU.mult, ALU.add))
                for i in range(2):
                    lane.seq(nc.vector.tensor_scalar(mixed[:, i, :], g.xT[:], mu[:, i:i + 1], None, ALU.mult))
                    nc.vector.scalar_tensor_tensor(mixed[:, i, 1:T], g.xT[:, 0:T - 1], mu[:, 2 + i:3 + i],
                                                   mixed[:, i, 1:T], ALU.mult, ALU.add).then_inc(mixed_ready, 1)
                for b in range(NB):
                    dve.wait_ge(v_made, b + 1)
                    s = slice(b * QB, (b + 1) * QB)
                    nc.vector.tensor_tensor(g.delta[:, s], ps[:, 1, b, :], r[:, s], ALU.mult)

            @block.tensor
            def _(pe):
                for i, n in enumerate(("rT", "kT")):
                    pe.wait_ge(mixed_ready, i + 1)
                    for b in range(NB):
                        nc.tensor.matmul(ps[:, i, b, :], w[n][:], mixed[:, i, b * QB:(b + 1) * QB],
                                         start=True, stop=True).then_inc(made, 1)
                for b in range(NB):
                    pe.wait_ge(k_sq, b + 1)
                    nc.tensor.matmul(ps[:, 1, b, :], w["vT"][:], k[:, b, :], start=True, stop=True).then_inc(v_made, 1)

            @block.scalar
            def _(act):
                act.wait_ge(made, NB)
                nc.scalar.activation(r[:], ps[:, 0].rearrange("p b q -> p (b q)"), ACT.Sigmoid).then_inc(act_own, 1)
                for b in range(NB):
                    act.wait_ge(made, NB + b + 1)
                    nc.scalar.activation(k[:, b, :], ps[:, 1, b, :], ACT.Relu).then_inc(act_own, 1)
                    act.wait_ge(act_own, b + 2)
                    nc.scalar.activation(k[:, b, :], k[:, b, :], ACT.Square).then_inc(k_sq, 1)
    layernorm(nc, g, "ln5", feature=g.delta)


HI = 352
HT = 3
FP4_BLOCK = 16


def quantise(nc, lane, x, out, scale, inv, a, hi, absolute, absolute_ready, sign, sign_ready, n):
    lane.eng.wait_ge(absolute_ready, n)
    lane.seq(nc.vector.reduce_max(scale, absolute, axis=AX.X))
    lane.seq(nc.vector.tensor_scalar(scale, scale, 1.0 / 6.0, 1e-12, ALU.mult, ALU.max))
    lane.seq(nc.vector.reciprocal(inv, scale))
    lane.seq(nc.vector.tensor_tensor(a, absolute, spread(inv, FP4_BLOCK), ALU.mult))
    lane.post(nc.vector.tensor_scalar(hi, a, 5.0, 2.0, ALU.is_gt, ALU.mult))
    lane.seq(nc.vector.tensor_scalar(out, a, 0.25, None, ALU.is_gt))
    for high, low in ((3.5, 0.75), (2.5, 1.25)):
        lane.post(nc.vector.scalar_tensor_tensor(hi, a, high, hi, ALU.is_gt, ALU.add))
        lane.seq(nc.vector.scalar_tensor_tensor(out, a, low, out, ALU.is_gt, ALU.add))
    lane.seq(nc.vector.scalar_tensor_tensor(out, a, 1.75, out, ALU.is_gt, ALU.add))
    lane.seq(nc.vector.scalar_tensor_tensor(out, hi, 2.0, out, ALU.mult, ALU.add))
    lane.post(nc.vector.tensor_scalar(scale, scale, 0.5, None, ALU.mult))
    lane.eng.wait_ge(sign_ready, n)
    lane.seq(nc.vector.tensor_tensor(out, out, sign, ALU.mult))
    return nc.vector.tensor_tensor(out, out, spread(scale, FP4_BLOCK), ALU.mult)


def stage_l3_ffn(nc, g, d, y):
    with ExitStack() as ctx:
        def sb(n, shape, dt=fp32):
            return ctx.enter_context(nc.sbuf_tensor(f"l3f_{n}", shape, dt))
        WC = 2 * HT * C + HI
        raw = sb("raw", [P, WC + NT * C])
        out = sb("out", [P, WC + NT * C])
        load(nc, "l3f", [(raw[:, 0:WC], d["h_l3f_w"])])
        wT = sb("wT", [P, 2 * HT, P])
        wdT = sb("wdT", [P, HT, C])
        xqT = sb("xqT", [C, T])
        quantise_inputs(nc, g, raw, out, WC, wT, wdT, xqT)
        gated_ffn(nc, g, wT, wdT, xqT)
    layernorm(nc, g, "ln7", token=g.delta[:].rearrange("p (t c) -> p t c", c=C), out_dram=y)


def quantise_inputs(nc, g, raw, out, WC, wT, wdT, xqT):
    with ExitStack() as ctx:
        def sb(n, shape, dt=fp32):
            return ctx.enter_context(nc.sbuf_tensor(f"qi_{n}", shape, dt))

        def sem(n):
            return nc.alloc_semaphore(f"qi_{n}")
        total = WC + NT * C
        absolute, a, hi, sign = (sb(n, [P, total]) for n in ("absolute", "a", "hi", "sign"))
        scale, inv = sb("scale", [P, total // FP4_BLOCK]), sb("inv", [P, total // FP4_BLOCK])
        wps = ctx.enter_context(nc.psum_tensor("qi_wps", [P, 4, QB], fp32))
        xps = ctx.enter_context(nc.psum_tensor("qi_xps", [P, 4, QB], fp32))
        x_copied, absolute_ready, sign_ready, done = (sem(n) for n in ("x_copied", "absolute_ready", "sign_ready", "done"))
        turned, own, copied = sem("turned"), sem("dve_steps"), sem("copied")
        block = ctx.enter_context(nc.Block())

        def blocks(t):
            return t[:].rearrange("p (b k) -> p b k", k=FP4_BLOCK)

        @block.vector
        def _(dve):
            lane = Lane(dve, own)
            nc.vector.tensor_copy(raw[:, WC:], g.x[:].rearrange("p t c -> p (t c)")).then_inc(x_copied, 1)
            quantise(nc, lane, blocks(raw), blocks(out), scale[:], inv[:], blocks(a), blocks(hi),
                     blocks(absolute), absolute_ready, blocks(sign), sign_ready, 1).then_inc(done, 1)
            dve.wait_ge(turned, 1)
            nc.vector.tensor_copy(wT[:, 0:3, :], wps[:, 0, 0:3 * P].rearrange("p (t c) -> p t c", c=P))
            nc.vector.tensor_copy(wT[:, 3:6, :], wps[:, 1, 0:3 * P].rearrange("p (t c) -> p t c", c=P))
            nc.vector.tensor_copy(wdT[:, 0:2, :], wps[:, 2, 0:2 * P].rearrange("p (t c) -> p t c", c=P))
            nc.vector.tensor_copy(wdT[0:HI - 2 * P, 2, :], wps[0:HI - 2 * P, 2, 2 * P:3 * P])

        @block.scalar
        def _(act):
            act.wait_ge(x_copied, 1)
            nc.scalar.activation(absolute[:], raw[:], ACT.Abs).then_inc(absolute_ready, 1)
            nc.scalar.activation(sign[:], raw[:], ACT.Sign).then_inc(sign_ready, 1)
            act.wait_ge(turned, 2)
            nc.scalar.copy(xqT[:], xps[:, :, :].rearrange("p b q -> p (b q)"))

        @block.tensor
        def _(pe):
            pe.wait_ge(done, 1)
            for i in range(2):
                for t in range(HT):
                    nc.tensor.transpose(wps[:, i, t * P:(t + 1) * P], out[:, (i * HT + t) * C:(i * HT + t + 1) * C], g.ident[:])
            for t in range(HT):
                rows = min(P, HI - t * P)
                at = 2 * HT * C + t * P
                last = nc.tensor.transpose(wps[0:rows, 2, t * P:(t + 1) * P], out[:, at:at + rows], g.ident[:])
            last.then_inc(turned, 1)
            for t in range(NT):
                last = nc.tensor.transpose(xps[:, t // 4, (t % 4) * P:(t % 4 + 1) * P], out[:, WC + t * C:WC + (t + 1) * C], g.ident[:])
            last.then_inc(turned, 1)


def gated_ffn(nc, g, wT, wdT, xqT):
    with ExitStack() as ctx:
        def sb(n, shape, dt=fp32):
            return ctx.enter_context(nc.sbuf_tensor(f"gf_{n}", shape, dt))

        def sem(n):
            return nc.alloc_semaphore(f"gf_{n}")
        G = 4
        W = G * HI
        silu = sb("silu", [P, HI])
        h = sb("h", [P, 2, W])
        out = sb("out", [P, 2, W])
        absolute, sign = sb("absolute", [P, 2, W]), sb("sign", [P, 2, W])
        a, hi = sb("a", [P, W]), sb("hi", [P, W])
        scale, inv = sb("scale", [P, W // FP4_BLOCK]), sb("inv", [P, W // FP4_BLOCK])
        hT = sb("hT", [P, 2, HT, P])
        gate_ps = ctx.enter_context(nc.psum_tensor("gf_gate", [P, 2, QB], fp32))
        up_ps = ctx.enter_context(nc.psum_tensor("gf_up", [P, 2, QB], fp32))
        hT_ps = ctx.enter_context(nc.psum_tensor("gf_hT_bank", [P, 2, QB], fp32))
        y_ps = ctx.enter_context(nc.psum_tensor("gf_y", [P, 2, QB], fp32))
        made = sem("made")
        silu_ready = sem("silu_ready")
        h_ready = sem("h_ready")
        absolute_ready, sign_ready = sem("absolute_ready"), sem("sign_ready")
        quantised = sem("quantised")
        turned = sem("turned")
        hT_copied = sem("hT_copied")
        y_made = sem("y_made")
        y_copied = sem("y_copied")
        own, own_act = sem("dve_steps"), sem("act_steps")
        block = ctx.enter_context(nc.Block())
        groups = NT // G

        def blocks(t):
            return t.rearrange("p (b k) -> p b k", k=FP4_BLOCK)

        @block.tensor
        def _(pe):
            def up(k):
                for t in range(k * G, (k + 1) * G):
                    if t >= 2:
                        pe.wait_ge(h_ready, t - 1)
                    s = slice(t * P, (t + 1) * P)
                    nc.tensor.matmul(gate_ps[:, t % 2, 0:HI], xqT[:, s], wT[:, 0:3, :].rearrange("p t c -> p (t c)")[:, 0:HI],
                                     start=True, stop=True)
                    nc.tensor.matmul(up_ps[:, t % 2, 0:HI], xqT[:, s], wT[:, 3:6, :].rearrange("p t c -> p (t c)")[:, 0:HI],
                                     start=True, stop=True).then_inc(made, 1)

            def down(k):
                pe.wait_ge(quantised, k + 1)
                for t in range(k * G, (k + 1) * G):
                    at = (t % G) * HI
                    if t >= 2:
                        pe.wait_ge(hT_copied, t - 1)
                    for j in range(HT):
                        rows = min(P, HI - j * P)
                        last = nc.tensor.transpose(hT_ps[0:rows, t % 2, j * P:(j + 1) * P],
                                                   out[:, k % 2, at + j * P:at + j * P + rows], g.ident[:])
                    last.then_inc(turned, 1)
                    pe.wait_ge(hT_copied, t + 1)
                    if t >= 2:
                        pe.wait_ge(y_copied, t - 1)
                    for j in range(HT):
                        rows = min(P, HI - j * P)
                        last = nc.tensor.matmul(y_ps[:, t % 2, 0:C], hT[0:rows, t % 2, j, :], wdT[0:rows, j, :],
                                                start=j == 0, stop=j == HT - 1)
                    last.then_inc(y_made, 1)
            up(0)
            for k in range(groups):
                if k + 1 < groups:
                    up(k + 1)
                down(k)

        @block.scalar
        def _(act):
            def silus(k):
                for t in range(k * G, (k + 1) * G):
                    act.wait_ge(made, t + 1)
                    if t >= 1:
                        act.wait_ge(h_ready, t)
                    nc.scalar.activation(silu[:], gate_ps[:, t % 2, 0:HI], ACT.Silu).then_inc(silu_ready, 1)
                act.wait_ge(h_ready, (k + 1) * G)
                if k >= 2:
                    act.wait_ge(quantised, k - 1)
                nc.scalar.activation(absolute[:, k % 2, :], h[:, k % 2, :], ACT.Abs).then_inc(absolute_ready, 1)
                nc.scalar.activation(sign[:, k % 2, :], h[:, k % 2, :], ACT.Sign).then_inc(sign_ready, 1)

            def copies(k):
                for t in range(k * G, (k + 1) * G):
                    act.wait_ge(turned, t + 1)
                    nc.scalar.copy(hT[:, t % 2, 0:2, :], hT_ps[:, t % 2, 0:2 * P].rearrange("p (t c) -> p t c", c=P)).then_inc(own_act, 1)
                    nc.scalar.copy(hT[0:HI - 2 * P, t % 2, 2, :], hT_ps[0:HI - 2 * P, t % 2, 2 * P:3 * P]).then_inc(hT_copied, 1)
                    act.wait_ge(y_made, t + 1)
                    nc.scalar.copy(g.delta[:, t * C:(t + 1) * C], y_ps[:, t % 2, 0:C]).then_inc(y_copied, 1)
            silus(0)
            for k in range(groups):
                if k + 1 < groups:
                    silus(k + 1)
                copies(k)

        @block.vector
        def _(dve):
            lane = Lane(dve, own)

            def products(k):
                for t in range(k * G, (k + 1) * G):
                    dve.wait_ge(silu_ready, t + 1)
                    at = (t % G) * HI
                    nc.vector.tensor_tensor(h[:, k % 2, at:at + HI], up_ps[:, t % 2, 0:HI], silu[:], ALU.mult).then_inc(h_ready, 1)

            def quantised_group(k):
                quantise(nc, lane, None, blocks(out[:, k % 2, :]), scale[:], inv[:], blocks(a[:]), blocks(hi[:]),
                         blocks(absolute[:, k % 2, :]), absolute_ready, blocks(sign[:, k % 2, :]), sign_ready,
                         k + 1).then_inc(quantised, 1)
                dve.wait_ge(quantised, k + 1)
            products(0)
            for k in range(groups):
                if k + 1 < groups:
                    products(k + 1)
                if k >= 2:
                    dve.wait_ge(turned, G * (k - 1))
                quantised_group(k)


KEY_SCALE_MAX = float(np.log(2 ** 16 - 1))
PER_OWN = {"l0": 5, "l1": 8, "l3": 0}


class Shared:
    pass


def load(nc, name, pairs):
    loaded = nc.alloc_semaphore(f"{name}_loaded")
    with nc.Block() as block:
        half = (len(pairs) + 1) // 2

        @block.sync
        def _(sp):
            for dst, src in pairs[:half]:
                sp.dma_start(dst, src).then_inc(loaded, 16)
            sp.wait_ge(loaded, 16 * len(pairs))

        @block.scalar
        def _(act):
            for dst, src in pairs[half:]:
                act.dma_start(dst, src).then_inc(loaded, 16)


def build(nc, d, y, dbg=None, upto=99, only=None):
    ctx = ExitStack()
    with ctx:
        g = Shared()
        def keep(n, shape, dt=fp32):
            return ctx.enter_context(nc.sbuf_tensor(n, shape, dt))
        g.x = keep("x", [P, NT, C])
        g.xT = keep("xT", [C, T])
        g.delta = keep("delta", [P, T])
        consts = {"ident": [P, P], "ones": [P, P], "e0": [P, 1], "head_ones": [P, P],
                  "mask_strict_q": [P, P], "mask_strict_k": [P, P], "mask_q": [P, P], "mask_k": [P, P]}
        consts = {n: keep(n, shape) for n, shape in consts.items()}
        g.ident, g.ones, g.e0, g.head_ones = (consts[n] for n in ("ident", "ones", "e0", "head_ones"))
        g.mask_strict_q, g.mask_strict_k = consts["mask_strict_q"], consts["mask_strict_k"]
        g.mask_q, g.mask_k = consts["mask_q"], consts["mask_k"]
        load(nc, "consts", [(t[:], d["c_" + n]) for n, t in consts.items()]
             + [(g.x[:], d["L0_attn_x"].rearrange("b (t p) c -> p (b t) c", p=P)),
                (g.xT[:], d["h_xT"])])
        stages = [stage_l0_attn, stage_l0_ffn, stage_l1_attn, stage_l1_ffn,
                  stage_l2_attn, stage_l2_ffn, stage_l3_attn, stage_l3_ffn]
        for n, s in enumerate(stages):
            if n > upto or (only is not None and n != only):
                continue
            with nc.cleanup_on_exit():
                s(nc, g, d, y if n == 7 else None)
            nc.all_engine_barrier()
            if dbg is not None and (n == upto or n == only) and n < 7:
                load(nc, "debug", [(dbg.rearrange("(t p) c -> p t c", p=P), g.x[:])])


def stage_l0_attn(nc, g, d, y):
    with ExitStack() as ctx:
        def sb(n, shape, dt=fp32):
            return ctx.enter_context(nc.sbuf_tensor(f"l0a_{n}", shape, dt))
        names = {"kT": [P, P], "vT": [P, P], "beta": [P, 1], "key_scale": [P, 1], "v_coef": [P, 1], "val_scale": [P, 1]}
        w = {n: sb(n, shape) for n, shape in names.items()}
        wo = sb("wo", [9, 16, C])
        pick = sb("pick", [P, 16, 18])
        load(nc, "l0a", [(t[:], d["h_l0_" + n]) for n, t in w.items()] + [(wo[:], d["h_l0_wo"]), (pick[:], d["c_pick8"])])
        keys, values = sb("keys", [C, T]), sb("values", [C, T])
        zero(nc, "l0a", g.delta)
        decayed_keys(nc, g, {n: t[:] for n, t in w.items()}, keys, values)
        attention(nc, g, "l0", 16, 8, keys, values, pick, wo, 1.0, g.delta, causal="strict", separate_q=False)
    layernorm(nc, g, "ln0", feature=g.delta)


def zero(nc, name, t):
    with nc.Block() as block:
        @block.gpsimd
        def _(pool):
            nc.gpsimd.memset(t[:], 0.0)


def stage_l1_attn(nc, g, d, y):
    with ExitStack() as ctx:
        def sb(n, shape, dt=fp32):
            return ctx.enter_context(nc.sbuf_tensor(f"l1a_{n}", shape, dt))
        w = sb("w", [P, 16, 325])
        wo = sb("wo", [65, 16, C])
        bias = sb("bias", [P, 1])
        cos, sin = sb("cos", [65, T]), sb("sin", [65, T])
        load(nc, "l1a", [(w[:], d["h_l1_w"]), (wo[:], d["h_l1_wo"]), (bias[:], d["h_l1_bo"]),
                         (cos[:], d["c_cos65"]), (sin[:], d["c_sin65"])])
        with nc.Block() as block:
            @block.vector
            def _(dve):
                nc.vector.tensor_copy(g.delta[:], bias[:, 0:1].to_broadcast([P, T]))
        attention(nc, g, "l1", 16, 64, g.xT, g.xT, w, wo, 64 ** -0.5, g.delta, rope=(cos, sin))
    layernorm(nc, g, "ln2", feature=g.delta)


def stage_l3_attn(nc, g, d, y):
    with ExitStack() as ctx:
        w = ctx.enter_context(nc.sbuf_tensor("l3a_w", [P, 1, 3 * P], fp32))
        load(nc, "l3a", [(w[:, 0, :], d["h_l3_w"])])
        attention(nc, g, "l3", 1, 128, g.xT, g.xT, w, None, 128 ** -0.5, g.delta, causal="upto")
    layernorm(nc, g, "ln6", feature=g.delta)




def constants():
    f = np.float32
    c = {}
    i = np.arange(P)
    c["ident"] = np.eye(P, dtype=f)
    c["ones"] = np.ones((P, P), f)
    c["e0"] = (i[:, None] == 0).astype(f)
    c["head_ones"] = (i[:, None] // 8 == i[None, :] // 8).astype(f)
    c["mask_strict_q"] = np.where(i[None, :] >= i[:, None], MASKED, 0).astype(f)
    c["mask_strict_k"] = np.ascontiguousarray(c["mask_strict_q"].T)
    c["mask_q"] = np.where(i[None, :] > i[:, None], MASKED, 0).astype(f)
    c["mask_k"] = np.ascontiguousarray(c["mask_q"].T)
    pick = np.zeros((P, 16, 9), f)
    for h in range(16):
        for j in range(8):
            pick[8 * h + j, h, 1 + j] = 1
    c["pick8"] = np.concatenate([pick, pick], axis=2)
    c["select16"] = np.repeat(np.eye(16, dtype=f)[:, :, None], P, axis=2)
    c["select8"] = np.repeat(np.eye(8, dtype=f)[:, :, None], P, axis=2)
    half = np.arange(32, dtype=f)
    theta = (f(1.0) / f(10000.0) ** (half / f(32))).astype(f)
    ang = (np.arange(T, dtype=f)[:, None] * theta[None, :]).astype(f)
    cos, sin = np.cos(ang).T.astype(f), np.sin(ang).T.astype(f)
    z = np.zeros((1, T), f)
    c["cos65"] = np.concatenate([z, cos, cos])
    c["sin65"] = np.concatenate([z, -sin, sin])
    even = np.arange(0, LD, 2, dtype=f)
    ang = np.arange(T, dtype=f)[:, None] * (f(1.0) / f(10000.0) ** (even / f(LD)))[None, :]
    cos, sin = np.cos(ang.astype(f)).astype(np.float64), np.sin(ang.astype(f)).astype(np.float64)
    base = (even.astype(np.float64) + 0.4 * LD) / (1.4 * LD)
    power = (np.arange(T) % P)[:, None] / (WIN // 2)
    up, down = base[None, :] ** power, base[None, :] ** -power
    tabs = np.stack([np.concatenate([cos * up, cos * up], 1), np.concatenate([-sin * up, sin * up], 1),
                     np.concatenate([cos * down, cos * down], 1), np.concatenate([-sin * down, sin * down], 1)], axis=1)
    c["rope"] = tabs.reshape(NT, P, 4, LD).transpose(1, 0, 2, 3).astype(f)
    c["halo_scale"] = np.tile(base ** (P / (WIN // 2)), 4)[:, None].astype(f)
    key = np.arange(SPAN)
    seen = (key[None, :] >= i[:, None]) & (key[None, :] <= i[:, None] + WIN)
    c["band"] = np.stack([np.where(seen, 0, MASKED), np.where(seen & (key[None, :] >= WIN), 0, MASKED)], axis=1).astype(f)
    return c


def layouts(a):
    h = {}
    def col(v):
        return np.ascontiguousarray(v.reshape(-1, 1))
    x = a["L0_attn_x"]
    h["xT"] = np.ascontiguousarray(x[0].T)
    h["l0_kT"] = np.ascontiguousarray(a["L0_attn_W_k"].T)
    h["l0_vT"] = np.ascontiguousarray(a["L0_attn_W_v"].T)
    for n, k in (("beta", "leaky_key_beta"), ("key_scale", "key_scale"), ("v_coef", "v_coef"), ("val_scale", "val_scale")):
        h["l0_" + n] = col(np.repeat(a["L0_attn_" + k].reshape(16), 8))
    wo = a["L0_attn_W_c"].T.reshape(16, 8, C).transpose(1, 0, 2)
    h["l0_wo"] = np.concatenate([np.zeros((1, 16, C), wo.dtype), wo])
    h["l0_bs"] = np.broadcast_to(a["L0_ffn_bs"], (P, NT, E_))
    h["l0_experts"] = np.concatenate([
        a["L0_ffn_W1"],
        a["L0_ffn_W2"].reshape(E_, FT, P, C).transpose(0, 2, 1, 3).reshape(E_, P, FT * C),
        a["L0_ffn_b1"].reshape(E_, FT, P).transpose(0, 2, 1),
        a["L0_ffn_b2"][:, :, None]], axis=2)
    swap = np.concatenate([np.arange(32, 64), np.arange(32)])
    def feature_tiles(v):
        return v.reshape(DT, P, -1).transpose(1, 0, 2)
    h["l2_w_in"] = a["L2_attn_W_in"]
    h["l2_w_out"] = feature_tiles(a["L2_attn_W_out"])
    h["l2_xproj"] = feature_tiles(a["L2_attn_W_xproj"])
    h["l2_w_dt"] = a["L2_attn_W_dt"]
    h["l2_a_log"] = feature_tiles(a["L2_attn_A_log"])
    h["l2_cols"] = np.concatenate([feature_tiles(a["L2_attn_W_conv"]), feature_tiles(a["L2_attn_b_conv"]),
                                   feature_tiles(a["L2_attn_b_dt"]), feature_tiles(a["L2_attn_D"])], axis=2)
    for n in "rkv":
        h[f"l2f_{n}T"] = a["L2_ffn_W_" + n].T
    h["l2f_mu"] = np.stack([a["L2_ffn_mu_r"], a["L2_ffn_mu_k"]], axis=1)
    h["lw_wo"] = a["L1_ffn_Wo"].reshape(DEPTH, INNER // P, P, C).transpose(0, 2, 1, 3)
    w2 = a["L1_ffn_W2"]
    w2 = np.concatenate([w2, np.zeros((DEPTH, len(FCH) * P - FI, C), w2.dtype)], axis=1)
    h["lw_w2"] = w2.reshape(DEPTH, len(FCH), P, C).transpose(0, 2, 1, 3)
    qs, ks = a["L1_ffn_q_scale"], a["L1_ffn_k_scale"]
    s4 = np.stack([qs, qs[:, swap], ks, ks[:, swap]], axis=1)
    h["lw_scales"] = np.broadcast_to(s4[:, None], (DEPTH, P, 4, LD))
    b1 = a["L1_ffn_b1"]
    pad = np.zeros((DEPTH, len(FCH) * P - FI), b1.dtype)
    b1 = np.concatenate([b1[:, :FI], pad, b1[:, FI:], pad], axis=1).reshape(DEPTH, 2 * len(FCH), P).transpose(0, 2, 1)
    h["lw_cols"] = np.concatenate([a["L1_ffn_ln_g"][:, :, None], a["L1_ffn_ln_b"][:, :, None],
                                   a["L1_ffn_b2"][:, :, None], b1], axis=2)
    rows = []
    for n in ("w_gate", "w_up"):
        v = a["L3_ffn_" + n]
        v = np.concatenate([v, np.zeros((HT * P - HI, C), v.dtype)])
        rows.append(v.reshape(HT, P, C).transpose(1, 0, 2).reshape(P, HT * C))
    h["l3f_w"] = np.concatenate(rows + [a["L3_ffn_w_down"]], axis=1)
    w = a["L1_attn_w_qkv"].reshape(C, 3, 16, 64)
    z = np.zeros((C, 16, 1), w.dtype)
    q, k, v = w[:, 0], w[:, 1], w[:, 2]
    h["l1_w"] = np.concatenate([z, q, z, q[:, :, swap], z, k, z, k[:, :, swap], z, v], axis=2)
    wo = a["L1_attn_w_out"].reshape(16, 64, C).transpose(1, 0, 2)
    h["l1_wo"] = np.concatenate([np.zeros((1, 16, C), wo.dtype), wo])
    h["l1_bo"] = col(a["L1_attn_b_out"])
    h["l3_w"] = np.concatenate([a["L3_attn_W_Q"], a["L3_attn_W_K"], a["L3_attn_W_V"]], axis=1)
    return h




def kernel(**inputs):
    import concourse.bacc as bacc
    from concourse.bass_utils import run_bass_kernel_spmd

    a = {n: np.asarray(v) for n, v in inputs.items()}
    arrays = {"h_" + n: v for n, v in layouts(a).items()}
    arrays |= {"c_" + n: v for n, v in constants().items()}
    arrays |= {n: a[n] for n in ("L0_attn_x", "L0_ffn_Ws", "L1_ffn_Wqkv", "L1_ffn_W1")}
    arrays = {n: np.ascontiguousarray(v) for n, v in arrays.items()}
    nc = bacc.Bacc("TRN2", target_bir_lowering=False, num_devices=1)
    d = {n: nc.dram_tensor(n, v.shape, mybir.dt.from_np(v.dtype), kind="ExternalInput").ap() for n, v in arrays.items()}
    y = nc.dram_tensor("y", (T, C), fp32, kind="ExternalOutput").ap()
    build(nc, d, y)
    got = run_bass_kernel_spmd(nc, [arrays], core_ids=[0])
    return got.results[0]["y"].reshape(1, T, C)
```

```python
import numpy as np
import concourse.bass as bass
from concourse import mybir
from contextlib import ExitStack, contextmanager

fp32 = mybir.dt.float32
bf16 = mybir.dt.bfloat16
ALU = mybir.AluOpType
ACT = mybir.ActivationFunctionType
AX = mybir.AxisListType

T = 2048
C = 128
P = 128
NT = T // P
QB = 512
NB = T // QB
LN_EPS = 1e-5
MASKED = -1e30


class Lane:

    def __init__(self, eng, own, base=None):
        self.eng, self.own = eng, own
        self.seen, self.base = {}, dict(base or {})

    def wait(self, sem, by=1):
        self.seen[sem] = self.seen.get(sem, 0) + by
        self.eng.wait_ge(sem, self.base.get(sem, 0) + self.seen[sem])

    def skip(self, sem, by):
        self.seen[sem] = self.seen.get(sem, 0) + by

    def ahead(self, sem, by):
        self.eng.wait_ge(sem, self.base.get(sem, 0) + self.seen.get(sem, 0) + by)

    def post(self, ins):
        ins.then_inc(self.own, 1)
        self.seen[self.own] = self.seen.get(self.own, 0) + 1

    def settle(self):
        self.eng.wait_ge(self.own, self.base.get(self.own, 0) + self.seen[self.own])

    def seq(self, ins):
        self.post(ins)
        self.settle()

    @contextmanager
    def loop(self, count, per):
        before, outer = dict(self.seen), dict(self.base)
        with self.eng.Fori(0, count) as i:
            for sem, by in per.items():
                self.base[sem] = outer.get(sem, 0) + i * by
            yield i
            added = {s: n - before.get(s, 0) for s, n in self.seen.items() if n != before.get(s, 0)}
            assert added == {s: per.get(s, 0) for s in added}, \
                ("per pass", {s.name: n for s, n in added.items()}, {s.name: n for s, n in per.items()})
        self.base = outer
        self.seen = {s: before.get(s, 0) + count * per.get(s, 0) for s in self.seen}


class Ring:

    def __init__(self, nc, ctx, banks, name):
        self.buf = ctx.enter_context(nc.psum_tensor(f"{name}_bank", [P, banks, QB], fp32))
        self.filled = nc.alloc_semaphore(f"{name}_filled")
        self.freed = nc.alloc_semaphore(f"{name}_freed")
        self.banks = banks

    def writer(self, lane):
        return RingEnd(self, lane, self.freed)

    def reader(self, lane):
        lane.eng.sem_inc(self.freed, self.banks)
        lane.seen[self.freed] = self.banks
        return RingEnd(self, lane, self.filled)


class RingEnd:
    def __init__(self, ring, lane, sem):
        self.ring, self.lane, self.sem, self.turn = ring, lane, sem, 0

    def take(self):
        self.lane.wait(self.sem)
        bank = self.ring.buf[:, self.turn % self.ring.banks, :]
        self.turn += 1
        return bank

    def filled(self, ins):
        ins.then_inc(self.ring.filled, 1)

    def free(self, ins):
        ins.then_inc(self.ring.freed, 1)
        self.lane.seen[self.ring.freed] += 1

    def settle(self):
        self.lane.eng.wait_ge(self.ring.freed, self.lane.base.get(self.ring.freed, 0) + self.lane.seen[self.ring.freed])


def layernorm(nc, g, name, feature=None, token=None, out_dram=None):
    with ExitStack() as ctx:
        def sb(n, shape, dt=fp32):
            return ctx.enter_context(nc.sbuf_tensor(f"{name}_{n}", shape, dt))

        def sem(n):
            return nc.alloc_semaphore(f"{name}_{n}")

        z = sb("z", [P, NT, C])
        stats = sb("stats", [P, NT, 6])
        meanvar = sb("meanvar", [P, NT, 2])
        std = sb("std", [P, NT])
        rstd = sb("rstd", [P, NT])
        eps = sb("eps", [P, 1])
        up = ctx.enter_context(nc.psum_tensor(f"{name}_up", [P, NT, C], fp32))
        down = ctx.enter_context(nc.psum_tensor(f"{name}_down", [P, NT, C], fp32))
        turned = sem("turned")
        z_ready = sem("z_ready")
        std_ready = sem("std_ready")
        x_ready = sem("x_ready")
        back = sem("back")
        xT_ready = sem("xT_ready")
        stored = sem("stored")
        own = sem("dve_steps")
        G = 4
        block = ctx.enter_context(nc.Block())

        @block.tensor
        def _(pe):
            if feature is not None:
                for t in range(NT):
                    last = nc.tensor.transpose(up[:, t, :], feature[:, t * P:(t + 1) * P], g.ident[:])
                    if t % G == G - 1:
                        last.then_inc(turned, 1)
            if out_dram is None:
                for k in range(NT // G):
                    pe.wait_ge(x_ready, k + 1)
                    for t in range(k * G, (k + 1) * G):
                        last = nc.tensor.transpose(down[:, t, :], g.x[:, t, :], g.ident[:])
                    last.then_inc(back, 1)

        @block.vector
        def _(dve):
            lane = Lane(dve, own)
            lane.seq(nc.vector.memset(eps[:], LN_EPS))
            for k in range(NT // G):
                s = slice(k * G, (k + 1) * G)
                if feature is not None:
                    dve.wait_ge(turned, k + 1)
                delta = up[:, s, :] if feature is not None else token[:, s, :]
                lane.seq(nc.vector.tensor_tensor(z[:, s, :], delta, g.x[:, s, :], ALU.add))
                for t in range(k * G, (k + 1) * G):
                    lane.post(nc.vector.bn_stats(stats[:, t, :], z[:, t, :]))
                lane.settle()
                for t in range(k * G, (k + 1) * G):
                    last = nc.vector.bn_aggr(meanvar[:, t, :], stats[:, t, :])
                last.then_inc(z_ready, 1)
            for k in range(NT // G):
                s = slice(k * G, (k + 1) * G)
                dve.wait_ge(std_ready, k + 1)
                lane.seq(nc.vector.reciprocal(rstd[:, s], std[:, s]))
                for t in range(k * G, (k + 1) * G):
                    last = nc.vector.tensor_scalar(g.x[:, t, :], z[:, t, :], meanvar[:, t, 0:1],
                                                   rstd[:, t:t + 1], ALU.subtract, ALU.mult)
                last.then_inc(x_ready, 1)

        @block.scalar
        def _(act):
            for k in range(NT // G):
                s = slice(k * G, (k + 1) * G)
                act.wait_ge(z_ready, k + 1)
                nc.scalar.activation(std[:, s], meanvar[:, s, 1], ACT.Sqrt, bias=eps[:]).then_inc(std_ready, 1)
            if out_dram is None:
                for k in range(NT // G):
                    act.wait_ge(back, k + 1)
                    nc.scalar.copy(g.xT[:, k * QB:(k + 1) * QB], down[:, k * G:(k + 1) * G, :]).then_inc(xT_ready, 1)

        @block.sync
        def _(sp):
            if out_dram is not None:
                for k in range(NT // G):
                    sp.wait_ge(x_ready, k + 1)
                    sp.dma_start(out_dram[k * QB:(k + 1) * QB, :].rearrange("(t p) c -> p t c", p=P),
                                 g.x[:, k * G:(k + 1) * G, :]).then_inc(stored, 16)
                sp.wait_ge(stored, 16 * (NT // G))


def attention(nc, g, name, heads, D, k_src, v_src, w_all, wo_all, scale, yT,
              causal=None, rope=None, separate_q=True, bias=None):
    one = D < P
    R = D + 1 if one else D
    DV = R
    pieces = (["q", "qr"] if rope else ["q"]) if separate_q else []
    pieces += ["k", "kr"] if rope else ["k"]
    NW = len(pieces) * R + DV
    with ExitStack() as ctx:
        def sb(n, shape, dt=fp32):
            return ctx.enter_context(nc.sbuf_tensor(f"{name}_{n}", shape, dt))

        def sem(n):
            return nc.alloc_semaphore(f"{name}_{n}")

        wh = sb("w_head", [P, NW])
        woh = sb("wo_head", [R, C])
        qT = sb("qT", [R, T])
        kT = sb("kT", [R, T])
        v = sb("v", [P, NT, DV])
        probs = sb("probs", [P, 4, QB])
        rotated = sb("rotated", [R, QB])
        chunk_max = sb("chunk_max", [P, 4, NB])
        row_max = sb("row_max", [P, 4])
        rsum = sb("rsum", [1, QB])
        rsum_all = sb("rsum_all", [R, QB])
        oT = sb("oT", [R, QB])
        negmax = sb("negmax", [1, T]) if not one else qT
        ring = Ring(nc, ctx, 4, name)
        scoresT = ctx.enter_context(nc.psum_tensor(f"{name}_scoresT", [P, 2, QB], fp32))
        out = ctx.enter_context(nc.psum_tensor(f"{name}_out", [P, 2, QB], fp32))

        w_ready = sem("w_ready")
        prepared = sem("prepared")
        w_used = sem("w_used")
        max_ready = sem("max_ready")
        negmax_ready = sem("negmax_ready")
        scores_ready = sem("scores_ready")
        probs_ready = sem("probs_ready")
        out_ready = sem("out_ready")
        rsum_ready = sem("rsum_ready")
        oT_ready = sem("oT_ready")
        projected = sem("projected")
        own = sem("dve_steps")
        pool_own = sem("pool_steps")
        block = ctx.enter_context(nc.Block())

        def chunks(b, qt):
            if causal is None:
                return [(c * QB, QB) for c in range(NB)]
            return [(c * QB, QB) for c in range(b)] + [(b * QB, P * (qt + 1))]

        def key_tiles(b):
            if causal is None:
                return [(k, 0) for k in range(NT)]
            return [(k, max(0, (k - 4 * b) * P)) for k in range(4 * (b + 1))]

        n_keys = sum(len(key_tiles(b)) for b in range(NB))
        n_chunks = sum(len(chunks(b, q)) for b in range(NB) for q in range(4))
        n_ring = NB * (len(pieces) + 1) + n_chunks + NB + NB + (NB if one else 0)
        assert n_ring % 4 == 0 or heads == 1
        wcols = {p: wh[:, i * R:(i + 1) * R] for i, p in enumerate(pieces)}
        wv = wh[:, len(pieces) * R:NW]
        diag_q, diag_k = (g.mask_strict_q, g.mask_strict_k) if causal == "strict" else (g.mask_q, g.mask_k)

        def maybe_loop(lane, per):
            return lane.loop(heads, per) if heads > 1 else once()

        @block.gpsimd
        def _(pool):
            lane = Lane(pool, pool_own)
            with maybe_loop(lane, {w_used: 1, projected: 1, pool_own: 1 if one else 0}) as h:
                lane.wait(w_used)
                copied = nc.gpsimd.tensor_copy(wh[:], w_all[:, h, :])
                if one:
                    lane.post(copied)
                    lane.wait(projected)
                    copied = nc.gpsimd.tensor_copy(woh[:], wo_all[:, h, :])
                    lane.settle()
                else:
                    lane.wait(projected)
                copied.then_inc(w_ready, 1)

        @block.tensor
        def _(pe):
            lane = Lane(pe, None)
            to_dve = ring.writer(lane)
            with maybe_loop(lane, {ring.freed: n_ring, w_ready: 1, prepared: 1, max_ready: NB,
                                   negmax_ready: NB, probs_ready: n_keys,
                                   rsum_ready: NB, oT_ready: NB if one else 0}) as h:
                lane.wait(w_ready)
                for b in range(NB):
                    for p in pieces:
                        bank = to_dve.take()
                        to_dve.filled(nc.tensor.matmul(bank[0:R, :], wcols[p], k_src[:, b * QB:(b + 1) * QB],
                                                       start=True, stop=True))
                    bank = to_dve.take()
                    for t in range(4):
                        tok = (4 * b + t) * P
                        last = nc.tensor.matmul(bank[:, t * DV:(t + 1) * DV] if 4 * DV <= QB else None,
                                                v_src[:, tok:tok + P], wv, start=True, stop=True)
                    to_dve.filled(last)
                lane.wait(prepared)

                def find_max(b):
                    for qt in range(4):
                        q0 = b * QB + qt * P
                        row0 = 1 if one else 0
                        for first, n in chunks(b, qt):
                            bank = to_dve.take()
                            diag = causal is not None and first == b * QB
                            last = nc.tensor.matmul(bank[:, 0:n], qT[:, q0:q0 + P], kT[:, first:first + n],
                                                    start=True, stop=not diag)
                            if diag:
                                last = nc.tensor.matmul(bank[:, n - P:n], g.ident[:], diag_q[:],
                                                        start=False, stop=True)
                            to_dve.filled(last)
                    lane.wait(max_ready)
                    bank = to_dve.take()
                    for qt in range(4):
                        last = nc.tensor.matmul(bank[0:1, qt * P:(qt + 1) * P], row_max[:, qt:qt + 1], g.ident[:],
                                                start=True, stop=True)
                    to_dve.filled(last)

                def weigh(b):
                    lane.wait(negmax_ready)
                    tiles = key_tiles(b)
                    acc = out[:, b % 2, :]

                    def values(j):
                        k, off = tiles[j]
                        lane.wait(probs_ready)
                        last = nc.tensor.matmul(acc[0:R, off:QB], v[:, k, :], probs[:, j % 4, off:QB],
                                                start=j == 0, stop=j == len(tiles) - 1)
                        if not one:
                            last = nc.tensor.matmul(sums[0:1, off:QB], g.ones[:, 0:1], probs[:, j % 4, off:QB],
                                                    start=j == 0, stop=j == len(tiles) - 1)
                        return last

                    sums = out[:, 1 - b % 2, :]
                    for j, (k, off) in enumerate(tiles):
                        bank = scoresT[:, j % 2, off:QB]
                        diag = causal is not None and k >= 4 * b
                        last = nc.tensor.matmul(bank, kT[:, k * P:(k + 1) * P], qT[:, b * QB + off:(b + 1) * QB],
                                                start=True, stop=one and not diag)
                        if not one:
                            last = nc.tensor.matmul(bank, g.ones[0:1, :], negmax[0:1, b * QB + off:(b + 1) * QB],
                                                    start=False, stop=not diag)
                        if diag:
                            last = nc.tensor.matmul(scoresT[:, j % 2, off:off + P], g.ident[:], diag_k[:],
                                                    start=False, stop=True)
                        last.then_inc(scores_ready, 1)
                        if j > 0:
                            values(j - 1)
                    values(len(tiles) - 1).then_inc(out_ready, 1)
                    lane.wait(rsum_ready)
                    bank = to_dve.take()
                    to_dve.filled(nc.tensor.matmul(bank[:, :], g.ones[0:1, :], rsum[:], start=True, stop=True))
                    if one:
                        lane.wait(oT_ready)
                        bank = to_dve.take()
                        to_dve.filled(nc.tensor.matmul(bank[:, :], woh[:], oT[:], start=True, stop=True))

                find_max(0)
                for b in range(NB):
                    if b + 1 < NB and one:
                        find_max(b + 1)
                    weigh(b)
                    if b + 1 < NB and not one:
                        find_max(b + 1)

        @block.scalar
        def _(act):
            lane = Lane(act, None)
            with maybe_loop(lane, {scores_ready: n_keys}) as h:
                for b in range(NB):
                    for j, (k, off) in enumerate(key_tiles(b)):
                        lane.wait(scores_ready)
                        nc.scalar.activation(probs[:, j % 4, off:QB], scoresT[:, j % 2, off:QB], ACT.Exp,
                                             scale=scale).then_inc(probs_ready, 1)

        @block.vector
        def _(dve):
            lane = Lane(dve, own)
            from_pe = ring.reader(lane)
            dve.sem_inc(projected, 1)
            dve.sem_inc(w_used, 1)
            per = {ring.filled: n_ring, ring.freed: n_ring, out_ready: NB, w_ready: 0,
                   own: PER_OWN[name]}
            if one:
                lane.seq(nc.vector.memset(v[:, :, 0:1], 1.0))
            with maybe_loop(lane, per) as h:
                for b in range(NB):
                    s = slice(b * QB, (b + 1) * QB)
                    for dst, names in ((qT, ["q", "qr"]), (kT, ["k", "kr"])):
                        if names[0] not in pieces:
                            continue
                        bank = from_pe.take()
                        if not rope:
                            if dst is kT and one:
                                if not separate_q:
                                    lane.post(nc.vector.tensor_copy(qT[:, s], bank[0:R, :]))
                                from_pe.free(nc.vector.tensor_scalar(kT[:, s], bank[0:R, :], g.e0[0:R, :], None, ALU.add))
                            else:
                                from_pe.free(nc.vector.tensor_copy(dst[:, s], bank[0:R, :]))
                            continue
                        cos, sin = rope
                        from_pe.free(nc.vector.tensor_tensor(dst[:, s], bank[0:R, :], cos[:, s], ALU.mult))
                        bank = from_pe.take()
                        from_pe.free(nc.vector.tensor_tensor(rotated[:], bank[0:R, :], sin[:, s], ALU.mult))
                        from_pe.settle()
                        if dst is kT:
                            lane.seq(nc.vector.scalar_tensor_tensor(kT[:, s], rotated[:], g.e0[0:R, :], kT[:, s],
                                                                    ALU.add, ALU.add))
                        else:
                            lane.seq(nc.vector.tensor_tensor(qT[:, s], rotated[:], qT[:, s], ALU.add))
                    bank = from_pe.take()
                    row0 = 1 if one else 0
                    src = bank[:, 0:4 * DV].rearrange("p (t d) -> p t d", t=4)
                    from_pe.free(nc.vector.tensor_copy(v[:, 4 * b:4 * b + 4, row0:DV], src[:, :, row0:DV]))
                from_pe.settle()
                dve.sem_inc(prepared, 1)
                dve.sem_inc(w_used, 1)

                def find_max(b):
                    for qt in range(4):
                        for c, (first, n) in enumerate(chunks(b, qt)):
                            bank = from_pe.take()
                            from_pe.free(nc.vector.reduce_max(chunk_max[:, qt, c:c + 1], bank[:, 0:n], axis=AX.X))
                    from_pe.settle()
                    n = len(chunks(b, 0))
                    nc.vector.reduce_max(row_max[:], chunk_max[:, :, 0:n], axis=AX.X).then_inc(max_ready, 1)
                    bank = from_pe.take()
                    from_pe.free(nc.vector.tensor_scalar(negmax[0:1, b * QB:(b + 1) * QB], bank[0:1, :], -1.0, None, ALU.mult))
                    from_pe.settle()
                    dve.sem_inc(negmax_ready, 1)

                def finish(b):
                    acc = out[:, b % 2, :]
                    sums = acc[0:1, :] if one else out[0:1, 1 - b % 2, :]
                    lane.wait(out_ready)
                    nc.vector.reciprocal(rsum[:], sums).then_inc(rsum_ready, 1)
                    bank = from_pe.take()
                    from_pe.free(nc.vector.tensor_copy(rsum_all[:], bank[0:R, :]))
                    from_pe.settle()
                    s = slice(b * QB, (b + 1) * QB)
                    if not one:
                        lane.post(nc.vector.tensor_tensor(yT[:, s], acc[0:R, :], rsum_all[:], ALU.mult))
                        return
                    ins = nc.vector.tensor_tensor(oT[:], acc[0:R, :], rsum_all[:], ALU.mult)
                    if causal == "strict" and b == 0:
                        lane.seq(ins)
                        ins = nc.vector.memset(oT[:, 0:1], 0.0)
                    ins.then_inc(oT_ready, 1)
                    bank = from_pe.take()
                    from_pe.free(nc.vector.tensor_tensor(yT[:, s], bank[:, :], yT[:, s], ALU.add))

                find_max(0)
                for b in range(NB):
                    if b + 1 < NB and one:
                        find_max(b + 1)
                    finish(b)
                    if b + 1 < NB and not one:
                        find_max(b + 1)
                from_pe.settle()
                dve.sem_inc(projected, 1)


@contextmanager
def once():
    yield 0


def decayed_keys(nc, g, w, kT_out, vT_out):
    with ExitStack() as ctx:
        def sb(n, shape, dt=fp32):
            return ctx.enter_context(nc.sbuf_tensor(f"dk_{n}", shape, dt))

        def sem(n):
            return nc.alloc_semaphore(f"dk_{n}")

        square = sb("square", [P, T])
        norm = sb("norm", [P, T])
        col = sb("col", [P, 8])
        acc = [ctx.enter_context(nc.psum_tensor(f"dk_acc{i}", [P, NB, QB], fp32)) for i in range(2)]
        projected = sem("projected")
        squared = sem("squared")
        summed = sem("summed")
        normed = sem("normed")
        cols_ready = sem("cols_ready")
        raw_ready = sem("raw_ready")
        clipped = sem("clipped")
        done = sem("done")
        own = sem("dve_steps")
        act_own = sem("act_steps")
        block = ctx.enter_context(nc.Block())
        outs = (kT_out, vT_out)

        @block.tensor
        def _(pe):
            for i, wt in enumerate((w["kT"], w["vT"])):
                for b in range(NB):
                    last = nc.tensor.matmul(acc[i][:, b, :], wt[:], g.xT[:, b * QB:(b + 1) * QB], start=True, stop=True)
                last.then_inc(projected, 1)
            for i in range(2):
                pe.wait_ge(squared, i + 1)
                for b in range(NB):
                    last = nc.tensor.matmul(acc[i][:, b, :], g.head_ones[:], square[:, b * QB:(b + 1) * QB],
                                            start=True, stop=True)
                last.then_inc(summed, 1)

        @block.scalar
        def _(act):
            nc.scalar.activation(col[:, 0:1], w["beta"], ACT.Abs).then_inc(act_own, 1)
            act.wait_ge(act_own, 1)
            nc.scalar.activation(col[:, 1:2], col[:, 0:1], ACT.Exp, scale=-10.0)
            nc.scalar.activation(col[:, 3:4], w["val_scale"], ACT.Exp, scale=10.0)
            act.wait_ge(clipped, 1)
            nc.scalar.activation(col[:, 2:3], col[:, 5:6], ACT.Exp).then_inc(cols_ready, 1)
            for i in range(2):
                act.wait_ge(raw_ready, i + 1)
                if i:
                    act.wait_ge(summed, i)
                nc.scalar.activation(square[:], outs[i][:], ACT.Square).then_inc(squared, 1)
                act.wait_ge(summed, i + 1)
                if i:
                    act.wait_ge(done, 1)
                nc.scalar.activation(norm[:], acc[i][:, :, :].rearrange("p b q -> p (b q)"), ACT.Sqrt).then_inc(normed, 1)

        @block.vector
        def _(dve):
            lane = Lane(dve, own)
            nc.vector.tensor_scalar(col[:, 5:6], w["key_scale"], 10.0, KEY_SCALE_MAX, ALU.mult, ALU.min).then_inc(clipped, 1)
            lane.post(nc.vector.tensor_scalar(col[:, 4:5], w["v_coef"], -1.0, 1.0, ALU.mult, ALU.add))
            dve.wait_ge(cols_ready, 1)
            dve.wait_ge(projected, 1)
            k_raw = acc[0][:, :, :].rearrange("p b q -> p (b q)")
            v_raw = acc[1][:, :, :].rearrange("p b q -> p (b q)")
            nc.vector.tensor_tensor_scan(kT_out[:], col[:, 1:2].to_broadcast([P, T]), k_raw, 0.0,
                                         ALU.mult, ALU.add).then_inc(raw_ready, 1)
            dve.wait_ge(projected, 2)
            lane.seq(nc.vector.tensor_scalar(vT_out[:], v_raw, w["v_coef"], None, ALU.mult))
            nc.vector.scalar_tensor_tensor(vT_out[:, 0:T - 1], v_raw[:, 1:T], col[:, 4:5], vT_out[:, 0:T - 1],
                                           ALU.mult, ALU.add).then_inc(raw_ready, 1)
            dve.wait_ge(raw_ready, 2)
            for i, factor in enumerate((col[:, 2:3], col[:, 3:4])):
                dve.wait_ge(normed, i + 1)
                lane.seq(nc.vector.tensor_scalar(norm[:], norm[:], 1e-10, None, ALU.add))
                lane.seq(nc.vector.reciprocal(norm[:], norm[:]))
                nc.vector.scalar_tensor_tensor(outs[i][:], outs[i][:], factor, norm[:],
                                               ALU.mult, ALU.mult).then_inc(done, 1)


def split_keys(nc, g, name, keys, values, hi, mid, lo, v_all):
    with ExitStack() as ctx:
        rest = ctx.enter_context(nc.sbuf_tensor(f"{name}_rest", [P, T], fp32))
        turned = ctx.enter_context(nc.psum_tensor(f"{name}_turned", [P, NT, P], fp32))
        hi_ready = nc.alloc_semaphore(f"{name}_hi_ready")
        rest_ready = nc.alloc_semaphore(f"{name}_rest_ready")
        mid_ready = nc.alloc_semaphore(f"{name}_mid_ready")
        v_turned = nc.alloc_semaphore(f"{name}_v_turned")
        block = ctx.enter_context(nc.Block())

        @block.scalar
        def _(act):
            nc.scalar.copy(hi[:], keys[:]).then_inc(hi_ready, 1)
            act.wait_ge(v_turned, 1)
            nc.scalar.copy(v_all[:], turned[:])
            act.wait_ge(rest_ready, 1)
            nc.scalar.copy(mid[:], rest[:]).then_inc(mid_ready, 1)

        @block.tensor
        def _(pe):
            for t in range(NT):
                last = nc.tensor.transpose(turned[:, t, :], values[:, t * P:(t + 1) * P], g.ident[:])
            last.then_inc(v_turned, 1)

        @block.vector
        def _(dve):
            dve.wait_ge(hi_ready, 1)
            nc.vector.tensor_tensor(rest[:], keys[:], hi[:], ALU.subtract).then_inc(rest_ready, 1)
            dve.wait_ge(rest_ready, 1)
            dve.wait_ge(mid_ready, 1)
            nc.vector.tensor_tensor(lo[:], rest[:], mid[:], ALU.subtract)


def head_attention(nc, g, name, heads, D, scale, yT, wo_all, rotary=None, picked=None):
    causal = picked is not None
    S0 = 32 if causal else 64
    M = S0 + D
    with ExitStack() as ctx:
        def sb(n, shape, dt=fp32):
            return ctx.enter_context(nc.sbuf_tensor(f"{name}_{n}", shape, dt))

        def sem(n):
            return nc.alloc_semaphore(f"{name}_{n}")

        woh = sb("wo_head", [P, C])
        v = sb("v", [P, NT, M])
        probs = sb("probs", [P, 4, QB])
        chunk_max = sb("chunk_max", [P, 4, NB])
        row_max = sb("row_max", [P, 4])
        rsum = sb("rsum", [D, QB])
        oT = sb("oT", [P, QB])
        if causal:
            hi, mid, lo, v_all, groups, head_mask = picked
            sel = sb("sel", [P, 6, P], bf16)
            qs = sb("qs", [P, T], bf16)
            ks = sb("ks", [P, T], bf16)
            neg_rest = sb("neg_rest", [P, 4])
            neg_parts = sb("neg_parts", [P, 3, 4], bf16)
            ident = sb("ident_bf", [P, P], bf16)
            mask_q, mask_k = sb("mask_q_bf", [P, P], bf16), sb("mask_k_bf", [P, P], bf16)
        else:
            w_all, cos, sin = rotary
            wh = sb("w_head", [P, 4, 2, D])
            wv = sb("wv_head", [P, D])
            qT = sb("qT", [P, T])
            kT = sb("kT", [P, T])
            k_twice = sb("k_twice", [P, T])
            rotated = sb("rotated", [P, QB])
            q_hm = sb("q_hm", [P, T], bf16)
            k_hh = sb("k_hh", [P, T], bf16)
            k_mm = sb("k_mm", [P, T], bf16)
            k_keep = sb("k_keep", [P, 2])
        ring = Ring(nc, ctx, 4, name)
        scoresT = ctx.enter_context(nc.psum_tensor(f"{name}_scoresT", [P, 2, QB], fp32))
        out = ctx.enter_context(nc.psum_tensor(f"{name}_out", [P, 2, QB], fp32))

        w_ready = sem("w_ready")
        wo_ready = sem("wo_ready")
        w_used = sem("w_used")
        sum_ready = sem("sum_ready")
        hi_ready = sem("hi_ready")
        prepared = sem("prepared")
        v_ready = sem("v_ready")
        max_ready = sem("max_ready")
        negmax_ready = sem("negmax_ready")
        scores_ready = sem("scores_ready")
        probs_ready = sem("probs_ready")
        out_ready = sem("out_ready")
        oT_ready = sem("oT_ready")
        projected = sem("projected")
        own = sem("dve_steps")
        pool_own = sem("pool_steps")

        with nc.Block() as block:
            @block.gpsimd
            def _(pool):
                nc.gpsimd.memset(woh[:], 0.0)
                nc.gpsimd.memset(v[:, :, 0:S0], 0.0)
                nc.gpsimd.memset(v[:, :, S0:M], 1.0)

            @block.vector
            def _(dve):
                nc.vector.memset(oT[:], 0.0)
                if causal:
                    nc.vector.tensor_copy(ident[:], g.ident[:])
                    nc.vector.tensor_copy(mask_q[:], g.mask_strict_q[:])
                    nc.vector.tensor_copy(mask_k[:], g.mask_strict_k[:])
                else:
                    nc.vector.memset(k_keep[:], 0.0).then_inc(sum_ready, 1)
                    dve.wait_ge(sum_ready, 1)
                    nc.vector.memset(k_keep[0:64, 0:1], 1.0)
                    nc.vector.memset(k_keep[64:65, 1:2], 1.0)
        begun = 0 if causal else 1

        block = ctx.enter_context(nc.Block())

        def chunks(b, qt):
            if not causal:
                return [(c * QB, QB) for c in range(NB)]
            return [(c * QB, QB) for c in range(b)] + [(b * QB, P * (qt + 1))]

        def key_tiles(b):
            if not causal:
                return [(k, 0) for k in range(NT)]
            return [(k, max(0, (k - 4 * b) * P)) for k in range(4 * (b + 1))]

        def maxima(b):
            return [(qt, c, first, n) for qt in range(4) for c, (first, n) in enumerate(chunks(b, qt))]

        def aside(b):
            n = len(key_tiles(b))
            plan = [[] for _ in range(n)]
            if b + 1 < NB:
                todo = maxima(b + 1)
                over = max(1, n - 2)
                for i, item in enumerate(todo):
                    plan[i * over // len(todo)].append(("max",) + item)
            if b > 0:
                plan[min(5, n - 1)].append(("project",))
            return plan

        n_keys = sum(len(key_tiles(b)) for b in range(NB))
        n_prep = NB * 2 if causal else NB * 5
        n_ring = n_prep + sum(len(maxima(b)) for b in range(NB)) + NB + NB

        @block.gpsimd
        def _(pool):
            lane = Lane(pool, pool_own)
            per = {w_used: 1, projected: 1, pool_own: 1}
            if not causal:
                per |= {hi_ready: 2 * NB, prepared: 2 * NB}
            with lane.loop(heads, per) as h:
                lane.wait(w_used)
                if causal:
                    copied = nc.gpsimd.tensor_tensor(sel[:], groups[:],
                                                     head_mask[:, h, :].unsqueeze(2).to_broadcast([P, 6, P]), ALU.mult)
                    copied.then_inc(w_ready, 1)
                else:
                    qk = w_all[:, h, 0:4 * D].rearrange("p (i d) -> p i d", i=4)
                    nc.gpsimd.tensor_copy(wh[:, :, 0, :], qk).then_inc(w_ready, 1)
                    nc.gpsimd.tensor_copy(wh[:, :, 1, :], qk).then_inc(w_ready, 1)
                    nc.gpsimd.tensor_copy(wv[:], w_all[:, h, 4 * D:5 * D]).then_inc(w_ready, 1)
                    for b in range(NB):
                        s = slice(b * QB, (b + 1) * QB)
                        lane.wait(hi_ready)
                        nc.gpsimd.tensor_tensor(q_hm[64:P, s], qT[64:P, s], q_hm[64:P, s], ALU.subtract).then_inc(prepared, 1)
                        lane.wait(prepared)
                        lane.wait(hi_ready)
                        nc.gpsimd.tensor_tensor(k_mm[:, s], k_twice[:, s], k_hh[:, s], ALU.subtract).then_inc(prepared, 1)
                        lane.wait(prepared)
                lane.wait(projected)
                lane.post(nc.gpsimd.tensor_copy(woh[0:D, :], wo_all[:, h, :]))
                lane.settle()
                pool.sem_inc(wo_ready, 1)

        @block.tensor
        def _(pe):
            lane = Lane(pe, None)
            to_dve = ring.writer(lane)

            def project():
                lane.wait(oT_ready)
                bank = to_dve.take()
                to_dve.filled(nc.tensor.matmul(bank[:, :], woh[:], oT[:], start=True, stop=True))

            def find_max(b, qt, c, first, n):
                q0 = b * QB + qt * P
                bank = to_dve.take()
                if causal:
                    diag = first == b * QB
                    last = nc.tensor.matmul(bank[:, 0:n], qs[:, q0:q0 + P], ks[:, first:first + n], start=True, stop=not diag)
                    if diag:
                        last = nc.tensor.matmul(bank[:, n - P:n], ident[:], mask_q[:], start=False, stop=True)
                else:
                    nc.tensor.matmul(bank[:, 0:n], q_hm[:, q0:q0 + P], k_hh[:, first:first + n], start=True, stop=False)
                    last = nc.tensor.matmul(bank[:, 0:n], q_hm[:, q0:q0 + P], k_mm[:, first:first + n], start=False, stop=True)
                to_dve.filled(last)

            def turn_max():
                lane.wait(max_ready)
                bank = to_dve.take()
                for qt in range(4):
                    cols = slice(qt * P, (qt + 1) * P)
                    if causal:
                        last = nc.tensor.matmul(bank[0:3, cols], neg_parts[:, :, qt], ident[:], start=True, stop=True)
                    else:
                        last = nc.tensor.matmul(bank[0:1, cols], row_max[:, qt:qt + 1], g.ident[:], start=True, stop=True)
                to_dve.filled(last)

            def weigh(b):
                lane.wait(negmax_ready)
                tiles = key_tiles(b)
                acc = out[:, b % 2, :]
                plan = aside(b)

                def values(j):
                    k, off = tiles[j]
                    lane.wait(probs_ready)
                    return nc.tensor.matmul(acc[0:M, off:QB], v[:, k, :], probs[:, j % 4, off:QB],
                                            start=j == 0, stop=j == len(tiles) - 1)

                for j, (k, off) in enumerate(tiles):
                    bank = scoresT[:, j % 2, off:QB]
                    diag = causal and k >= 4 * b
                    kk, qq = (ks, qs) if causal else (kT, qT)
                    last = nc.tensor.matmul(bank, kk[:, k * P:(k + 1) * P], qq[:, b * QB + off:(b + 1) * QB],
                                            start=True, stop=not diag)
                    if diag:
                        last = nc.tensor.matmul(scoresT[:, j % 2, off:off + P], ident[:], mask_k[:], start=False, stop=True)
                    last.then_inc(scores_ready, 1)
                    for kind, *item in plan[j]:
                        if kind == "max":
                            find_max(b + 1, *item)
                        else:
                            project()
                    if j == len(tiles) - 1 and b + 1 < NB:
                        turn_max()
                    if j > 0:
                        values(j - 1)
                values(len(tiles) - 1).then_inc(out_ready, 1)

            per = {ring.freed: n_ring, w_ready: 1 if causal else 3, wo_ready: 1, prepared: 1 if causal else 2 * NB,
                   v_ready: 1, max_ready: NB, negmax_ready: NB, probs_ready: n_keys, oT_ready: NB}
            with lane.loop(heads, per) as h:
                lane.wait(w_ready, per[w_ready])
                for b in range(NB):
                    s = slice(b * QB, (b + 1) * QB)
                    if causal:
                        for side in range(2):
                            bank = to_dve.take()
                            for i, part in enumerate((hi, mid, lo)):
                                last = nc.tensor.matmul(bank[:, :], sel[:, 3 * side + i, :], part[:, s],
                                                        start=i == 0, stop=i == 2)
                            to_dve.filled(last)
                    else:
                        for i in range(4):
                            bank = to_dve.take()
                            to_dve.filled(nc.tensor.matmul(bank[:, :], wh[:, i, :, :].rearrange("p a d -> p (a d)"),
                                                           g.xT[:, s], start=True, stop=True))
                        bank = to_dve.take()
                        for t in range(4):
                            tok = (4 * b + t) * P
                            last = nc.tensor.matmul(bank[:, t * D:(t + 1) * D], g.xT[:, tok:tok + P], wv[:],
                                                    start=True, stop=True)
                        to_dve.filled(last)
                project()
                lane.wait(wo_ready)
                lane.wait(prepared, per[prepared])
                for item in maxima(0):
                    find_max(0, *item)
                turn_max()
                lane.wait(v_ready)
                for b in range(NB):
                    weigh(b)
            project()

        @block.scalar
        def _(act):
            lane = Lane(act, None)
            lane.seen[sum_ready] = begun
            per = {scores_ready: n_keys}
            if not causal:
                per |= {sum_ready: 2 * NB}
            with lane.loop(heads, per) as h:
                if not causal:
                    for b in range(NB):
                        s = slice(b * QB, (b + 1) * QB)
                        lane.wait(sum_ready)
                        nc.scalar.copy(q_hm[:, s], qT[:, s]).then_inc(hi_ready, 1)
                        lane.wait(sum_ready)
                        nc.scalar.activation(kT[:, s], k_twice[:, s], ACT.Identity, bias=k_keep[:, 1:2], scale=k_keep[:, 0:1])
                        nc.scalar.copy(k_hh[:, s], k_twice[:, s]).then_inc(hi_ready, 1)
                for b in range(NB):
                    for j, (k, off) in enumerate(key_tiles(b)):
                        lane.wait(scores_ready)
                        nc.scalar.activation(probs[:, j % 4, off:QB], scoresT[:, j % 2, off:QB], ACT.Exp,
                                             scale=scale).then_inc(probs_ready, 1)

        @block.vector
        def _(dve):
            lane = Lane(dve, own)
            from_pe = ring.reader(lane)
            dve.sem_inc(w_used, 1)
            dve.sem_inc(oT_ready, 1)

            def prepare(h):
                for b in range(NB):
                    s = slice(b * QB, (b + 1) * QB)
                    if causal:
                        bank = from_pe.take()
                        from_pe.free(nc.vector.tensor_copy(qs[:, s], bank[:, :]))
                        bank = from_pe.take()
                        from_pe.free(nc.vector.tensor_scalar(ks[:, s], bank[:, :], g.e012[:], None, ALU.add))
                        continue
                    for dst in (qT, k_twice):
                        bank = from_pe.take()
                        from_pe.free(nc.vector.tensor_tensor(dst[:, s], bank[:, :], cos[:, s], ALU.mult))
                        bank = from_pe.take()
                        from_pe.free(nc.vector.tensor_tensor(rotated[:], bank[:, :], sin[:, s], ALU.mult))
                        from_pe.settle()
                        lane.post(nc.vector.tensor_tensor(dst[:, s], rotated[:], dst[:, s], ALU.add))
                        lane.settle()
                        dve.sem_inc(sum_ready, 1)
                    bank = from_pe.take()
                    from_pe.free(nc.vector.tensor_copy(v[:, 4 * b:4 * b + 4, 0:D],
                                                       bank[:, 0:4 * D].rearrange("p (t d) -> p t d", t=4)))
                if causal:
                    from_pe.settle()
                    dve.sem_inc(prepared, 1)
                    lane.seq(nc.vector.tensor_copy(v[:, :, 0:D], v_all[:, :, h, :]))
                from_pe.settle()
                dve.sem_inc(v_ready, 1)
                dve.sem_inc(w_used, 1)

            def add_projected(b):
                s = slice(b * QB, (b + 1) * QB)
                bank = from_pe.take()
                from_pe.free(nc.vector.tensor_tensor(yT[:, s], bank[:, :], yT[:, s], ALU.add))

            def read_max(qt, c, first, n):
                bank = from_pe.take()
                from_pe.free(nc.vector.reduce_max(chunk_max[:, qt, c:c + 1], bank[:, 0:n], axis=AX.X))

            def finish_max(b):
                from_pe.settle()
                n = len(chunks(b, 0))
                ins = nc.vector.reduce_max(row_max[:], chunk_max[:, :, 0:n], axis=AX.X)
                if causal:
                    lane.seq(ins)
                    lane.seq(nc.vector.tensor_scalar(neg_parts[:, 0, :], row_max[:], -1.0, None, ALU.mult))
                    lane.seq(nc.vector.scalar_tensor_tensor(neg_rest[:], row_max[:], -1.0, neg_parts[:, 0, :],
                                                            ALU.mult, ALU.subtract))
                    lane.seq(nc.vector.tensor_copy(neg_parts[:, 1, :], neg_rest[:]))
                    ins = nc.vector.tensor_tensor(neg_parts[:, 2, :], neg_rest[:], neg_parts[:, 1, :], ALU.subtract)
                ins.then_inc(max_ready, 1)

            def write_max(b):
                s = slice(b * QB, (b + 1) * QB)
                bank = from_pe.take()
                if causal:
                    from_pe.free(nc.vector.tensor_copy(qs[0:3, s], bank[0:3, :]))
                else:
                    from_pe.free(nc.vector.tensor_scalar(qT[64:65, s], bank[0:1, :], -1.0, None, ALU.mult))
                from_pe.settle()
                dve.sem_inc(negmax_ready, 1)

            def normalise(b):
                acc = out[:, b % 2, :]
                lane.wait(out_ready)
                lane.seq(nc.vector.reciprocal(rsum[:], acc[S0:M, :]))
                ins = nc.vector.tensor_tensor(oT[0:D, :], acc[0:D, :], rsum[:], ALU.mult)
                if causal and b == 0:
                    lane.seq(ins)
                    ins = nc.vector.memset(oT[:, 0:1], 0.0)
                ins.then_inc(oT_ready, 1)

            per = {ring.filled: n_ring, ring.freed: n_ring, out_ready: NB, own: HEAD_STEPS[name]}
            with lane.loop(heads, per) as h:
                prepare(h)
                add_projected(NB - 1)
                from_pe.settle()
                dve.sem_inc(projected, 1)
                for item in maxima(0):
                    read_max(*item)
                finish_max(0)
                write_max(0)
                for b in range(NB):
                    if b > 0:
                        normalise(b - 1)
                    for items in aside(b):
                        for kind, *item in items:
                            if kind == "max":
                                read_max(*item)
                            else:
                                add_projected(b - 1)
                    if b + 1 < NB:
                        finish_max(b + 1)
                        write_max(b + 1)
                normalise(NB - 1)
            add_projected(NB - 1)


E_ = 8
F_ = 512
FT = F_ // P
TOPK = T // E_
EXPERT_COLS = F_ + FT * C + FT + 1


def stage_l0_ffn(nc, g, d, y):
    with ExitStack() as ctx:
        def sb(n, shape, dt=fp32):
            return ctx.enter_context(nc.sbuf_tensor(f"l0f_{n}", shape, dt))
        ws, bs = sb("ws", [P, E_]), sb("bs", [P, NT, E_])
        probsT = sb("probsT", [E_, T])
        left = sb("left", [E_, T])
        gates = sb("gates", [E_, T])
        expert_out = sb("expert_out", [C, E_, T])
        select = sb("select", [E_, E_, P])
        load(nc, "l0f", [(ws[:], d["L0_ffn_Ws"]), (bs[:], d["h_l0_bs"]), (select[:], d["c_select8"])])
        route(nc, g, ws, bs, probsT, left)
        experts(nc, g, d, probsT, left, gates, expert_out)
        combine(nc, g, select, gates, expert_out)
    layernorm(nc, g, "ln1", feature=g.delta)


def route(nc, g, ws, bs, probsT, left):
    with ExitStack() as ctx:
        def sb(n, shape, dt=fp32):
            return ctx.enter_context(nc.sbuf_tensor(f"rt_{n}", shape, dt))

        def sem(n):
            return nc.alloc_semaphore(f"rt_{n}")
        p = sb("p", [P, NT, E_])
        row = sb("row", [P, NT])
        logits = ctx.enter_context(nc.psum_tensor("rt_logits", [P, NT, E_], fp32))
        turned = ctx.enter_context(nc.psum_tensor("rt_turned", [E_, T], fp32))
        logits_ready, shifted = sem("logits_ready"), sem("shifted")
        exp_ready, p_ready, turned_ready = sem("exp_ready"), sem("p_ready"), sem("turned_ready")
        own = sem("dve_steps")
        block = ctx.enter_context(nc.Block())

        @block.tensor
        def _(pe):
            for t in range(NT):
                last = nc.tensor.matmul(logits[:, t, :], g.xT[:, t * P:(t + 1) * P], ws[:], start=True, stop=True)
            last.then_inc(logits_ready, 1)
            pe.wait_ge(p_ready, 1)
            for t in range(NT):
                last = nc.tensor.transpose(turned[:, t * P:(t + 1) * P], p[:, t, :], g.ident[:])
            last.then_inc(turned_ready, 1)

        @block.vector
        def _(dve):
            lane = Lane(dve, own)
            dve.wait_ge(logits_ready, 1)
            lane.seq(nc.vector.tensor_tensor(p[:], logits[:], bs[:], ALU.add))
            lane.seq(nc.vector.reduce_max(row[:], p[:], axis=AX.X))
            nc.vector.tensor_tensor(p[:], p[:], spread(row[:], E_), ALU.subtract).then_inc(shifted, 1)
            dve.wait_ge(exp_ready, 1)
            lane.seq(nc.vector.reduce_sum(row[:], p[:], axis=AX.X))
            lane.seq(nc.vector.reciprocal(row[:], row[:]))
            nc.vector.tensor_tensor(p[:], p[:], spread(row[:], E_), ALU.mult).then_inc(p_ready, 1)
            dve.wait_ge(turned_ready, 1)
            nc.vector.tensor_copy(probsT[:], turned[:])
            nc.vector.tensor_copy(left[:], turned[:])

        @block.scalar
        def _(act):
            act.wait_ge(shifted, 1)
            nc.scalar.activation(p[:], p[:], ACT.Exp).then_inc(exp_ready, 1)


def spread(ap, n):
    return ap.unsqueeze(2).to_broadcast([ap.shape[0], ap.shape[1], n])


def experts(nc, g, d, probsT, left, gates, expert_out):
    with ExitStack() as ctx:
        def sb(n, shape, dt=fp32):
            return ctx.enter_context(nc.sbuf_tensor(f"ex_{n}", shape, dt))

        def sem(n):
            return nc.alloc_semaphore(f"ex_{n}")
        w = sb("w", [P, 2, EXPERT_COLS])
        hidden = sb("hidden", [P, 2, FT, QB])
        best = sb("best", [E_, 8])
        up = ctx.enter_context(nc.psum_tensor("ex_up", [P, FT, QB], fp32))
        down = ctx.enter_context(nc.psum_tensor("ex_down", [P, 2, QB], fp32))
        loaded = [sem(f"loaded{s}") for s in range(2)]
        w_free = sem("w_free")
        up_ready = sem("up_ready")
        up_done = sem("up_done")
        down_ready = sem("down_ready")
        down_done = sem("down_done")
        own = sem("dve_steps")
        block = ctx.enter_context(nc.Block())
        b1_at, b2_at = F_ + FT * C, F_ + FT * C + FT

        @block.sync
        def _(sp):
            lane = Lane(sp, None)
            with lane.loop(E_ // 2, {w_free: 2}) as i:
                for s in range(2):
                    lane.wait(w_free)
                    sp.dma_start(w[:, s, :], d["h_l0_experts"][2 * i + s]).then_inc(loaded[s], 16)

        @block.tensor
        def _(pe):
            lane = Lane(pe, None)
            with lane.loop(E_ // 2, {loaded[0]: 16, loaded[1]: 16, up_done: 2 * NB * FT,
                                     down_done: 2 * NB}) as i:
                for s in range(2):
                    lane.wait(loaded[s], 16)

                    def make_up(b):
                        for f in range(FT):
                            lane.wait(up_done)
                            nc.tensor.matmul(up[:, f, :], w[:, s, f * P:(f + 1) * P], g.xT[:, b * QB:(b + 1) * QB],
                                             start=True, stop=True).then_inc(up_ready, 1)

                    def make_down(b):
                        lane.wait(down_done)
                        for f in range(FT):
                            last = nc.tensor.matmul(down[:, b % 2, :], w[:, s, F_ + f * C:F_ + (f + 1) * C],
                                                    hidden[:, b % 2, f, :], start=f == 0, stop=f == FT - 1)
                        last.then_inc(down_ready, 1)
                    make_up(0)
                    for b in range(1, NB):
                        make_up(b)
                        make_down(b - 1)
                    pe.wait_ge(up_done, lane.base[up_done] + lane.seen[up_done] + FT)
                    make_down(NB - 1)

        @block.scalar
        def _(act):
            lane = Lane(act, None)
            act.sem_inc(up_done, FT)
            act.sem_inc(down_done, 2)
            act.sem_inc(w_free, 2)
            with lane.loop(E_ // 2, {up_ready: 2 * NB * FT, down_ready: 2 * NB}) as i:
                for s in range(2):
                    def gelu(b):
                        for f in range(FT):
                            lane.wait(up_ready)
                            nc.scalar.activation(hidden[:, b % 2, f, :], up[:, f, :], ACT.Gelu_apprx_tanh,
                                                 bias=w[:, s, b1_at + f:b1_at + f + 1]).then_inc(up_done, 1)

                    def store(b):
                        lane.wait(down_ready)
                        nc.scalar.activation(expert_out[:, 2 * i + s, b * QB:(b + 1) * QB], down[:, b % 2, :],
                                             ACT.Identity, bias=w[:, s, b2_at:b2_at + 1]).then_inc(down_done, 1)
                    gelu(0)
                    for b in range(1, NB):
                        gelu(b)
                        store(b - 1)
                    store(NB - 1)
                    act.wait_ge(down_done, 2 + NB * (2 * i + s + 1))
                    act.sem_inc(w_free, 1)

        @block.vector
        def _(dve):
            lane = Lane(dve, own)
            for _ in range(TOPK // 8):
                lane.seq(nc.vector.max(best[:], left[:]))
                lane.seq(nc.vector.match_replace(left[:], best[:], left[:], -1.0))
            nc.vector.scalar_tensor_tensor(gates[:], left[:], 0.0, probsT[:], ALU.is_lt, ALU.mult)


def combine(nc, g, select, gates, expert_out):
    with ExitStack() as ctx:
        def sem(n):
            return nc.alloc_semaphore(f"cb_{n}")
        part = ctx.enter_context(nc.sbuf_tensor("cb_part", [P, 2, T // 2], fp32))
        spread_gate = ctx.enter_context(nc.psum_tensor("cb_gate", [P, 2, 2, QB], fp32))
        gate_ready, gate_used = sem("gate_ready"), sem("gate_used")
        own = sem("dve_steps")
        block = ctx.enter_context(nc.Block())
        H = T // 2

        @block.tensor
        def _(pe):
            n = 0
            for e in range(E_):
                for half in range(2):
                    if n >= 2:
                        pe.wait_ge(gate_used, n - 1)
                    for b in range(2):
                        at = half * H + b * QB
                        last = nc.tensor.matmul(spread_gate[:, half, b, :], select[:, e, :], gates[:, at:at + QB],
                                                start=True, stop=True)
                    last.then_inc(gate_ready, 1)
                    n += 1

        @block.vector
        def _(dve):
            lane = Lane(dve, own)
            n = 0
            for e in range(E_):
                for half in range(2):
                    n += 1
                    s = slice(half * H, (half + 1) * H)
                    dve.wait_ge(gate_ready, n)
                    weight = spread_gate[:, half].rearrange("p b q -> p (b q)")
                    dst = g.delta[:, s] if e == 0 else part[:, half, :]
                    nc.vector.tensor_tensor(dst, weight, expert_out[:, e, s], ALU.mult).then_inc(gate_used, 1)
                    dve.wait_ge(gate_used, n)
                    if e:
                        lane.seq(nc.vector.tensor_tensor(g.delta[:, s], part[:, half, :], g.delta[:, s], ALU.add))


DEPTH = 6
LH = 16
LD = 64
INNER = LH * LD
WIN = 32
SPAN = WIN + P
GROUP = 3
GROUPS = [list(range(a, min(a + GROUP, LH))) for a in range(0, LH, GROUP)]
FI = int(C * 4 * 2 / 3)
FCH = [(a, min(P, FI - a)) for a in range(0, FI, P)]
LEFT = 64
QK_SCALE = 8.0
PIECES = 6
A_RING, C_RING = PIECES + 4, 3


def hold(eng, sem):
    eng.sem_inc(sem, 1)


def shift_copy(nc, lane, held, dst, src, first, count, ready):
    hold(lane.eng, held)
    lane.seq(nc.gpsimd.tensor_copy(dst[0:C // 2, :], src[0:C // 2, bass.ds(first + LEFT, count)]))
    hold(lane.eng, held)
    nc.gpsimd.tensor_copy(dst[C // 2:C, :], src[C // 2:C, bass.ds(first + LEFT - 1, count)]).then_inc(ready, 1)


def stage_l1_ffn(nc, g, d, y):
    with ExitStack() as ctx:
        def sb(n, shape, dt=fp32):
            return ctx.enter_context(nc.sbuf_tensor(f"lw_{n}", shape, dt))

        def sem(n):
            return nc.alloc_semaphore(f"lw_{n}")
        L = Shared()
        L.sb = sb
        L.xa, L.xb = sb("xa", [C, LEFT + T + P]), sb("xb", [C, LEFT + T + P])
        L.wqkv, L.wo = sb("wqkv", [C, 3 * INNER]), sb("wo", [P, INNER // P, C])
        L.w1, L.w2 = sb("w1", [C, 2 * FI]), sb("w2", [P, len(FCH), C])
        L.scales = sb("scales", [P, 4, LD])
        L.cols = sb("cols", [P, 3 + 2 * len(FCH)])
        L.rope = sb("rope", [P, NT, 4, LD])
        L.band = sb("band", [P, 2, SPAN], bf16)
        L.ident16 = sb("ident16", [P, P], bf16)
        L.halo_scale = sb("halo_scale", [P, 1])
        L.minus_half = sb("minus_half", [P, 2 * LH])
        L.bank = ctx.enter_context(nc.psum_tensor("lw_bank", [P, 8, QB], fp32))
        band32 = sb("band32", [P, 2, SPAN])
        cleared = sem("cleared")
        L.held, L.held_sp = sem("held"), sem("held_sp")
        load(nc, "lw", [(L.rope[:], d["c_rope"]), (band32[:], d["c_band"]), (L.halo_scale[:], d["c_halo_scale"])])
        with nc.Block() as block:
            @block.vector
            def _(dve):
                nc.vector.memset(L.xa[:], 0.0).then_inc(cleared, 1)
                nc.vector.memset(L.xb[:], 0.0)
                nc.vector.tensor_copy(L.band[:], band32[:])
                nc.vector.tensor_copy(L.ident16[:], g.ident[:])
                dve.wait_ge(cleared, 1)
                nc.vector.tensor_copy(L.xa[:, LEFT:LEFT + T], g.xT[:])

            @block.gpsimd
            def _(pool):
                nc.gpsimd.memset(L.minus_half[:], -0.5)
        A = LocalAttention(nc, g, L, ctx)
        with nc.Block() as block:
            @block.scalar
            def _(act):
                act.sem_inc(A.ring_freed, 2)
        F = LocalFfn(nc, g, L, ctx)
        w_loaded = sem("w_loaded")
        with nc.Fori(0, DEPTH) as layer:
            with nc.Block() as block:
                @block.sync
                def _(sp):
                    for dst, src in ((L.wqkv[:], "L1_ffn_Wqkv"), (L.wo[:], "h_lw_wo"), (L.w1[:], "L1_ffn_W1"),
                                     (L.w2[:], "h_lw_w2"), (L.scales[:], "h_lw_scales"), (L.cols[:], "h_lw_cols")):
                        sp.dma_start(dst, d[src][layer]).then_inc(w_loaded, 16)
                    sp.wait_ge(w_loaded, 16 * 6 * (layer + 1))
                    hold(sp, L.held_sp)
            A.run(layer)
            F.run(layer)
        with nc.Block() as block:
            @block.vector
            def _(dve):
                nc.vector.tensor_copy(g.delta[:], L.xa[:, LEFT:LEFT + T])
    layernorm(nc, g, "ln3", feature=g.delta)


class LocalAttention:

    def __init__(self, nc, g, L, ctx):
        self.nc, self.g, self.L = nc, g, L

        def sem(n):
            return nc.alloc_semaphore(f"la_{n}")

        def sb(n, shape, dt=fp32):
            return ctx.enter_context(nc.sbuf_tensor(f"la_{n}", shape, dt))
        self.xs = sb("xs", [C, 2, P])
        self.raw = sb("raw", [P, 2 * LH, LD])
        self.square = sb("square", [P, 2 * LH, LD])
        self.roped = sb("roped", [P, 2 * LH, LD])
        self.turn = sb("turn", [P, 2 * LH, LD])
        self.tab = sb("tab", [P, 4, LD])
        self.sumsq = sb("sumsq", [P, 2 * LH])
        self.rnorm = sb("rnorm", [P, 2, 2 * LH])
        self.qfac = sb("qfac", [P, 2, 2, LH])
        self.v = sb("v", [P, 2, INNER])
        self.vh = sb("vh", [WIN, 2, INNER])
        self.qT = sb("qT", [P, 2, LH // 2, P])
        self.kT = sb("kT", [P, 2, LH, SPAN])
        self.rowmax = sb("rowmax", [P, LH])
        self.bias = sb("bias", [P, LH])
        self.rowsum = sb("rowsum", [P, LH])
        self.rrow = sb("rrow", [P, LH])
        self.p = sb("p", [P, 3, GROUP, SPAN])
        self.pT = sb("pT", [P, 2, GROUP, P])
        self.pTh = sb("pTh", [WIN, 2, GROUP, WIN])
        self.o = sb("o", [P, INNER])
        self.oT = sb("oT", [P, INNER // P, C])
        self.ring_filled = sem("ring_filled")
        self.ring_freed = sem("ring_freed")
        self.scores_ready = sem("scores_ready")
        self.bias_ready = sem("bias_ready")
        self.probs_ready = sem("probs_ready")
        self.pT_ready = sem("pT_ready")
        self.pT_copied = sem("pT_copied")
        self.out_ready = sem("out_ready")
        self.o_ready = sem("o_ready")
        self.vh_ready = sem("vh_ready")
        self.q_roped = sem("q_roped")
        self.xs_ready = sem("xs_ready")
        self.tab_ready = sem("tab_ready")
        self.squares_ready = sem("squares_ready")
        self.sums_ready = sem("sums_ready")
        self.rot_ready = sem("rot_ready")
        self.rope_done = sem("rope_done")
        self.halo_ready = sem("halo_ready")
        self.dve_steps = sem("dve_steps")
        self.act_steps = sem("act_steps")
        self.pool_steps = sem("pool_steps")
        with nc.Block() as block:
            @block.vector
            def _(dve):
                nc.vector.memset(self.kT[:], 0.0)
                nc.vector.memset(self.vh[:], 0.0)
        groups = len(GROUPS)
        self.per_tile = {
            self.ring_filled: A_RING + C_RING, self.ring_freed: A_RING + C_RING,
            self.scores_ready: groups, self.bias_ready: groups, self.probs_ready: groups,
            self.pT_ready: groups, self.pT_copied: groups, self.out_ready: 1, self.o_ready: 1,
            self.vh_ready: 1, self.q_roped: 1, self.xs_ready: 1, self.tab_ready: 1,
            self.squares_ready: 2, self.sums_ready: 1, self.rot_ready: 2, self.rope_done: 1,
            self.halo_ready: 1, self.dve_steps: groups + 1, self.pool_steps: 6}

    def steps(self, lane, body):
        body(0, None, None, 0, False)
        body(1, 0, None, 1, True)
        with lane.loop((NT - 2) // 2, {sem: 2 * by for sem, by in self.per_tile.items()}) as i:
            body(2 * i + 2, 2 * i + 1, 2 * i, 0, False)
            body(2 * i + 3, 2 * i + 2, 2 * i + 1, 1, False)
        body(None, NT - 1, NT - 2, 0, False)
        body(None, None, NT - 1, 1, False)

    def base(self, layer, given=0):
        base = {sem: layer * by * NT for sem, by in self.per_tile.items()}
        base[self.ring_freed] = layer * (A_RING + C_RING) * NT + given
        base[self.xs_ready] = layer * (NT + 1)
        base[self.pool_steps] = layer * (6 * NT + 1)
        return base

    def check(self, lane):
        for sem, by in self.per_tile.items():
            assert lane.seen.get(sem, 0) <= by * NT + 1, (sem.name, lane.seen[sem], by * NT)

    def run(self, layer):
        nc, g, L = self.nc, self.g, self.L
        S = self
        bank = L.bank
        RING, SCORES, PT, OUT = 0, 2, 5, 6
        out = bank[:, OUT:OUT + 2, :].rearrange("p b q -> p (b q)")

        def scores_of(k):
            return bank[:, SCORES + k % 3, 0:GROUP * SPAN].rearrange("p (h s) -> p h s", s=SPAN)
        with nc.Block() as block:
            @block.gpsimd
            def _(pool):
                lane = Lane(pool, S.pool_steps, S.base(layer, given=2))
                one = nc.gpsimd

                def shifted(t, slot):
                    shift_copy(nc, lane, L.held, S.xs[:, slot, :], L.xa, t * P, P, S.xs_ready)
                    lane.wait(S.xs_ready)
                    hold(pool, L.held)

                def body(a, b, c, s, first):
                    if a is None:
                        return
                    one.tensor_tensor(S.tab[:], L.rope[:, a, :, :], L.scales[:], ALU.mult).then_inc(S.tab_ready, 1)
                    for half in range(2):
                        hs = slice(half * LH, (half + 1) * LH)
                        lane.wait(S.ring_freed, 2)
                        one.tensor_tensor(S.square[:, hs, :], S.raw[:, hs, :], S.raw[:, hs, :],
                                          ALU.mult).then_inc(S.squares_ready, 1)
                    lane.skip(S.ring_freed, A_RING - 4 + (C_RING if c is not None else 0))
                    lane.wait(S.rot_ready)
                    one.tensor_tensor(S.roped[:, 0:LH, :], S.roped[:, 0:LH, :], S.turn[:, 0:LH, :], ALU.add).then_inc(S.q_roped, 1)
                    lane.wait(S.sums_ready)
                    hold(pool, L.held)
                    lane.seq(one.tensor_scalar(S.sumsq[:], S.sumsq[:], 1e-24, None, ALU.max))
                    lane.seq(one.tensor_tensor(S.rnorm[:, s, :], S.sumsq[:], L.minus_half[:], ALU.pow))
                    hold(pool, L.held)
                    lane.post(one.tensor_scalar(S.qfac[:, s, 0, :], S.rnorm[:, s, 0:LH], QK_SCALE, None, ALU.mult))
                    lane.post(one.tensor_scalar(S.qfac[:, s, 1, :], S.rnorm[:, s, 0:LH], -QK_SCALE, None, ALU.mult))
                    lane.wait(S.rot_ready)
                    lane.seq(one.tensor_tensor(S.roped[:, LH:, :], S.roped[:, LH:, :], S.turn[:, LH:, :], ALU.add))
                    one.tensor_tensor(S.roped[:, LH:, :], S.roped[:, LH:, :], spread(S.rnorm[:, s, LH:], LD),
                                      ALU.mult).then_inc(S.rope_done, 1)
                    lane.wait(S.rope_done)
                    shifted(a + 1, 1 - s)
                shifted(0, 0)
                S.steps(lane, body)
                S.check(lane)

            @block.tensor
            def _(pe):
                lane = Lane(pe, None, S.base(layer))
                place = [0]

                def ring():
                    lane.wait(S.ring_freed)
                    place[0] += 1
                    return bank[:, RING + (place[0] - 1) % 2, :]

                def body(a, b, c, s, first):
                    o = 1 - s

                    def scores(k):
                        dst = scores_of(k)
                        for i, h in enumerate(GROUPS[k]):
                            nc.tensor.matmul(dst[:, i, :], S.qT[:, o, h // 2, :], S.kT[:, o, h, :], start=True, stop=False)
                            last = nc.tensor.matmul(dst[:, i, :], L.ident16[:], L.band[:, 1 if first else 0, :],
                                                    start=False, stop=True)
                        last.then_inc(S.scores_ready, 1)

                    def transpose_probs(k):
                        lane.wait(S.probs_ready)
                        for i, h in enumerate(GROUPS[k]):
                            nc.tensor.transpose(bank[:, PT, i * P:(i + 1) * P], S.p[:, k % 3, i, WIN:SPAN], g.ident[:])
                        for i, h in enumerate(GROUPS[k]):
                            at = GROUP * P + i * WIN
                            last = nc.tensor.transpose(bank[0:WIN, PT, at:at + WIN], S.p[0:WIN, k % 3, i, 0:WIN],
                                                       g.ident[0:WIN, 0:WIN])
                        last.then_inc(S.pT_ready, 1)

                    def values(k):
                        lane.wait(S.pT_copied)
                        for i, h in enumerate(GROUPS[k]):
                            cols = slice(h * LD, (h + 1) * LD)
                            nc.tensor.matmul(out[:, cols], S.pT[:, k % 2, i, :], S.v[:, o, cols], start=True, stop=True)
                            last = nc.tensor.matmul(out[0:WIN, cols], S.pTh[:, k % 2, i, :], S.vh[:, o, cols],
                                                    start=False, stop=True, skip_group_check=True)
                        return last

                    def project(j):
                        nc.tensor.matmul(ring(), S.xs[:, s, :], L.wqkv[:, j * QB:(j + 1) * QB],
                                         start=True, stop=True).then_inc(S.ring_filled, 1)

                    def turn(src, j):
                        dst = ring()
                        for i in range(4):
                            at = (4 * j + i) * P
                            last = nc.tensor.transpose(dst[:, i * P:(i + 1) * P], src[:, at:at + P], g.ident[:])
                        last.then_inc(S.ring_filled, 1)

                    def output():
                        dst = ring()
                        lane.ahead(S.ring_freed, 1)
                        for i in range(INNER // P):
                            nc.tensor.matmul(dst[:, 0:P], L.wo[:, i, :], S.oT[:, i, :], start=i == 0, stop=False)
                        nc.tensor.matmul(dst[:, 0:P], g.ident[:], L.xa[:, bass.ds(c * P + LEFT, P)],
                                         start=False, stop=True).then_inc(S.ring_filled, 1)
                    flat = S.roped[:].rearrange("p h d -> p (h d)")
                    if a is not None:
                        lane.wait(S.xs_ready)
                        for k in range(4):
                            project(k)
                    if b is not None:
                        lane.ahead(S.ring_freed, 0 if a is not None else 2)
                        lane.wait(S.halo_ready)
                        lane.wait(S.vh_ready)
                        for k in range(3):
                            scores(k)
                    if c is not None:
                        lane.wait(S.o_ready)
                        for j in range(2):
                            turn(S.o[:], j)
                    for k in range(PIECES):
                        if b is not None:
                            transpose_probs(k)
                            if k + 3 < PIECES:
                                scores(k + 3)
                        if a is not None and k in (0, 2):
                            project(4 + k // 2)
                        if c is not None and k == 1:
                            output()
                        if a is not None and k in (3, 4):
                            if k == 3:
                                lane.wait(S.q_roped)
                            turn(flat, k - 3)
                        if b is not None:
                            last = values(k)
                    if b is not None:
                        last.then_inc(S.out_ready, 1)
                    if a is not None:
                        lane.wait(S.rope_done)
                        for j in (2, 3):
                            turn(flat, j)
                S.steps(lane, body)
                S.check(lane)

            @block.scalar
            def _(act):
                lane = Lane(act, S.act_steps, S.base(layer, given=2))
                place = [0]

                def taken():
                    lane.wait(S.ring_filled)
                    lane.skip(S.ring_freed, 1)
                    place[0] += 1
                    return bank[:, RING + (place[0] - 1) % 2, :]

                def copy(dst, shape=None):
                    src = taken()
                    if shape:
                        src = src.rearrange("p (a b) -> p a b", b=shape)
                    nc.scalar.copy(dst, src).then_inc(S.ring_freed, 1)

                def body(a, b, c, s, first):
                    o = 1 - s

                    def weigh(k):
                        lane.wait(S.bias_ready)
                        src = scores_of(k)
                        for i, h in enumerate(GROUPS[k]):
                            last = nc.scalar.activation(S.p[:, k % 3, i, :], src[:, i, :], ACT.Exp,
                                                        bias=S.bias[:, h:h + 1], scale=S.qfac[:, o, 0, h:h + 1],
                                                        accum_out=S.rowsum[:, h:h + 1])
                        last.then_inc(S.probs_ready, 1)
                    if a is not None:
                        for k in range(4):
                            copy(S.raw[:, 8 * k:8 * k + 8, :], shape=LD)
                    if b is not None:
                        weigh(0)
                    if c is not None:
                        for j in range(2):
                            copy(S.oT[:, 4 * j:4 * j + 4, :], shape=C)
                    for k in range(PIECES):
                        if b is not None and k + 1 < PIECES:
                            weigh(k + 1)
                        if a is not None and k in (0, 2):
                            copy(S.v[:, s, (k // 2) * QB:(k // 2 + 1) * QB])
                        if c is not None and k == 1:
                            copy_y = taken()
                            nc.scalar.copy(L.xb[:, bass.ds(c * P + LEFT, P)], copy_y[:, 0:P]).then_inc(S.ring_freed, 1)
                        if a is not None and k in (3, 4):
                            copy(S.qT[:, s, 4 * (k - 3):4 * (k - 3) + 4, :], shape=P)
                        if a is not None and k == 4:
                            if b is not None:
                                lane.ahead(S.ring_freed, 0)
                                nc.scalar.copy(S.vh[:, s, :], S.v[P - WIN:P, o, :]).then_inc(S.vh_ready, 1)
                            else:
                                act.sem_inc(S.vh_ready, 1)
                    if a is not None:
                        for j in range(2):
                            src = taken().rearrange("p (a b) -> p a b", b=P)
                            nc.scalar.copy(S.kT[0:LD, s, 8 * j:8 * j + 8:2, WIN:SPAN], src[0:LD])
                            nc.scalar.copy(S.kT[LD:P, s, 8 * j + 1:8 * j + 8:2, WIN:SPAN], src[LD:P]).then_inc(S.ring_freed, 1)
                S.steps(lane, body)
                S.check(lane)

            @block.vector
            def _(dve):
                lane = Lane(dve, S.dve_steps, S.base(layer, given=2))

                def body(a, b, c, s, first):
                    o = 1 - s

                    def find_bias(k):
                        lane.wait(S.scores_ready)
                        src = scores_of(k)
                        h0, n = GROUPS[k][0], len(GROUPS[k])
                        hs = slice(h0, h0 + n)
                        lane.seq(nc.vector.reduce_max(S.rowmax[:, hs], src[:, 0:n, :], axis=AX.X))
                        nc.vector.tensor_tensor(S.bias[:, hs], S.rowmax[:, hs], S.qfac[:, o, 1, hs],
                                                ALU.mult).then_inc(S.bias_ready, 1)

                    def copy_probs(k):
                        lane.wait(S.pT_ready)
                        n = len(GROUPS[k])
                        nc.vector.tensor_copy(S.pT[:, k % 2, 0:n, :],
                                              bank[:, PT, 0:n * P].rearrange("p (h q) -> p h q", q=P))
                        at = GROUP * P
                        nc.vector.tensor_copy(S.pTh[:, k % 2, 0:n, :],
                                              bank[0:WIN, PT, at:at + n * WIN].rearrange("p (h q) -> p h q", q=WIN)
                                              ).then_inc(S.pT_copied, 1)

                    def rotate(half):
                        hs = slice(half * LH, (half + 1) * LH)
                        lane.wait(S.ring_freed, 2)
                        if half == 0:
                            lane.wait(S.tab_ready)
                        tab = S.tab[:, 2 * half:2 * half + 2, :]

                        def heads_of(x):
                            return x.unsqueeze(1).to_broadcast([P, LH, x.shape[-1]])
                        H2 = LD // 2
                        nc.vector.tensor_tensor(S.roped[:, hs, :], S.raw[:, hs, :], heads_of(tab[:, 0, :]), ALU.mult)
                        nc.vector.tensor_tensor(S.turn[:, hs, 0:H2], S.raw[:, hs, H2:LD], heads_of(tab[:, 1, 0:H2]), ALU.mult)
                        nc.vector.tensor_tensor(S.turn[:, hs, H2:LD], S.raw[:, hs, 0:H2], heads_of(tab[:, 1, H2:LD]),
                                                ALU.mult).then_inc(S.rot_ready, 1)
                    if b is not None:
                        lane.wait(S.rope_done)
                        if first:
                            nc.vector.memset(S.kT[:, o, :, 0:WIN], 0.0).then_inc(S.halo_ready, 1)
                        else:
                            nc.vector.tensor_scalar(S.kT[:, o, :, 0:WIN], S.kT[:, s, :, P:SPAN], L.halo_scale[:], None,
                                                    ALU.mult).then_inc(S.halo_ready, 1)
                        for k in range(3):
                            find_bias(k)
                    if a is not None:
                        rotate(0)
                    for k in range(PIECES):
                        if b is not None:
                            copy_probs(k)
                            if k + 3 < PIECES:
                                find_bias(k + 3)
                        if a is not None and k == 1:
                            rotate(1)
                        if a is not None and k == 0:
                            lane.wait(S.squares_ready, 2)
                            nc.vector.reduce_sum(S.sumsq[:], S.square[:], axis=AX.X).then_inc(S.sums_ready, 1)
                    if b is not None:
                        lane.seq(nc.vector.reciprocal(S.rrow[:], S.rowsum[:]))
                        lane.wait(S.out_ready)
                        nc.vector.tensor_tensor(S.o[:].rearrange("p (h d) -> p h d", d=LD),
                                                out.rearrange("p (h d) -> p h d", d=LD), spread(S.rrow[:], LD),
                                                ALU.mult).then_inc(S.o_ready, 1)
                    lane.skip(S.ring_freed, (A_RING - 4 if a is not None else 0) + (C_RING if c is not None else 0))
                S.steps(lane, body)
                S.check(lane)


class LocalFfn:

    def __init__(self, nc, g, L, ctx):
        self.nc, self.g, self.L = nc, g, L

        def sb(n, shape, dt=fp32):
            return ctx.enter_context(nc.sbuf_tensor(f"lf_{n}", shape, dt))
        self.xs = sb("xs", [C, 2, QB])
        self.stats = sb("stats", [P, 4, 6])
        self.meanvar = sb("meanvar", [P, 2, 4, 2])
        self.rstd = sb("rstd", [P, 2, 4])
        self.xn = sb("xn", [P, 2, 4, C])
        self.xnT = sb("xnT", [C, QB])
        self.gelu = sb("gelu", [P, 2, QB])
        self.h = sb("h", [P, len(FCH), QB])
        self.xs_ready = nc.alloc_semaphore("lf_xs_ready")
        self.turned = nc.alloc_semaphore("lf_turned")
        self.stats_ready = nc.alloc_semaphore("lf_stats_ready")
        self.rstd_ready = nc.alloc_semaphore("lf_rstd_ready")
        self.xn_ready = nc.alloc_semaphore("lf_xn_ready")
        self.xn_turned = nc.alloc_semaphore("lf_xn_turned")
        self.xnT_ready = nc.alloc_semaphore("lf_xnT_ready")
        self.gate_ready = nc.alloc_semaphore("lf_gate_ready")
        self.gelu_ready = nc.alloc_semaphore("lf_gelu_ready")
        self.a_ready = nc.alloc_semaphore("lf_a_ready")
        self.h_ready = nc.alloc_semaphore("lf_h_ready")
        self.y_ready = nc.alloc_semaphore("lf_y_ready")
        self.y_added = nc.alloc_semaphore("lf_y_added")
        self.dve_steps = nc.alloc_semaphore("lf_dve_steps")
        self.pool_steps = nc.alloc_semaphore("lf_pool_steps")

    def run(self, layer):
        nc, g, L, S = self.nc, self.g, self.L, self
        bank = L.bank
        TURN, BACK, GATE, AFACT, Y = 0, 2, 3, 5, 7
        NCH = len(FCH)

        def upto(sem, per_block, n):
            return layer * (per_block * NB) + n

        def tokens(b):
            return slice(LEFT + b * QB, LEFT + (b + 1) * QB)
        with nc.Block() as block:
            @block.gpsimd
            def _(pool):
                lane = Lane(pool, S.pool_steps, {S.pool_steps: layer * 2 * NB})

                def shifted(b):
                    if b >= 2:
                        pool.wait_ge(S.turned, upto(S.turned, 1, b - 1))
                    shift_copy(nc, lane, L.held, S.xs[:, b % 2, :], L.xb, b * QB, QB, S.xs_ready)
                    pool.wait_ge(S.xs_ready, upto(S.xs_ready, 1, b + 1))
                shifted(0)
                for b in range(NB):
                    if b + 1 < NB:
                        shifted(b + 1)
                    pool.wait_ge(S.stats_ready, upto(S.stats_ready, 1, b + 1))
                    hold(pool, L.held)
                    lane.seq(nc.gpsimd.tensor_scalar(S.rstd[:, b % 2, :], S.meanvar[:, b % 2, :, 1], LN_EPS, None, ALU.add))
                    nc.gpsimd.tensor_tensor(S.rstd[:, b % 2, :], S.rstd[:, b % 2, :], L.minus_half[:, 0:4],
                                            ALU.pow).then_inc(S.rstd_ready, 1)
                    pool.wait_ge(S.rstd_ready, upto(S.rstd_ready, 1, b + 1))

            @block.tensor
            def _(pe):
                def turn(b):
                    pe.wait_ge(S.xs_ready, upto(S.xs_ready, 1, b + 1))
                    if b >= 2:
                        pe.wait_ge(S.xn_ready, upto(S.xn_ready, 1, b - 1))
                    for t in range(4):
                        last = nc.tensor.transpose(bank[:, TURN + b % 2, t * P:(t + 1) * P],
                                                   S.xs[:, b % 2, t * P:(t + 1) * P], g.ident[:])
                    last.then_inc(S.turned, 1)
                turn(0)
                for b in range(NB):
                    if b + 1 < NB:
                        turn(b + 1)
                    pe.wait_ge(S.xn_ready, upto(S.xn_ready, 1, b + 1))
                    for t in range(4):
                        last = nc.tensor.transpose(bank[:, BACK, t * P:(t + 1) * P], S.xn[:, b % 2, t, :], g.ident[:])
                    last.then_inc(S.xn_turned, 1)
                    pe.wait_ge(S.xnT_ready, upto(S.xnT_ready, 1, b + 1))
                    for j, (at, n) in enumerate(FCH):
                        c = NCH * b + j
                        if c >= 2:
                            pe.wait_ge(S.gelu_ready, upto(S.gelu_ready, NCH, c - 1))
                        nc.tensor.matmul(bank[0:n, GATE + c % 2, :], L.w1[:, FI + at:FI + at + n], S.xnT[:],
                                         start=True, stop=True).then_inc(S.gate_ready, 1)
                        if c >= 2:
                            pe.wait_ge(S.h_ready, upto(S.h_ready, NCH, c - 1))
                        nc.tensor.matmul(bank[0:n, AFACT + c % 2, :], L.w1[:, at:at + n], S.xnT[:],
                                         start=True, stop=True).then_inc(S.a_ready, 1)
                    if b:
                        pe.wait_ge(S.y_added, upto(S.y_added, 1, b))
                    for j, (at, n) in enumerate(FCH):
                        pe.wait_ge(S.h_ready, upto(S.h_ready, NCH, NCH * b + j + 1))
                        last = nc.tensor.matmul(bank[:, Y, :], L.w2[0:n, j, :], S.h[0:n, j, :],
                                                start=j == 0, stop=j == NCH - 1)
                    last.then_inc(S.y_ready, 1)

            @block.scalar
            def _(act):
                for b in range(NB):
                    act.wait_ge(S.xn_turned, upto(S.xn_turned, 1, b + 1))
                    if b:
                        act.wait_ge(S.a_ready, upto(S.a_ready, NCH, NCH * b))
                    nc.scalar.activation(S.xnT[:], bank[:, BACK, :], ACT.Identity, bias=L.cols[:, 1:2],
                                         scale=L.cols[:, 0:1]).then_inc(S.xnT_ready, 1)
                    for j, (at, n) in enumerate(FCH):
                        c = NCH * b + j
                        act.wait_ge(S.gate_ready, upto(S.gate_ready, NCH, c + 1))
                        if c >= 2:
                            act.wait_ge(S.h_ready, upto(S.h_ready, NCH, c - 1))
                        nc.scalar.activation(S.gelu[0:n, c % 2, :], bank[0:n, GATE + c % 2, :], ACT.Gelu,
                                             bias=L.cols[0:n, 3 + NCH + j:4 + NCH + j]).then_inc(S.gelu_ready, 1)

            @block.vector
            def _(dve):
                lane = Lane(dve, S.dve_steps, {S.dve_steps: layer * 4 * NB})

                def normalise(b):
                    dve.wait_ge(S.turned, upto(S.turned, 1, b + 1))
                    src = bank[:, TURN + b % 2, :].rearrange("p (t c) -> p t c", c=C)
                    for t in range(4):
                        lane.post(nc.vector.bn_stats(S.stats[:, t, :], src[:, t, :]))
                    lane.settle()
                    hold(dve, L.held)
                    for t in range(4):
                        last = nc.vector.bn_aggr(S.meanvar[:, b % 2, t, :], S.stats[:, t, :])
                    last.then_inc(S.stats_ready, 1)
                    dve.wait_ge(S.stats_ready, upto(S.stats_ready, 1, b + 1))
                    dve.wait_ge(S.rstd_ready, upto(S.rstd_ready, 1, b + 1))
                    if b >= 2:
                        dve.wait_ge(S.xn_turned, upto(S.xn_turned, 1, b - 1))
                    for t in range(4):
                        last = nc.vector.tensor_scalar(S.xn[:, b % 2, t, :], src[:, t, :], S.meanvar[:, b % 2, t, 0:1],
                                                       S.rstd[:, b % 2, t:t + 1], ALU.subtract, ALU.mult)
                    last.then_inc(S.xn_ready, 1)
                normalise(0)
                for b in range(NB):
                    if b + 1 < NB:
                        normalise(b + 1)
                    for j, (at, n) in enumerate(FCH):
                        c = NCH * b + j
                        dve.wait_ge(S.a_ready, upto(S.a_ready, NCH, c + 1))
                        dve.wait_ge(S.gelu_ready, upto(S.gelu_ready, NCH, c + 1))
                        nc.vector.scalar_tensor_tensor(S.h[0:n, j, :], bank[0:n, AFACT + c % 2, :], L.cols[0:n, 3 + j:4 + j],
                                                       S.gelu[0:n, c % 2, :], ALU.add, ALU.mult).then_inc(S.h_ready, 1)
                    dve.wait_ge(S.y_ready, upto(S.y_ready, 1, b + 1))
                    nc.vector.scalar_tensor_tensor(L.xa[:, tokens(b)], bank[:, Y, :], L.cols[:, 2:3], L.xb[:, tokens(b)],
                                                   ALU.add, ALU.add).then_inc(S.y_added, 1)


DI = 256
DT = DI // P
NS = 16
RANK = 8
TAPS = 4
SERIES_BELOW = 0.01


def stage_l2_attn(nc, g, d, y):
    with ExitStack() as ctx:
        def sb(n, shape, dt=fp32):
            return ctx.enter_context(nc.sbuf_tensor(f"l2a_{n}", shape, dt))
        shapes = {"w_in": [C, 4 * P], "w_out": [P, DT, C], "xproj": [P, DT, RANK + 2 * NS], "w_dt": [RANK, DI],
                  "cols": [P, DT, TAPS + 3], "a_log": [P, DT, NS]}
        w = {n: sb(n, s) for n, s in shapes.items()}
        select = sb("select", [NS, NS, P])
        load(nc, "l2a", [(t[:], d["h_l2_" + n]) for n, t in w.items()] + [(select[:], d["c_select16"])])
        xc, zs = sb("xc", [P, DT, T]), sb("zs", [P, DT, T])
        step, dx = sb("step", [P, DT, T]), sb("dx", [P, DT, T])
        bT, cT = sb("bT", [NS, T]), sb("cT", [NS, T])
        ysum = sb("ysum", [P, DT, T])
        scan_inputs(nc, g, w, xc, zs)
        scan_steps(nc, g, w, xc, step, dx, bT, cT)
        scan_states(nc, g, w, select, xc, zs, step, dx, bT, cT, ysum)
    layernorm(nc, g, "ln4", feature=g.delta)


def scan_inputs(nc, g, w, xc, zs):
    with ExitStack() as ctx:
        def sb(n, shape, dt=fp32):
            return ctx.enter_context(nc.sbuf_tensor(f"si_{n}", shape, dt))

        def sem(n):
            return nc.alloc_semaphore(f"si_{n}")
        padded = sb("padded", [P, DT, TAPS - 1 + T])
        conv = sb("conv", [P, DT, T])
        acc = [ctx.enter_context(nc.psum_tensor(f"si_acc{i}", [P, NB, QB], fp32)) for i in range(2)]
        made, taken = sem("made"), sem("taken")
        conv_ready = sem("conv_ready")
        z_taken = sem("z_taken")
        own = sem("dve_steps")
        block = ctx.enter_context(nc.Block())

        def flat(i):
            return acc[i][:, :, :].rearrange("p b q -> p (b q)")

        @block.tensor
        def _(pe):
            for m in range(2 * DT):
                if m >= 2:
                    pe.wait_ge(taken, m - 1)
                for b in range(NB):
                    last = nc.tensor.matmul(acc[m % 2][:, b, :], w["w_in"][:, m * P:(m + 1) * P],
                                            g.xT[:, b * QB:(b + 1) * QB], start=True, stop=True)
                last.then_inc(made, 1)

        @block.vector
        def _(dve):
            lane = Lane(dve, own)
            lane.post(nc.vector.memset(padded[:, :, 0:TAPS - 1], 0.0))
            for m in range(DT):
                dve.wait_ge(made, m + 1)
                nc.vector.tensor_copy(padded[:, m, TAPS - 1:], flat(m)).then_inc(taken, 1)
            dve.wait_ge(taken, DT)
            lane.settle()
            for m in range(DT):
                lane.seq(nc.vector.tensor_scalar(conv[:, m, :], padded[:, m, 0:T], w["cols"][:, m, 0:1], None, ALU.mult))
                for j in range(1, TAPS):
                    ins = nc.vector.scalar_tensor_tensor(conv[:, m, :], padded[:, m, j:j + T], w["cols"][:, m, j:j + 1],
                                                         conv[:, m, :], ALU.mult, ALU.add)
                    if j < TAPS - 1:
                        lane.seq(ins)
                ins.then_inc(conv_ready, 1)

        @block.scalar
        def _(act):
            for m in range(DT):
                act.wait_ge(made, DT + m + 1)
                nc.scalar.activation(zs[:, m, :], flat(m), ACT.Silu)
            for m in range(DT):
                act.wait_ge(conv_ready, m + 1)
                nc.scalar.activation(xc[:, m, :], conv[:, m, :], ACT.Silu, bias=w["cols"][:, m, TAPS:TAPS + 1])


def scan_steps(nc, g, w, xc, step, dx, bT, cT):
    with ExitStack() as ctx:
        def sb(n, shape, dt=fp32):
            return ctx.enter_context(nc.sbuf_tensor(f"ss_{n}", shape, dt))

        def sem(n):
            return nc.alloc_semaphore(f"ss_{n}")
        low = sb("low", [RANK, T])
        raw, ex, one_ex = (sb(n, [P, DT, T]) for n in ("raw", "ex", "one_ex"))
        ps = [ctx.enter_context(nc.psum_tensor(f"ss_ps{i}", [P, NB, QB], fp32)) for i in range(2)]
        made, taken = sem("made"), sem("taken")
        low_ready = sem("low_ready")
        raw_ready, abs_ready, ex_ready, one_ready, ln_ready = (sem(n) for n in ("raw_ready", "abs_ready", "ex_ready", "one_ready", "ln_ready"))
        own = sem("dve_steps")
        block = ctx.enter_context(nc.Block())

        def flat(i, rows=P):
            return ps[i][0:rows, :, :].rearrange("p b q -> p (b q)")

        @block.tensor
        def _(pe):
            for n, (at, rows) in enumerate(((0, RANK), (RANK, NS), (RANK + NS, NS))):
                if n >= 2:
                    pe.wait_ge(taken, n - 1)
                for b in range(NB):
                    for m in range(DT):
                        last = nc.tensor.matmul(ps[n % 2][0:rows, b, :], w["xproj"][:, m, at:at + rows],
                                                xc[:, m, b * QB:(b + 1) * QB], start=m == 0, stop=m == DT - 1)
                last.then_inc(made, 1)
            for m in range(DT):
                pe.wait_ge(taken, 2 + m)
                for b in range(NB):
                    last = nc.tensor.matmul(ps[(m + 1) % 2][:, b, :], w["w_dt"][:, m * P:(m + 1) * P],
                                            low[:, b * QB:(b + 1) * QB], start=True, stop=True)
                last.then_inc(made, 1)

        @block.vector
        def _(dve):
            lane = Lane(dve, own)
            for n, (dst, rows) in enumerate(((low, RANK), (bT, NS), (cT, NS))):
                dve.wait_ge(made, n + 1)
                nc.vector.tensor_copy(dst[:], flat(n % 2, rows)).then_inc(taken, 1)
            for m in range(DT):
                dve.wait_ge(made, 4 + m)
                nc.vector.tensor_scalar(raw[:, m, :], flat((m + 1) % 2), w["cols"][:, m, TAPS + 1:TAPS + 2], None,
                                        ALU.add).then_inc(raw_ready, 1)
            dve.wait_ge(ex_ready, 1)
            lane.post(nc.vector.tensor_scalar(dx[:], ex[:], -0.25, 1.0 / 3.0, ALU.mult, ALU.add))
            nc.vector.tensor_scalar(one_ex[:], ex[:], 1.0, None, ALU.add).then_inc(one_ready, 1)
            lane.settle()
            lane.seq(nc.vector.tensor_tensor(dx[:], dx[:], ex[:], ALU.mult))
            lane.seq(nc.vector.scalar_tensor_tensor(dx[:], dx[:], -0.5, ex[:], ALU.add, ALU.mult))
            lane.seq(nc.vector.scalar_tensor_tensor(dx[:], dx[:], 1.0, ex[:], ALU.add, ALU.mult))
            dve.wait_ge(ln_ready, 1)
            lane.seq(nc.vector.tensor_tensor(dx[:], dx[:], step[:], ALU.subtract))
            lane.seq(nc.vector.scalar_tensor_tensor(dx[:], ex[:], SERIES_BELOW, dx[:], ALU.is_lt, ALU.mult))
            lane.seq(nc.vector.scalar_tensor_tensor(step[:], raw[:], 0.0, step[:], ALU.max, ALU.add))
            lane.seq(nc.vector.tensor_tensor(step[:], step[:], dx[:], ALU.add))
            nc.vector.tensor_tensor(dx[:], step[:], xc[:], ALU.mult)

        @block.scalar
        def _(act):
            act.wait_ge(raw_ready, DT)
            nc.scalar.activation(ex[:], raw[:], ACT.Abs).then_inc(abs_ready, 1)
            act.wait_ge(abs_ready, 1)
            nc.scalar.activation(ex[:], ex[:], ACT.Exp, scale=-1.0).then_inc(ex_ready, 1)
            act.wait_ge(one_ready, 1)
            nc.scalar.activation(step[:], one_ex[:], ACT.Ln).then_inc(ln_ready, 1)


def scan_states(nc, g, w, select, xc, zs, step, dx, bT, cT, ysum):
    with ExitStack() as ctx:
        def sb(n, shape, dt=fp32):
            return ctx.enter_context(nc.sbuf_tensor(f"st_{n}", shape, dt))

        def sem(n):
            return nc.alloc_semaphore(f"st_{n}")
        a = sb("a", [P, DT, NS])
        bn, cn = sb("bn", [P, 2, T]), sb("cn", [P, 2, T])
        decay = sb("decay", [P, 2, T])
        h = g.delta
        hc = sb("hc", [P, 2, T])
        bps = ctx.enter_context(nc.psum_tensor("st_bps", [P, NB, QB], fp32))
        cps = ctx.enter_context(nc.psum_tensor("st_cps", [P, NB, QB], fp32))
        a_exp, a_ready = sem("a_exp"), sem("a_ready")
        spread_ready = sem("spread_ready")
        spread_copied = sem("spread_copied")
        decay_ready = sem("decay_ready")
        scanned = sem("scanned")
        hc_ready = sem("hc_ready")
        added = sem("added")
        y_ready = sem("y_ready")
        out_ready = sem("out_ready")
        own = sem("dve_steps")
        block = ctx.enter_context(nc.Block())

        @block.tensor
        def _(pe):
            for n in range(NS):
                for i, (ps, src) in enumerate(((bps, bT), (cps, cT))):
                    if n:
                        pe.wait_ge(spread_copied, 2 * n - 1 + i)
                    for b in range(NB):
                        last = nc.tensor.matmul(ps[:, b, :], select[:, n, :], src[:, b * QB:(b + 1) * QB],
                                                start=True, stop=True)
                    last.then_inc(spread_ready, 1)
            pe.wait_ge(y_ready, DT)
            pe.wait_ge(spread_copied, 2 * NS)
            for b in range(NB):
                for m in range(DT):
                    last = nc.tensor.matmul(bps[:, b, :], w["w_out"][:, m, :], ysum[:, m, b * QB:(b + 1) * QB],
                                            start=m == 0, stop=m == DT - 1)
            last.then_inc(out_ready, 1)

        @block.scalar
        def _(act):
            nc.scalar.activation(a[:], w["a_log"][:], ACT.Exp).then_inc(a_exp, 1)
            act.wait_ge(a_ready, 1)
            for n in range(NS):
                for i, (ps, dst) in enumerate(((bps, bn), (cps, cn))):
                    act.wait_ge(spread_ready, 2 * n + i + 1)
                    if n >= 2:
                        act.wait_ge(hc_ready, DT * (n - 1))
                    nc.scalar.copy(dst[:, n % 2, :], ps[:, :, :].rearrange("p b q -> p (b q)")).then_inc(spread_copied, 1)
                for m in range(DT):
                    k = DT * n + m
                    if k >= 2:
                        act.wait_ge(scanned, k - 1)
                    nc.scalar.activation(decay[:, k % 2, :], step[:, m, :], ACT.Exp,
                                         scale=a[:, m, n:n + 1]).then_inc(decay_ready, 1)

        @block.vector
        def _(dve):
            lane = Lane(dve, own)
            dve.wait_ge(a_exp, 1)
            nc.vector.tensor_scalar(a[:], a[:], -1.0, None, ALU.mult).then_inc(a_ready, 1)
            for n in range(NS):
                dve.wait_ge(spread_copied, 2 * n + 2)
                for m in range(DT):
                    k = DT * n + m
                    if k >= 2:
                        dve.wait_ge(added, k - 1)
                    lane.seq(nc.vector.tensor_tensor(hc[:, k % 2, :], dx[:, m, :], bn[:, n % 2, :], ALU.mult))
                    dve.wait_ge(decay_ready, k + 1)
                    if k:
                        dve.wait_ge(hc_ready, k)
                    nc.vector.tensor_tensor_scan(h[:], decay[:, k % 2, :], hc[:, k % 2, :], 0.0,
                                                 ALU.mult, ALU.add).then_inc(scanned, 1)
                    dve.wait_ge(scanned, k + 1)
                    nc.vector.tensor_tensor(hc[:, k % 2, :], h[:], cn[:, n % 2, :], ALU.mult).then_inc(hc_ready, 1)
            dve.wait_ge(added, DT * NS)
            for m in range(DT):
                lane.seq(nc.vector.scalar_tensor_tensor(ysum[:, m, :], xc[:, m, :], w["cols"][:, m, TAPS + 2:TAPS + 3],
                                                        ysum[:, m, :], ALU.mult, ALU.add))
                nc.vector.tensor_tensor(ysum[:, m, :], ysum[:, m, :], zs[:, m, :], ALU.mult).then_inc(y_ready, 1)
            dve.wait_ge(out_ready, 1)
            nc.vector.tensor_copy(g.delta[:], bps[:, :, :].rearrange("p b q -> p (b q)"))

        @block.gpsimd
        def _(pool):
            for k in range(DT * NS):
                m = k % DT
                pool.wait_ge(hc_ready, k + 1)
                if k < DT:
                    nc.gpsimd.tensor_copy(ysum[:, m, :], hc[:, k % 2, :]).then_inc(added, 1)
                else:
                    pool.wait_ge(added, k - 1)
                    nc.gpsimd.tensor_tensor(ysum[:, m, :], hc[:, k % 2, :], ysum[:, m, :], ALU.add).then_inc(added, 1)


def stage_l2_ffn(nc, g, d, y):
    with ExitStack() as ctx:
        def sb(n, shape, dt=fp32):
            return ctx.enter_context(nc.sbuf_tensor(f"l2f_{n}", shape, dt))

        def sem(n):
            return nc.alloc_semaphore(f"l2f_{n}")
        w = {n: sb(n, [P, P]) for n in ("rT", "kT", "vT")}
        mu = sb("mu", [P, 4])
        load(nc, "l2f", [(t[:], d["h_l2f_" + n]) for n, t in w.items()] + [(mu[:, 0:2], d["h_l2f_mu"])])
        mixed = sb("mixed", [P, 2, T])
        r = sb("r", [P, T])
        k = sb("k", [P, NB, QB])
        ps = ctx.enter_context(nc.psum_tensor("l2f_ps", [P, 2, NB, QB], fp32))
        mixed_ready = sem("mixed_ready")
        made, v_made = sem("made"), sem("v_made")
        sig, k_sq = sem("sig"), sem("k_sq")
        own, act_own = sem("dve_steps"), sem("act_steps")
        with nc.Block() as block:
            @block.vector
            def _(dve):
                lane = Lane(dve, own)
                lane.seq(nc.vector.tensor_scalar(mu[:, 2:4], mu[:, 0:2], -1.0, 1.0, ALU.mult, ALU.add))
                for i in range(2):
                    lane.seq(nc.vector.tensor_scalar(mixed[:, i, :], g.xT[:], mu[:, i:i + 1], None, ALU.mult))
                    nc.vector.scalar_tensor_tensor(mixed[:, i, 1:T], g.xT[:, 0:T - 1], mu[:, 2 + i:3 + i],
                                                   mixed[:, i, 1:T], ALU.mult, ALU.add).then_inc(mixed_ready, 1)
                for b in range(NB):
                    dve.wait_ge(v_made, b + 1)
                    s = slice(b * QB, (b + 1) * QB)
                    nc.vector.tensor_tensor(g.delta[:, s], ps[:, 1, b, :], r[:, s], ALU.mult)

            @block.tensor
            def _(pe):
                for i, n in enumerate(("rT", "kT")):
                    pe.wait_ge(mixed_ready, i + 1)
                    for b in range(NB):
                        nc.tensor.matmul(ps[:, i, b, :], w[n][:], mixed[:, i, b * QB:(b + 1) * QB],
                                         start=True, stop=True).then_inc(made, 1)
                for b in range(NB):
                    pe.wait_ge(k_sq, b + 1)
                    nc.tensor.matmul(ps[:, 1, b, :], w["vT"][:], k[:, b, :], start=True, stop=True).then_inc(v_made, 1)

            @block.scalar
            def _(act):
                act.wait_ge(made, NB)
                nc.scalar.activation(r[:], ps[:, 0].rearrange("p b q -> p (b q)"), ACT.Sigmoid).then_inc(act_own, 1)
                for b in range(NB):
                    act.wait_ge(made, NB + b + 1)
                    nc.scalar.activation(k[:, b, :], ps[:, 1, b, :], ACT.Relu).then_inc(act_own, 1)
                    act.wait_ge(act_own, b + 2)
                    nc.scalar.activation(k[:, b, :], k[:, b, :], ACT.Square).then_inc(k_sq, 1)
    layernorm(nc, g, "ln5", feature=g.delta)


HI = 352
HT = 3
FP4_BLOCK = 16


def quantise(nc, lane, x, out, scale, inv, a, hi, absolute, absolute_ready, sign, sign_ready, n):
    lane.eng.wait_ge(absolute_ready, n)
    lane.seq(nc.vector.reduce_max(scale, absolute, axis=AX.X))
    lane.seq(nc.vector.tensor_scalar(scale, scale, 1.0 / 6.0, 1e-12, ALU.mult, ALU.max))
    lane.seq(nc.vector.reciprocal(inv, scale))
    lane.seq(nc.vector.tensor_tensor(a, absolute, spread(inv, FP4_BLOCK), ALU.mult))
    lane.post(nc.vector.tensor_scalar(hi, a, 5.0, 2.0, ALU.is_gt, ALU.mult))
    lane.seq(nc.vector.tensor_scalar(out, a, 0.25, None, ALU.is_gt))
    for high, low in ((3.5, 0.75), (2.5, 1.25)):
        lane.post(nc.vector.scalar_tensor_tensor(hi, a, high, hi, ALU.is_gt, ALU.add))
        lane.seq(nc.vector.scalar_tensor_tensor(out, a, low, out, ALU.is_gt, ALU.add))
    lane.seq(nc.vector.scalar_tensor_tensor(out, a, 1.75, out, ALU.is_gt, ALU.add))
    lane.seq(nc.vector.scalar_tensor_tensor(out, hi, 2.0, out, ALU.mult, ALU.add))
    lane.post(nc.vector.tensor_scalar(scale, scale, 0.5, None, ALU.mult))
    lane.eng.wait_ge(sign_ready, n)
    lane.seq(nc.vector.tensor_tensor(out, out, sign, ALU.mult))
    return nc.vector.tensor_tensor(out, out, spread(scale, FP4_BLOCK), ALU.mult)


def stage_l3_ffn(nc, g, d, y):
    with ExitStack() as ctx:
        def sb(n, shape, dt=fp32):
            return ctx.enter_context(nc.sbuf_tensor(f"l3f_{n}", shape, dt))
        WC = 2 * HT * C + HI
        raw = sb("raw", [P, WC + NT * C])
        out = sb("out", [P, WC + NT * C])
        load(nc, "l3f", [(raw[:, 0:WC], d["h_l3f_w"])])
        wT = sb("wT", [P, 2 * HT, P])
        wdT = sb("wdT", [P, HT, C])
        xqT = sb("xqT", [C, T])
        quantise_inputs(nc, g, raw, out, WC, wT, wdT, xqT)
        gated_ffn(nc, g, wT, wdT, xqT)
    layernorm(nc, g, "ln7", token=g.delta[:].rearrange("p (t c) -> p t c", c=C), out_dram=y)


def quantise_inputs(nc, g, raw, out, WC, wT, wdT, xqT):
    with ExitStack() as ctx:
        def sb(n, shape, dt=fp32):
            return ctx.enter_context(nc.sbuf_tensor(f"qi_{n}", shape, dt))

        def sem(n):
            return nc.alloc_semaphore(f"qi_{n}")
        total = WC + NT * C
        absolute, a, hi, sign = (sb(n, [P, total]) for n in ("absolute", "a", "hi", "sign"))
        scale, inv = sb("scale", [P, total // FP4_BLOCK]), sb("inv", [P, total // FP4_BLOCK])
        wps = ctx.enter_context(nc.psum_tensor("qi_wps", [P, 4, QB], fp32))
        xps = ctx.enter_context(nc.psum_tensor("qi_xps", [P, 4, QB], fp32))
        x_copied, absolute_ready, sign_ready, done = (sem(n) for n in ("x_copied", "absolute_ready", "sign_ready", "done"))
        turned, own, copied = sem("turned"), sem("dve_steps"), sem("copied")
        block = ctx.enter_context(nc.Block())

        def blocks(t):
            return t[:].rearrange("p (b k) -> p b k", k=FP4_BLOCK)

        @block.vector
        def _(dve):
            lane = Lane(dve, own)
            nc.vector.tensor_copy(raw[:, WC:], g.x[:].rearrange("p t c -> p (t c)")).then_inc(x_copied, 1)
            quantise(nc, lane, blocks(raw), blocks(out), scale[:], inv[:], blocks(a), blocks(hi),
                     blocks(absolute), absolute_ready, blocks(sign), sign_ready, 1).then_inc(done, 1)
            dve.wait_ge(turned, 1)
            nc.vector.tensor_copy(wT[:, 0:3, :], wps[:, 0, 0:3 * P].rearrange("p (t c) -> p t c", c=P))
            nc.vector.tensor_copy(wT[:, 3:6, :], wps[:, 1, 0:3 * P].rearrange("p (t c) -> p t c", c=P))
            nc.vector.tensor_copy(wdT[:, 0:2, :], wps[:, 2, 0:2 * P].rearrange("p (t c) -> p t c", c=P))
            nc.vector.tensor_copy(wdT[0:HI - 2 * P, 2, :], wps[0:HI - 2 * P, 2, 2 * P:3 * P])

        @block.scalar
        def _(act):
            act.wait_ge(x_copied, 1)
            nc.scalar.activation(absolute[:], raw[:], ACT.Abs).then_inc(absolute_ready, 1)
            nc.scalar.activation(sign[:], raw[:], ACT.Sign).then_inc(sign_ready, 1)
            act.wait_ge(turned, 2)
            nc.scalar.copy(xqT[:], xps[:, :, :].rearrange("p b q -> p (b q)"))

        @block.tensor
        def _(pe):
            pe.wait_ge(done, 1)
            for i in range(2):
                for t in range(HT):
                    nc.tensor.transpose(wps[:, i, t * P:(t + 1) * P], out[:, (i * HT + t) * C:(i * HT + t + 1) * C], g.ident[:])
            for t in range(HT):
                rows = min(P, HI - t * P)
                at = 2 * HT * C + t * P
                last = nc.tensor.transpose(wps[0:rows, 2, t * P:(t + 1) * P], out[:, at:at + rows], g.ident[:])
            last.then_inc(turned, 1)
            for t in range(NT):
                last = nc.tensor.transpose(xps[:, t // 4, (t % 4) * P:(t % 4 + 1) * P], out[:, WC + t * C:WC + (t + 1) * C], g.ident[:])
            last.then_inc(turned, 1)


def gated_ffn(nc, g, wT, wdT, xqT):
    with ExitStack() as ctx:
        def sb(n, shape, dt=fp32):
            return ctx.enter_context(nc.sbuf_tensor(f"gf_{n}", shape, dt))

        def sem(n):
            return nc.alloc_semaphore(f"gf_{n}")
        G = 4
        W = G * HI
        silu = sb("silu", [P, HI])
        h = sb("h", [P, 2, W])
        out = sb("out", [P, 2, W])
        absolute, sign = sb("absolute", [P, 2, W]), sb("sign", [P, 2, W])
        a, hi = sb("a", [P, W]), sb("hi", [P, W])
        scale, inv = sb("scale", [P, W // FP4_BLOCK]), sb("inv", [P, W // FP4_BLOCK])
        hT = sb("hT", [P, 2, HT, P])
        gate_ps = ctx.enter_context(nc.psum_tensor("gf_gate", [P, 2, QB], fp32))
        up_ps = ctx.enter_context(nc.psum_tensor("gf_up", [P, 2, QB], fp32))
        hT_ps = ctx.enter_context(nc.psum_tensor("gf_hT_bank", [P, 2, QB], fp32))
        y_ps = ctx.enter_context(nc.psum_tensor("gf_y", [P, 2, QB], fp32))
        made = sem("made")
        silu_ready = sem("silu_ready")
        h_ready = sem("h_ready")
        absolute_ready, sign_ready = sem("absolute_ready"), sem("sign_ready")
        quantised = sem("quantised")
        turned = sem("turned")
        hT_copied = sem("hT_copied")
        y_made = sem("y_made")
        y_copied = sem("y_copied")
        own, own_act = sem("dve_steps"), sem("act_steps")
        block = ctx.enter_context(nc.Block())
        groups = NT // G

        def blocks(t):
            return t.rearrange("p (b k) -> p b k", k=FP4_BLOCK)

        @block.tensor
        def _(pe):
            def up(k):
                for t in range(k * G, (k + 1) * G):
                    if t >= 2:
                        pe.wait_ge(h_ready, t - 1)
                    s = slice(t * P, (t + 1) * P)
                    nc.tensor.matmul(gate_ps[:, t % 2, 0:HI], xqT[:, s], wT[:, 0:3, :].rearrange("p t c -> p (t c)")[:, 0:HI],
                                     start=True, stop=True)
                    nc.tensor.matmul(up_ps[:, t % 2, 0:HI], xqT[:, s], wT[:, 3:6, :].rearrange("p t c -> p (t c)")[:, 0:HI],
                                     start=True, stop=True).then_inc(made, 1)

            def down(k):
                pe.wait_ge(quantised, k + 1)
                for t in range(k * G, (k + 1) * G):
                    at = (t % G) * HI
                    if t >= 2:
                        pe.wait_ge(hT_copied, t - 1)
                    for j in range(HT):
                        rows = min(P, HI - j * P)
                        last = nc.tensor.transpose(hT_ps[0:rows, t % 2, j * P:(j + 1) * P],
                                                   out[:, k % 2, at + j * P:at + j * P + rows], g.ident[:])
                    last.then_inc(turned, 1)
                    pe.wait_ge(hT_copied, t + 1)
                    if t >= 2:
                        pe.wait_ge(y_copied, t - 1)
                    for j in range(HT):
                        rows = min(P, HI - j * P)
                        last = nc.tensor.matmul(y_ps[:, t % 2, 0:C], hT[0:rows, t % 2, j, :], wdT[0:rows, j, :],
                                                start=j == 0, stop=j == HT - 1)
                    last.then_inc(y_made, 1)
            up(0)
            for k in range(groups):
                if k + 1 < groups:
                    up(k + 1)
                down(k)

        @block.scalar
        def _(act):
            def silus(k):
                for t in range(k * G, (k + 1) * G):
                    act.wait_ge(made, t + 1)
                    if t >= 1:
                        act.wait_ge(h_ready, t)
                    nc.scalar.activation(silu[:], gate_ps[:, t % 2, 0:HI], ACT.Silu).then_inc(silu_ready, 1)
                act.wait_ge(h_ready, (k + 1) * G)
                if k >= 2:
                    act.wait_ge(quantised, k - 1)
                nc.scalar.activation(absolute[:, k % 2, :], h[:, k % 2, :], ACT.Abs).then_inc(absolute_ready, 1)
                nc.scalar.activation(sign[:, k % 2, :], h[:, k % 2, :], ACT.Sign).then_inc(sign_ready, 1)

            def copies(k):
                for t in range(k * G, (k + 1) * G):
                    act.wait_ge(turned, t + 1)
                    nc.scalar.copy(hT[:, t % 2, 0:2, :], hT_ps[:, t % 2, 0:2 * P].rearrange("p (t c) -> p t c", c=P)).then_inc(own_act, 1)
                    nc.scalar.copy(hT[0:HI - 2 * P, t % 2, 2, :], hT_ps[0:HI - 2 * P, t % 2, 2 * P:3 * P]).then_inc(hT_copied, 1)
                    act.wait_ge(y_made, t + 1)
                    nc.scalar.copy(g.delta[:, t * C:(t + 1) * C], y_ps[:, t % 2, 0:C]).then_inc(y_copied, 1)
            silus(0)
            for k in range(groups):
                if k + 1 < groups:
                    silus(k + 1)
                copies(k)

        @block.vector
        def _(dve):
            lane = Lane(dve, own)

            def products(k):
                for t in range(k * G, (k + 1) * G):
                    dve.wait_ge(silu_ready, t + 1)
                    at = (t % G) * HI
                    nc.vector.tensor_tensor(h[:, k % 2, at:at + HI], up_ps[:, t % 2, 0:HI], silu[:], ALU.mult).then_inc(h_ready, 1)

            def quantised_group(k):
                quantise(nc, lane, None, blocks(out[:, k % 2, :]), scale[:], inv[:], blocks(a[:]), blocks(hi[:]),
                         blocks(absolute[:, k % 2, :]), absolute_ready, blocks(sign[:, k % 2, :]), sign_ready,
                         k + 1).then_inc(quantised, 1)
                dve.wait_ge(quantised, k + 1)
            products(0)
            for k in range(groups):
                if k + 1 < groups:
                    products(k + 1)
                if k >= 2:
                    dve.wait_ge(turned, G * (k - 1))
                quantised_group(k)


KEY_SCALE_MAX = float(np.log(2 ** 16 - 1))
PER_OWN = {"l3": 0}
HEAD_STEPS = {"l0": 22, "l1": 12}


class Shared:
    pass


def load(nc, name, pairs):
    loaded = nc.alloc_semaphore(f"{name}_loaded")
    with nc.Block() as block:
        half = (len(pairs) + 1) // 2

        @block.sync
        def _(sp):
            for dst, src in pairs[:half]:
                sp.dma_start(dst, src).then_inc(loaded, 16)
            sp.wait_ge(loaded, 16 * len(pairs))

        @block.scalar
        def _(act):
            for dst, src in pairs[half:]:
                act.dma_start(dst, src).then_inc(loaded, 16)


def build(nc, d, y, dbg=None, upto=99, only=None):
    ctx = ExitStack()
    with ctx:
        g = Shared()
        def keep(n, shape, dt=fp32):
            return ctx.enter_context(nc.sbuf_tensor(n, shape, dt))
        g.x = keep("x", [P, NT, C])
        g.xT = keep("xT", [C, T])
        g.delta = keep("delta", [P, T])
        consts = {"ident": [P, P], "ones": [P, P], "e012": [P, 1], "head_ones": [P, P],
                  "mask_strict_q": [P, P], "mask_strict_k": [P, P], "mask_q": [P, P], "mask_k": [P, P]}
        consts = {n: keep(n, shape) for n, shape in consts.items()}
        g.ident, g.ones, g.e012, g.head_ones = (consts[n] for n in ("ident", "ones", "e012", "head_ones"))
        g.mask_strict_q, g.mask_strict_k = consts["mask_strict_q"], consts["mask_strict_k"]
        g.mask_q, g.mask_k = consts["mask_q"], consts["mask_k"]
        load(nc, "consts", [(t[:], d["c_" + n]) for n, t in consts.items()]
             + [(g.x[:], d["L0_attn_x"].rearrange("b (t p) c -> p (b t) c", p=P)),
                (g.xT[:], d["h_xT"])])
        stages = [stage_l0_attn, stage_l0_ffn, stage_l1_attn, stage_l1_ffn,
                  stage_l2_attn, stage_l2_ffn, stage_l3_attn, stage_l3_ffn]
        for n, s in enumerate(stages):
            if n > upto or (only is not None and n != only):
                continue
            with nc.cleanup_on_exit():
                s(nc, g, d, y if n == 7 else None)
            nc.all_engine_barrier()
            if dbg is not None and (n == upto or n == only) and n < 7:
                load(nc, "debug", [(dbg.rearrange("(t p) c -> p t c", p=P), g.x[:])])


def stage_l0_attn(nc, g, d, y):
    with ExitStack() as ctx:
        def sb(n, shape, dt=fp32):
            return ctx.enter_context(nc.sbuf_tensor(f"l0a_{n}", shape, dt))
        names = {"kT": [P, P], "vT": [P, P], "beta": [P, 1], "key_scale": [P, 1], "v_coef": [P, 1], "val_scale": [P, 1]}
        w = {n: sb(n, shape) for n, shape in names.items()}
        wo = sb("wo", [8, 16, C])
        groups, head_mask = sb("groups", [P, 6, P]), sb("head_mask", [P, 16, 1])
        load(nc, "l0a", [(t[:], d["h_l0_" + n]) for n, t in w.items()]
             + [(wo[:], d["h_l0_wo"]), (groups[:], d["c_groups"]), (head_mask[:, :, 0], d["c_head_mask"])])
        hi, mid, lo = (sb(n, [P, T], bf16) for n in ("hi", "mid", "lo"))
        v_all = sb("v_all", [P, NT, 16, 8])
        zero(nc, "l0a", g.delta)
        with ExitStack() as ctx2:
            keys = ctx2.enter_context(nc.sbuf_tensor("l0a_keys", [C, T], fp32))
            values = ctx2.enter_context(nc.sbuf_tensor("l0a_values", [C, T], fp32))
            decayed_keys(nc, g, {n: t[:] for n, t in w.items()}, keys, values)
            split_keys(nc, g, "l0s", keys, values, hi, mid, lo, v_all[:, :, :, :].rearrange("p t h d -> p t (h d)"))
        head_attention(nc, g, "l0", 16, 8, 1.0, g.delta, wo, picked=(hi, mid, lo, v_all, groups, head_mask))
    layernorm(nc, g, "ln0", feature=g.delta)


def zero(nc, name, t):
    with nc.Block() as block:
        @block.gpsimd
        def _(pool):
            nc.gpsimd.memset(t[:], 0.0)


def stage_l1_attn(nc, g, d, y):
    with ExitStack() as ctx:
        def sb(n, shape, dt=fp32):
            return ctx.enter_context(nc.sbuf_tensor(f"l1a_{n}", shape, dt))
        w = sb("w", [P, 16, 320])
        wo = sb("wo", [64, 16, C])
        bias = sb("bias", [P, 1])
        cos, sin = sb("cos", [P, T]), sb("sin", [P, T])
        load(nc, "l1a", [(w[:], d["h_l1_w"]), (wo[:], d["h_l1_wo"]), (bias[:], d["h_l1_bo"]),
                         (cos[:], d["c_cos"]), (sin[:], d["c_sin"])])
        with nc.Block() as block:
            @block.vector
            def _(dve):
                nc.vector.tensor_copy(g.delta[:], bias[:, 0:1].to_broadcast([P, T]))
        head_attention(nc, g, "l1", 16, 64, 64 ** -0.5, g.delta, wo, rotary=(w, cos, sin))
    layernorm(nc, g, "ln2", feature=g.delta)


def stage_l3_attn(nc, g, d, y):
    with ExitStack() as ctx:
        w = ctx.enter_context(nc.sbuf_tensor("l3a_w", [P, 1, 3 * P], fp32))
        load(nc, "l3a", [(w[:, 0, :], d["h_l3_w"])])
        attention(nc, g, "l3", 1, 128, g.xT, g.xT, w, None, 128 ** -0.5, g.delta, causal="upto")
    layernorm(nc, g, "ln6", feature=g.delta)




def constants():
    f = np.float32
    c = {}
    i = np.arange(P)
    c["ident"] = np.eye(P, dtype=f)
    c["ones"] = np.ones((P, P), f)
    c["e012"] = (i[:, None] < 3).astype(f)
    c["head_ones"] = (i[:, None] // 8 == i[None, :] // 8).astype(f)
    c["mask_strict_q"] = np.where(i[None, :] >= i[:, None], MASKED, 0).astype(f)
    c["mask_strict_k"] = np.ascontiguousarray(c["mask_strict_q"].T)
    c["mask_q"] = np.where(i[None, :] > i[:, None], MASKED, 0).astype(f)
    c["mask_k"] = np.ascontiguousarray(c["mask_q"].T)
    groups = np.zeros((P, 6, P), f)
    for n, (q, k) in enumerate(((0, 0), (0, 1), (1, 0), (1, 1), (0, 2), (2, 0))):
        for p in range(P):
            groups[p, q, 32 + 8 * n + p % 8] = 1
            groups[p, 3 + k, 32 + 8 * n + p % 8] = 1
    c["groups"] = groups
    c["head_mask"] = (i[:, None] // 8 == np.arange(16)[None, :]).astype(f)
    c["select16"] = np.repeat(np.eye(16, dtype=f)[:, :, None], P, axis=2)
    c["select8"] = np.repeat(np.eye(8, dtype=f)[:, :, None], P, axis=2)
    half = np.arange(32, dtype=f)
    theta = (f(1.0) / f(10000.0) ** (half / f(32))).astype(f)
    ang = (np.arange(T, dtype=f)[:, None] * theta[None, :]).astype(f)
    cos, sin = np.cos(ang).T.astype(f), np.sin(ang).T.astype(f)
    c["cos"] = np.concatenate([cos, cos, cos, cos])
    c["sin"] = np.concatenate([-sin, sin, -sin, sin])
    even = np.arange(0, LD, 2, dtype=f)
    ang = np.arange(T, dtype=f)[:, None] * (f(1.0) / f(10000.0) ** (even / f(LD)))[None, :]
    cos, sin = np.cos(ang.astype(f)).astype(np.float64), np.sin(ang.astype(f)).astype(np.float64)
    base = (even.astype(np.float64) + 0.4 * LD) / (1.4 * LD)
    power = (np.arange(T) % P)[:, None] / (WIN // 2)
    up, down = base[None, :] ** power, base[None, :] ** -power
    tabs = np.stack([np.concatenate([cos * up, cos * up], 1), np.concatenate([-sin * up, sin * up], 1),
                     np.concatenate([cos * down, cos * down], 1), np.concatenate([-sin * down, sin * down], 1)], axis=1)
    c["rope"] = tabs.reshape(NT, P, 4, LD).transpose(1, 0, 2, 3).astype(f)
    c["halo_scale"] = np.tile(base ** (P / (WIN // 2)), 4)[:, None].astype(f)
    key = np.arange(SPAN)
    seen = (key[None, :] >= i[:, None]) & (key[None, :] <= i[:, None] + WIN)
    c["band"] = np.stack([np.where(seen, 0, MASKED), np.where(seen & (key[None, :] >= WIN), 0, MASKED)], axis=1).astype(f)
    return c


def layouts(a):
    h = {}
    def col(v):
        return np.ascontiguousarray(v.reshape(-1, 1))
    x = a["L0_attn_x"]
    h["xT"] = np.ascontiguousarray(x[0].T)
    h["l0_kT"] = np.ascontiguousarray(a["L0_attn_W_k"].T)
    h["l0_vT"] = np.ascontiguousarray(a["L0_attn_W_v"].T)
    for n, k in (("beta", "leaky_key_beta"), ("key_scale", "key_scale"), ("v_coef", "v_coef"), ("val_scale", "val_scale")):
        h["l0_" + n] = col(np.repeat(a["L0_attn_" + k].reshape(16), 8))
    h["l0_wo"] = a["L0_attn_W_c"].T.reshape(16, 8, C).transpose(1, 0, 2)
    h["l0_bs"] = np.broadcast_to(a["L0_ffn_bs"], (P, NT, E_))
    h["l0_experts"] = np.concatenate([
        a["L0_ffn_W1"],
        a["L0_ffn_W2"].reshape(E_, FT, P, C).transpose(0, 2, 1, 3).reshape(E_, P, FT * C),
        a["L0_ffn_b1"].reshape(E_, FT, P).transpose(0, 2, 1),
        a["L0_ffn_b2"][:, :, None]], axis=2)
    swap = np.concatenate([np.arange(32, 64), np.arange(32)])
    def feature_tiles(v):
        return v.reshape(DT, P, -1).transpose(1, 0, 2)
    h["l2_w_in"] = a["L2_attn_W_in"]
    h["l2_w_out"] = feature_tiles(a["L2_attn_W_out"])
    h["l2_xproj"] = feature_tiles(a["L2_attn_W_xproj"])
    h["l2_w_dt"] = a["L2_attn_W_dt"]
    h["l2_a_log"] = feature_tiles(a["L2_attn_A_log"])
    h["l2_cols"] = np.concatenate([feature_tiles(a["L2_attn_W_conv"]), feature_tiles(a["L2_attn_b_conv"]),
                                   feature_tiles(a["L2_attn_b_dt"]), feature_tiles(a["L2_attn_D"])], axis=2)
    for n in "rkv":
        h[f"l2f_{n}T"] = a["L2_ffn_W_" + n].T
    h["l2f_mu"] = np.stack([a["L2_ffn_mu_r"], a["L2_ffn_mu_k"]], axis=1)
    h["lw_wo"] = a["L1_ffn_Wo"].reshape(DEPTH, INNER // P, P, C).transpose(0, 2, 1, 3)
    w2 = a["L1_ffn_W2"]
    w2 = np.concatenate([w2, np.zeros((DEPTH, len(FCH) * P - FI, C), w2.dtype)], axis=1)
    h["lw_w2"] = w2.reshape(DEPTH, len(FCH), P, C).transpose(0, 2, 1, 3)
    qs, ks = a["L1_ffn_q_scale"], a["L1_ffn_k_scale"]
    s4 = np.stack([qs, qs[:, swap], ks, ks[:, swap]], axis=1)
    h["lw_scales"] = np.broadcast_to(s4[:, None], (DEPTH, P, 4, LD))
    b1 = a["L1_ffn_b1"]
    pad = np.zeros((DEPTH, len(FCH) * P - FI), b1.dtype)
    b1 = np.concatenate([b1[:, :FI], pad, b1[:, FI:], pad], axis=1).reshape(DEPTH, 2 * len(FCH), P).transpose(0, 2, 1)
    h["lw_cols"] = np.concatenate([a["L1_ffn_ln_g"][:, :, None], a["L1_ffn_ln_b"][:, :, None],
                                   a["L1_ffn_b2"][:, :, None], b1], axis=2)
    rows = []
    for n in ("w_gate", "w_up"):
        v = a["L3_ffn_" + n]
        v = np.concatenate([v, np.zeros((HT * P - HI, C), v.dtype)])
        rows.append(v.reshape(HT, P, C).transpose(1, 0, 2).reshape(P, HT * C))
    h["l3f_w"] = np.concatenate(rows + [a["L3_ffn_w_down"]], axis=1)
    w = a["L1_attn_w_qkv"].reshape(C, 3, 16, 64)
    q, k, v = w[:, 0], w[:, 1], w[:, 2]
    h["l1_w"] = np.concatenate([q, q[:, :, swap], k, k[:, :, swap], v], axis=2)
    h["l1_wo"] = a["L1_attn_w_out"].reshape(16, 64, C).transpose(1, 0, 2)
    h["l1_bo"] = col(a["L1_attn_b_out"])
    h["l3_w"] = np.concatenate([a["L3_attn_W_Q"], a["L3_attn_W_K"], a["L3_attn_W_V"]], axis=1)
    return h




def kernel(**inputs):
    import concourse.bacc as bacc
    from concourse.bass_utils import run_bass_kernel_spmd

    a = {n: np.asarray(v) for n, v in inputs.items()}
    arrays = {"h_" + n: v for n, v in layouts(a).items()}
    arrays |= {"c_" + n: v for n, v in constants().items()}
    arrays |= {n: a[n] for n in ("L0_attn_x", "L0_ffn_Ws", "L1_ffn_Wqkv", "L1_ffn_W1")}
    arrays = {n: np.ascontiguousarray(v) for n, v in arrays.items()}
    nc = bacc.Bacc("TRN2", target_bir_lowering=False, num_devices=1)
    d = {n: nc.dram_tensor(n, v.shape, mybir.dt.from_np(v.dtype), kind="ExternalInput").ap() for n, v in arrays.items()}
    y = nc.dram_tensor("y", (T, C), fp32, kind="ExternalOutput").ap()
    build(nc, d, y)
    got = run_bass_kernel_spmd(nc, [arrays], core_ids=[0])
    return got.results[0]["y"].reshape(1, T, C)
```

```python
import numpy as np
import concourse.bass as bass
from concourse import mybir
from contextlib import ExitStack, contextmanager

fp32 = mybir.dt.float32
bf16 = mybir.dt.bfloat16
ALU = mybir.AluOpType
ACT = mybir.ActivationFunctionType
AX = mybir.AxisListType

T = 2048
C = 128
P = 128
NT = T // P
QB = 512
NB = T // QB
LN_EPS = 1e-5
MASKED = -1e30


class Lane:

    def __init__(self, eng, own, base=None):
        self.eng, self.own = eng, own
        self.seen, self.base = {}, dict(base or {})

    def wait(self, sem, by=1):
        self.seen[sem] = self.seen.get(sem, 0) + by
        self.eng.wait_ge(sem, self.base.get(sem, 0) + self.seen[sem])

    def skip(self, sem, by):
        self.seen[sem] = self.seen.get(sem, 0) + by

    def ahead(self, sem, by):
        self.eng.wait_ge(sem, self.base.get(sem, 0) + self.seen.get(sem, 0) + by)

    def post(self, ins):
        ins.then_inc(self.own, 1)
        self.seen[self.own] = self.seen.get(self.own, 0) + 1

    def settle(self):
        self.eng.wait_ge(self.own, self.base.get(self.own, 0) + self.seen[self.own])

    def seq(self, ins):
        self.post(ins)
        self.settle()

    @contextmanager
    def loop(self, count, per):
        before, outer = dict(self.seen), dict(self.base)
        with self.eng.Fori(0, count) as i:
            for sem, by in per.items():
                self.base[sem] = outer.get(sem, 0) + i * by
            yield i
            added = {s: n - before.get(s, 0) for s, n in self.seen.items() if n != before.get(s, 0)}
            assert added == {s: per.get(s, 0) for s in added}, \
                ("per pass", {s.name: n for s, n in added.items()}, {s.name: n for s, n in per.items()})
        self.base = outer
        self.seen = {s: before.get(s, 0) + count * per.get(s, 0) for s in self.seen}


class Ring:

    def __init__(self, nc, ctx, banks, name):
        self.buf = ctx.enter_context(nc.psum_tensor(f"{name}_bank", [P, banks, QB], fp32))
        self.filled = nc.alloc_semaphore(f"{name}_filled")
        self.freed = nc.alloc_semaphore(f"{name}_freed")
        self.banks = banks

    def writer(self, lane):
        return RingEnd(self, lane, self.freed)

    def reader(self, lane):
        lane.eng.sem_inc(self.freed, self.banks)
        lane.seen[self.freed] = self.banks
        return RingEnd(self, lane, self.filled)


class RingEnd:
    def __init__(self, ring, lane, sem):
        self.ring, self.lane, self.sem, self.turn = ring, lane, sem, 0

    def take(self):
        self.lane.wait(self.sem)
        bank = self.ring.buf[:, self.turn % self.ring.banks, :]
        self.turn += 1
        return bank

    def filled(self, ins):
        ins.then_inc(self.ring.filled, 1)

    def free(self, ins):
        ins.then_inc(self.ring.freed, 1)
        self.lane.seen[self.ring.freed] += 1

    def settle(self):
        self.lane.eng.wait_ge(self.ring.freed, self.lane.base.get(self.ring.freed, 0) + self.lane.seen[self.ring.freed])


def layernorm(nc, g, name, feature=None, token=None, out_dram=None):
    with ExitStack() as ctx:
        def sb(n, shape, dt=fp32):
            return ctx.enter_context(nc.sbuf_tensor(f"{name}_{n}", shape, dt))

        def sem(n):
            return nc.alloc_semaphore(f"{name}_{n}")

        z = sb("z", [P, NT, C])
        stats = sb("stats", [P, NT, 6])
        meanvar = sb("meanvar", [P, NT, 2])
        std = sb("std", [P, NT])
        rstd = sb("rstd", [P, NT])
        eps = sb("eps", [P, 1])
        up = ctx.enter_context(nc.psum_tensor(f"{name}_up", [P, NT, C], fp32))
        down = ctx.enter_context(nc.psum_tensor(f"{name}_down", [P, NT, C], fp32))
        turned = sem("turned")
        z_ready = sem("z_ready")
        std_ready = sem("std_ready")
        x_ready = sem("x_ready")
        back = sem("back")
        xT_ready = sem("xT_ready")
        stored = sem("stored")
        own = sem("dve_steps")
        G = 4
        block = ctx.enter_context(nc.Block())

        @block.tensor
        def _(pe):
            if feature is not None:
                for t in range(NT):
                    last = nc.tensor.transpose(up[:, t, :], feature[:, t * P:(t + 1) * P], g.ident[:])
                    if t % G == G - 1:
                        last.then_inc(turned, 1)
            if out_dram is None:
                for k in range(NT // G):
                    pe.wait_ge(x_ready, k + 1)
                    for t in range(k * G, (k + 1) * G):
                        last = nc.tensor.transpose(down[:, t, :], g.x[:, t, :], g.ident[:])
                    last.then_inc(back, 1)

        @block.vector
        def _(dve):
            lane = Lane(dve, own)
            lane.seq(nc.vector.memset(eps[:], LN_EPS))
            for k in range(NT // G):
                s = slice(k * G, (k + 1) * G)
                if feature is not None:
                    dve.wait_ge(turned, k + 1)
                delta = up[:, s, :] if feature is not None else token[:, s, :]
                lane.seq(nc.vector.tensor_tensor(z[:, s, :], delta, g.x[:, s, :], ALU.add))
                for t in range(k * G, (k + 1) * G):
                    lane.post(nc.vector.bn_stats(stats[:, t, :], z[:, t, :]))
                lane.settle()
                for t in range(k * G, (k + 1) * G):
                    last = nc.vector.bn_aggr(meanvar[:, t, :], stats[:, t, :])
                last.then_inc(z_ready, 1)
            for k in range(NT // G):
                s = slice(k * G, (k + 1) * G)
                dve.wait_ge(std_ready, k + 1)
                lane.seq(nc.vector.reciprocal(rstd[:, s], std[:, s]))
                for t in range(k * G, (k + 1) * G):
                    last = nc.vector.tensor_scalar(g.x[:, t, :], z[:, t, :], meanvar[:, t, 0:1],
                                                   rstd[:, t:t + 1], ALU.subtract, ALU.mult)
                last.then_inc(x_ready, 1)

        @block.scalar
        def _(act):
            for k in range(NT // G):
                s = slice(k * G, (k + 1) * G)
                act.wait_ge(z_ready, k + 1)
                nc.scalar.activation(std[:, s], meanvar[:, s, 1], ACT.Sqrt, bias=eps[:]).then_inc(std_ready, 1)
            if out_dram is None:
                for k in range(NT // G):
                    act.wait_ge(back, k + 1)
                    nc.scalar.copy(g.xT[:, k * QB:(k + 1) * QB], down[:, k * G:(k + 1) * G, :]).then_inc(xT_ready, 1)

        @block.sync
        def _(sp):
            if out_dram is not None:
                for k in range(NT // G):
                    sp.wait_ge(x_ready, k + 1)
                    sp.dma_start(out_dram[k * QB:(k + 1) * QB, :].rearrange("(t p) c -> p t c", p=P),
                                 g.x[:, k * G:(k + 1) * G, :]).then_inc(stored, 16)
                sp.wait_ge(stored, 16 * (NT // G))


def causal_attention(nc, g, name, w, scale, yT):
    with ExitStack() as ctx:
        def sb(n, shape, dt=fp32):
            return ctx.enter_context(nc.sbuf_tensor(f"{name}_{n}", shape, dt))

        def sem(n):
            return nc.alloc_semaphore(f"{name}_{n}")

        qT = sb("qT", [P, T])
        kT = sb("kT", [P, T])
        v = sb("v", [P, NT, C])
        probs = sb("probs", [P, 4, QB])
        chunk_max = sb("chunk_max", [P, 4, NB])
        row_max = sb("row_max", [P, 4])
        neg_rest = sb("neg_rest", [P, 4])
        neg_parts = sb("neg_parts", [P, 3, 4], bf16)
        negmax = sb("negmax", [P, T], bf16)
        ident, ones = sb("ident_bf", [P, P], bf16), sb("ones_bf", [P, P], bf16)
        mask_q, mask_k = sb("mask_q_bf", [P, P], bf16), sb("mask_k_bf", [P, P], bf16)
        rsum = sb("rsum", [P, QB])
        ring = Ring(nc, ctx, 4, name)
        scoresT = ctx.enter_context(nc.psum_tensor(f"{name}_scoresT", [P, 2, QB], fp32))
        out = ctx.enter_context(nc.psum_tensor(f"{name}_out", [P, QB], fp32))
        sums = ctx.enter_context(nc.psum_tensor(f"{name}_sums", [P, QB], fp32))

        prepared = sem("prepared")
        max_ready = sem("max_ready")
        negmax_ready = sem("negmax_ready")
        scores_ready = sem("scores_ready")
        probs_ready = sem("probs_ready")
        out_ready = sem("out_ready")
        out_taken = sem("out_taken")
        own = sem("dve_steps")

        with nc.Block() as block:
            @block.vector
            def _(dve):
                nc.vector.memset(negmax[:], 0.0)
                for dst, src in ((ident, g.ident), (ones, g.ones), (mask_q, g.mask_q), (mask_k, g.mask_k)):
                    nc.vector.tensor_copy(dst[:], src[:])
        block = ctx.enter_context(nc.Block())

        def chunks(b, qt):
            return [(c * QB, QB) for c in range(b)] + [(b * QB, P * (qt + 1))]

        def key_tiles(b):
            return [(k, max(0, (k - 4 * b) * P)) for k in range(4 * (b + 1))]

        def maxima(b):
            return [(qt, c, first, n) for qt in range(4) for c, (first, n) in enumerate(chunks(b, qt))]

        def aside(b):
            n = len(key_tiles(b))
            plan = [[] for _ in range(n)]
            todo = maxima(b + 1) if b + 1 < NB else []
            for i, item in enumerate(todo):
                plan[i * max(1, n - 2) // len(todo)].append(item)
            return plan

        @block.tensor
        def _(pe):
            lane = Lane(pe, None)
            to_dve = ring.writer(lane)
            for b in range(NB):
                for i in range(2):
                    to_dve.filled(nc.tensor.matmul(to_dve.take(), w[:, i * C:(i + 1) * C], g.xT[:, b * QB:(b + 1) * QB],
                                                   start=True, stop=True))
                bank = to_dve.take()
                for t in range(4):
                    tok = (4 * b + t) * P
                    last = nc.tensor.matmul(bank[:, t * C:(t + 1) * C], g.xT[:, tok:tok + P], w[:, 2 * C:3 * C],
                                            start=True, stop=True)
                to_dve.filled(last)
            lane.wait(prepared)

            def find_max(b, qt, c, first, n):
                q0 = b * QB + qt * P
                bank = to_dve.take()
                diag = first == b * QB
                last = nc.tensor.matmul(bank[:, 0:n], qT[:, q0:q0 + P], kT[:, first:first + n], start=True, stop=not diag)
                if diag:
                    last = nc.tensor.matmul(bank[:, n - P:n], ident[:], mask_q[:], start=False, stop=True)
                to_dve.filled(last)

            def turn_max():
                lane.wait(max_ready)
                bank = to_dve.take()
                for qt in range(4):
                    last = nc.tensor.matmul(bank[0:3, qt * P:(qt + 1) * P], neg_parts[:, :, qt], ident[:],
                                            start=True, stop=True)
                to_dve.filled(last)

            def weigh(b):
                lane.wait(negmax_ready)
                tiles = key_tiles(b)
                plan = aside(b)

                def values(j):
                    k, off = tiles[j]
                    lane.wait(probs_ready)
                    if b and j == 0:
                        lane.wait(out_taken)
                    edge = dict(start=j == 0, stop=j == len(tiles) - 1)
                    nc.tensor.matmul(out[:, off:QB], v[:, k, :], probs[:, j % 4, off:QB], **edge)
                    return nc.tensor.matmul(sums[:, off:QB], g.ones[:], probs[:, j % 4, off:QB], **edge)

                for j, (k, off) in enumerate(tiles):
                    bank = scoresT[:, j % 2, off:QB]
                    diag = k >= 4 * b
                    q = slice(b * QB + off, (b + 1) * QB)
                    nc.tensor.matmul(bank, kT[:, k * P:(k + 1) * P], qT[:, q], start=True, stop=False)
                    last = nc.tensor.matmul(bank, ones[:], negmax[:, q], start=False, stop=not diag)
                    if diag:
                        last = nc.tensor.matmul(scoresT[:, j % 2, off:off + P], ident[:], mask_k[:], start=False, stop=True)
                    last.then_inc(scores_ready, 1)
                    for item in plan[j]:
                        find_max(b + 1, *item)
                    if j == len(tiles) - 1 and b + 1 < NB:
                        turn_max()
                    if j > 0:
                        values(j - 1)
                values(len(tiles) - 1).then_inc(out_ready, 1)

            for item in maxima(0):
                find_max(0, *item)
            turn_max()
            for b in range(NB):
                weigh(b)

        @block.scalar
        def _(act):
            lane = Lane(act, None)
            for b in range(NB):
                for j, (k, off) in enumerate(key_tiles(b)):
                    lane.wait(scores_ready)
                    nc.scalar.activation(probs[:, j % 4, off:QB], scoresT[:, j % 2, off:QB], ACT.Exp,
                                         scale=scale).then_inc(probs_ready, 1)

        @block.vector
        def _(dve):
            lane = Lane(dve, own)
            from_pe = ring.reader(lane)
            for b in range(NB):
                s = slice(b * QB, (b + 1) * QB)
                for dst in (qT[:, s], kT[:, s]):
                    bank = from_pe.take()
                    from_pe.free(nc.vector.tensor_copy(dst, bank))
                bank = from_pe.take()
                from_pe.free(nc.vector.tensor_copy(v[:, 4 * b:4 * b + 4, :], bank.rearrange("p (t c) -> p t c", t=4)))
            from_pe.settle()
            dve.sem_inc(prepared, 1)

            def read_max(qt, c, first, n):
                bank = from_pe.take()
                from_pe.free(nc.vector.reduce_max(chunk_max[:, qt, c:c + 1], bank[:, 0:n], axis=AX.X))

            def finish_max(b):
                from_pe.settle()
                n = len(chunks(b, 0))
                lane.seq(nc.vector.reduce_max(row_max[:], chunk_max[:, :, 0:n], axis=AX.X))
                lane.seq(nc.vector.tensor_scalar(neg_parts[:, 0, :], row_max[:], -1.0, None, ALU.mult))
                lane.seq(nc.vector.scalar_tensor_tensor(neg_rest[:], row_max[:], -1.0, neg_parts[:, 0, :],
                                                        ALU.mult, ALU.subtract))
                lane.seq(nc.vector.tensor_copy(neg_parts[:, 1, :], neg_rest[:]))
                nc.vector.tensor_tensor(neg_parts[:, 2, :], neg_rest[:], neg_parts[:, 1, :],
                                        ALU.subtract).then_inc(max_ready, 1)
                bank = from_pe.take()
                from_pe.free(nc.vector.tensor_copy(negmax[0:3, b * QB:(b + 1) * QB], bank[0:3, :]))
                from_pe.settle()
                dve.sem_inc(negmax_ready, 1)

            for item in maxima(0):
                read_max(*item)
            finish_max(0)
            for b in range(NB):
                for items in aside(b):
                    for item in items:
                        read_max(*item)
                if b + 1 < NB:
                    finish_max(b + 1)
                lane.wait(out_ready)
                lane.seq(nc.vector.reciprocal(rsum[:], sums[:]))
                nc.vector.tensor_tensor(yT[:, b * QB:(b + 1) * QB], out[:], rsum[:], ALU.mult).then_inc(out_taken, 1)


def decayed_keys(nc, g, w, kT_out, vT_out):
    with ExitStack() as ctx:
        def sb(n, shape, dt=fp32):
            return ctx.enter_context(nc.sbuf_tensor(f"dk_{n}", shape, dt))

        def sem(n):
            return nc.alloc_semaphore(f"dk_{n}")

        square = sb("square", [P, T])
        norm = sb("norm", [P, T])
        col = sb("col", [P, 8])
        acc = [ctx.enter_context(nc.psum_tensor(f"dk_acc{i}", [P, NB, QB], fp32)) for i in range(2)]
        projected = sem("projected")
        squared = sem("squared")
        summed = sem("summed")
        normed = sem("normed")
        cols_ready = sem("cols_ready")
        raw_ready = sem("raw_ready")
        clipped = sem("clipped")
        done = sem("done")
        own = sem("dve_steps")
        act_own = sem("act_steps")
        block = ctx.enter_context(nc.Block())
        outs = (kT_out, vT_out)

        @block.tensor
        def _(pe):
            for i, wt in enumerate((w["kT"], w["vT"])):
                for b in range(NB):
                    last = nc.tensor.matmul(acc[i][:, b, :], wt[:], g.xT[:, b * QB:(b + 1) * QB], start=True, stop=True)
                last.then_inc(projected, 1)
            for i in range(2):
                pe.wait_ge(squared, i + 1)
                for b in range(NB):
                    last = nc.tensor.matmul(acc[i][:, b, :], g.head_ones[:], square[:, b * QB:(b + 1) * QB],
                                            start=True, stop=True)
                last.then_inc(summed, 1)

        @block.scalar
        def _(act):
            nc.scalar.activation(col[:, 0:1], w["beta"], ACT.Abs).then_inc(act_own, 1)
            act.wait_ge(act_own, 1)
            nc.scalar.activation(col[:, 1:2], col[:, 0:1], ACT.Exp, scale=-10.0)
            nc.scalar.activation(col[:, 3:4], w["val_scale"], ACT.Exp, scale=10.0)
            act.wait_ge(clipped, 1)
            nc.scalar.activation(col[:, 2:3], col[:, 5:6], ACT.Exp).then_inc(cols_ready, 1)
            for i in range(2):
                act.wait_ge(raw_ready, i + 1)
                if i:
                    act.wait_ge(summed, i)
                nc.scalar.activation(square[:], outs[i][:], ACT.Square).then_inc(squared, 1)
                act.wait_ge(summed, i + 1)
                if i:
                    act.wait_ge(done, 1)
                nc.scalar.activation(norm[:], acc[i][:, :, :].rearrange("p b q -> p (b q)"), ACT.Sqrt).then_inc(normed, 1)

        @block.vector
        def _(dve):
            lane = Lane(dve, own)
            nc.vector.tensor_scalar(col[:, 5:6], w["key_scale"], 10.0, KEY_SCALE_MAX, ALU.mult, ALU.min).then_inc(clipped, 1)
            lane.post(nc.vector.tensor_scalar(col[:, 4:5], w["v_coef"], -1.0, 1.0, ALU.mult, ALU.add))
            dve.wait_ge(cols_ready, 1)
            dve.wait_ge(projected, 1)
            k_raw = acc[0][:, :, :].rearrange("p b q -> p (b q)")
            v_raw = acc[1][:, :, :].rearrange("p b q -> p (b q)")
            nc.vector.tensor_tensor_scan(kT_out[:], col[:, 1:2].to_broadcast([P, T]), k_raw, 0.0,
                                         ALU.mult, ALU.add).then_inc(raw_ready, 1)
            dve.wait_ge(projected, 2)
            lane.seq(nc.vector.tensor_scalar(vT_out[:], v_raw, w["v_coef"], None, ALU.mult))
            nc.vector.scalar_tensor_tensor(vT_out[:, 0:T - 1], v_raw[:, 1:T], col[:, 4:5], vT_out[:, 0:T - 1],
                                           ALU.mult, ALU.add).then_inc(raw_ready, 1)
            dve.wait_ge(raw_ready, 2)
            for i, factor in enumerate((col[:, 2:3], col[:, 3:4])):
                dve.wait_ge(normed, i + 1)
                lane.seq(nc.vector.tensor_scalar(norm[:], norm[:], 1e-10, None, ALU.add))
                lane.seq(nc.vector.reciprocal(norm[:], norm[:]))
                nc.vector.scalar_tensor_tensor(outs[i][:], outs[i][:], factor, norm[:],
                                               ALU.mult, ALU.mult).then_inc(done, 1)


def split_keys(nc, g, name, keys, values, hi, mid, lo, v_all):
    with ExitStack() as ctx:
        rest = ctx.enter_context(nc.sbuf_tensor(f"{name}_rest", [P, T], fp32))
        turned = ctx.enter_context(nc.psum_tensor(f"{name}_turned", [P, NT, P], fp32))
        hi_ready = nc.alloc_semaphore(f"{name}_hi_ready")
        rest_ready = nc.alloc_semaphore(f"{name}_rest_ready")
        mid_ready = nc.alloc_semaphore(f"{name}_mid_ready")
        v_turned = nc.alloc_semaphore(f"{name}_v_turned")
        block = ctx.enter_context(nc.Block())

        @block.scalar
        def _(act):
            nc.scalar.copy(hi[:], keys[:]).then_inc(hi_ready, 1)
            act.wait_ge(v_turned, 1)
            nc.scalar.copy(v_all[:], turned[:])
            act.wait_ge(rest_ready, 1)
            nc.scalar.copy(mid[:], rest[:]).then_inc(mid_ready, 1)

        @block.tensor
        def _(pe):
            for t in range(NT):
                last = nc.tensor.transpose(turned[:, t, :], values[:, t * P:(t + 1) * P], g.ident[:])
            last.then_inc(v_turned, 1)

        @block.vector
        def _(dve):
            dve.wait_ge(hi_ready, 1)
            nc.vector.tensor_tensor(rest[:], keys[:], hi[:], ALU.subtract).then_inc(rest_ready, 1)
            dve.wait_ge(rest_ready, 1)
            dve.wait_ge(mid_ready, 1)
            nc.vector.tensor_tensor(lo[:], rest[:], mid[:], ALU.subtract)


def head_attention(nc, g, name, heads, D, scale, yT, wo_all, rotary=None, picked=None):
    causal = picked is not None
    S0 = 32 if causal else 64
    M = S0 + D
    with ExitStack() as ctx:
        def sb(n, shape, dt=fp32):
            return ctx.enter_context(nc.sbuf_tensor(f"{name}_{n}", shape, dt))

        def sem(n):
            return nc.alloc_semaphore(f"{name}_{n}")

        woh = sb("wo_head", [P, C])
        v = sb("v", [P, NT, M])
        probs = sb("probs", [P, 4, QB])
        chunk_max = sb("chunk_max", [P, 4, NB])
        row_max = sb("row_max", [P, 4])
        rsum = sb("rsum", [D, QB])
        oT = sb("oT", [P, QB])
        if causal:
            hi, mid, lo, v_all, groups, head_mask = picked
            sel = sb("sel", [P, 6, P], bf16)
            qs = sb("qs", [P, T], bf16)
            ks = sb("ks", [P, T], bf16)
            neg_rest = sb("neg_rest", [P, 4])
            neg_parts = sb("neg_parts", [P, 3, 4], bf16)
            ident = sb("ident_bf", [P, P], bf16)
            mask_q, mask_k = sb("mask_q_bf", [P, P], bf16), sb("mask_k_bf", [P, P], bf16)
        else:
            w_all, cos, sin = rotary
            wh = sb("w_head", [P, 5 * D])
            wv = wh[:, 4 * D:5 * D]
            qT = sb("qT", [P, T])
            kT = sb("kT", [P, T])
            rotated = sb("rotated", [P, QB])
            q_hm = sb("q_hm", [P, T], bf16)
            k_hh = sb("k_hh", [P, T], bf16)
            k_mm = sb("k_mm", [P, T], bf16)
        ring = Ring(nc, ctx, 4, name)
        scoresT = ctx.enter_context(nc.psum_tensor(f"{name}_scoresT", [P, 2, QB], fp32))
        out = ctx.enter_context(nc.psum_tensor(f"{name}_out", [P, 2, QB], fp32))

        w_ready = sem("w_ready")
        wo_ready = sem("wo_ready")
        w_used = sem("w_used")
        sum_ready = sem("sum_ready")
        k_hi_ready = sem("k_hi_ready")
        hi_ready = sem("hi_ready")
        kT_ready = sem("kT_ready")
        prepared = sem("prepared")
        k_ready = sem("k_ready")
        v_ready = sem("v_ready")
        max_ready = sem("max_ready")
        negmax_ready = sem("negmax_ready")
        scores_ready = sem("scores_ready")
        probs_ready = sem("probs_ready")
        out_ready = sem("out_ready")
        oT_ready = sem("oT_ready")
        projected = sem("projected")
        own = sem("dve_steps")
        pool_own = sem("pool_steps")

        with nc.Block() as block:
            @block.gpsimd
            def _(pool):
                nc.gpsimd.memset(woh[:], 0.0)
                nc.gpsimd.memset(v[:, :, 0:S0], 0.0)
                nc.gpsimd.memset(v[:, :, S0:M], 1.0)

            @block.vector
            def _(dve):
                nc.vector.memset(oT[:], 0.0)
                nc.vector.memset(out[:], 1.0)
                if causal:
                    nc.vector.tensor_copy(ident[:], g.ident[:])
                    nc.vector.tensor_copy(mask_q[:], g.mask_strict_q[:])
                    nc.vector.tensor_copy(mask_k[:], g.mask_strict_k[:])
                else:
                    nc.vector.memset(kT[:], 0.0).then_inc(sum_ready, 1)
                    dve.wait_ge(sum_ready, 1)
                    nc.vector.memset(kT[64:65, :], 1.0)
        begun = 0 if causal else 1

        block = ctx.enter_context(nc.Block())

        def chunks(b, qt):
            if not causal:
                return [(c * QB, QB) for c in range(NB)]
            return [(c * QB, QB) for c in range(b)] + [(b * QB, P * (qt + 1))]

        def key_tiles(b):
            if not causal:
                return [(k, 0) for k in range(NT)]
            return [(k, max(0, (k - 4 * b) * P)) for k in range(4 * (b + 1))]

        def maxima(b):
            return [(qt, c, first, n) for qt in range(4) for c, (first, n) in enumerate(chunks(b, qt))]

        def first_maxima(c):
            return [item for item in maxima(0) if item[1] == c]

        def aside(b):
            n = len(key_tiles(b))
            plan = [[] for _ in range(n)]
            if b + 1 < NB:
                todo = maxima(b + 1)
                over = max(1, n - 2)
                for i, item in enumerate(todo):
                    plan[i * over // len(todo)].append(("max",) + item)
            if b > 0:
                plan[min(6, n - 1)].append(("project",))
            return plan

        n_keys = sum(len(key_tiles(b)) for b in range(NB))
        n_prep = NB * 2 if causal else NB * 3
        n_ring = n_prep + sum(len(maxima(b)) for b in range(NB)) + NB + NB

        @block.gpsimd
        def _(pool):
            lane = Lane(pool, pool_own)
            per = {w_used: 1, projected: 1, pool_own: 1}
            if not causal:
                per |= {hi_ready: NB, prepared: 2 * NB}
            with lane.loop(heads, per) as h:
                lane.wait(w_used)
                if causal:
                    copied = nc.gpsimd.tensor_tensor(sel[:], groups[:],
                                                     head_mask[:, h, :].unsqueeze(2).to_broadcast([P, 6, P]), ALU.mult)
                    copied.then_inc(w_ready, 1)
                else:
                    nc.gpsimd.tensor_copy(wh[:], w_all[:, h, :]).then_inc(w_ready, 1)
                    for b in range(NB):
                        s = slice(b * QB, (b + 1) * QB)
                        lane.wait(hi_ready)
                        for dst, whole, upper in ((q_hm[64:P, s], qT[0:64, s], q_hm[0:64, s]),
                                                  (k_mm[64:P, s], qT[64:P, s], k_hh[64:P, s])):
                            nc.gpsimd.tensor_tensor(dst, whole, upper, ALU.subtract).then_inc(prepared, 1)
                            lane.wait(prepared)
                lane.wait(projected)
                lane.post(nc.gpsimd.tensor_copy(woh[0:D, :], wo_all[:, h, :]))
                lane.settle()
                pool.sem_inc(wo_ready, 1)

        @block.tensor
        def _(pe):
            lane = Lane(pe, None)
            to_dve = ring.writer(lane)

            def project():
                lane.wait(oT_ready)
                bank = to_dve.take()
                to_dve.filled(nc.tensor.matmul(bank[:, :], woh[:], oT[:], start=True, stop=True))

            def find_max(b, qt, c, first, n):
                q0 = b * QB + qt * P
                bank = to_dve.take()
                if causal:
                    diag = first == b * QB
                    last = nc.tensor.matmul(bank[:, 0:n], qs[:, q0:q0 + P], ks[:, first:first + n], start=True, stop=not diag)
                    if diag:
                        last = nc.tensor.matmul(bank[:, n - P:n], ident[:], mask_q[:], start=False, stop=True)
                else:
                    nc.tensor.matmul(bank[:, 0:n], q_hm[:, q0:q0 + P], k_hh[:, first:first + n], start=True, stop=False)
                    last = nc.tensor.matmul(bank[:, 0:n], q_hm[:, q0:q0 + P], k_mm[:, first:first + n], start=False, stop=True)
                to_dve.filled(last)

            def turn_max():
                lane.wait(max_ready)
                bank = to_dve.take()
                for qt in range(4):
                    cols = slice(qt * P, (qt + 1) * P)
                    if causal:
                        last = nc.tensor.matmul(bank[0:3, cols], neg_parts[:, :, qt], ident[:], start=True, stop=True)
                    else:
                        last = nc.tensor.matmul(bank[0:1, cols], row_max[:, qt:qt + 1], g.ident[:], start=True, stop=True)
                to_dve.filled(last)

            def weigh(b):
                lane.wait(negmax_ready)
                tiles = key_tiles(b)
                acc = out[:, b % 2, :]
                plan = aside(b)

                def values(j):
                    k, off = tiles[j]
                    lane.wait(probs_ready)
                    return nc.tensor.matmul(acc[0:M, off:QB], v[:, k, :], probs[:, j % 4, off:QB],
                                            start=j == 0, stop=j == len(tiles) - 1)

                for j, (k, off) in enumerate(tiles):
                    bank = scoresT[:, j % 2, off:QB]
                    diag = causal and k >= 4 * b
                    kk, qq = (ks, qs) if causal else (kT, qT)
                    last = nc.tensor.matmul(bank, kk[:, k * P:(k + 1) * P], qq[:, b * QB + off:(b + 1) * QB],
                                            start=True, stop=not diag)
                    if diag:
                        last = nc.tensor.matmul(scoresT[:, j % 2, off:off + P], ident[:], mask_k[:], start=False, stop=True)
                    last.then_inc(scores_ready, 1)
                    for kind, *item in plan[j]:
                        if kind == "max":
                            find_max(b + 1, *item)
                        else:
                            project()
                    if j == len(tiles) - 1 and b + 1 < NB:
                        turn_max()
                    if j > 0:
                        values(j - 1)
                values(len(tiles) - 1).then_inc(out_ready, 1)

            per = {ring.freed: n_ring, w_ready: 1, wo_ready: 1, prepared: NB if causal else 2 * NB,
                   v_ready: 1, k_ready: NB, kT_ready: NB, max_ready: NB, negmax_ready: NB, probs_ready: n_keys, oT_ready: NB}
            with lane.loop(heads, per) as h:
                lane.wait(w_ready)
                for b in range(NB):
                    s = slice(b * QB, (b + 1) * QB)
                    if causal:
                        for side in range(2):
                            bank = to_dve.take()
                            for i, part in enumerate((hi, mid, lo)):
                                last = nc.tensor.matmul(bank[:, :], sel[:, 3 * side + i, :], part[:, s],
                                                        start=i == 0, stop=i == 2)
                            to_dve.filled(last)
                    else:
                        for i in range(2):
                            bank = to_dve.take()
                            to_dve.filled(nc.tensor.matmul(bank[:, :], wh[:, 2 * i * D:2 * (i + 1) * D],
                                                           g.xT[:, s], start=True, stop=True))
                        bank = to_dve.take()
                        for t in range(4):
                            tok = (4 * b + t) * P
                            last = nc.tensor.matmul(bank[:, t * D:(t + 1) * D], g.xT[:, tok:tok + P], wv,
                                                    start=True, stop=True)
                        to_dve.filled(last)
                    if b == 2:
                        project()
                    if b > 1:
                        lane.wait(prepared, per[prepared] // NB)
                        if not causal:
                            lane.wait(k_ready)
                        for item in first_maxima(b - 2):
                            find_max(0, *item)
                for c in (NB - 2, NB - 1):
                    lane.wait(prepared, per[prepared] // NB)
                    if not causal:
                        lane.wait(k_ready)
                    for item in first_maxima(c):
                        find_max(0, *item)
                turn_max()
                lane.wait(v_ready)
                lane.wait(wo_ready)
                if not causal:
                    lane.wait(kT_ready, NB)
                for b in range(NB):
                    weigh(b)
            project()

        @block.scalar
        def _(act):
            lane = Lane(act, None)
            lane.seen[sum_ready] = begun
            per = {scores_ready: n_keys}
            if not causal:
                per |= {sum_ready: NB}
            with lane.loop(heads, per) as h:
                if not causal:
                    for b in range(NB):
                        s = slice(b * QB, (b + 1) * QB)
                        lane.wait(sum_ready)
                        nc.scalar.copy(k_hh[0:64, s], qT[64:P, s])
                        nc.scalar.copy(k_hh[64:P, s], qT[64:P, s]).then_inc(k_hi_ready, 1)
                        nc.scalar.copy(q_hm[0:64, s], qT[0:64, s]).then_inc(hi_ready, 1)
                        nc.scalar.copy(kT[0:64, s], qT[64:P, s]).then_inc(kT_ready, 1)
                for b in range(NB):
                    for j, (k, off) in enumerate(key_tiles(b)):
                        lane.wait(scores_ready)
                        nc.scalar.activation(probs[:, j % 4, off:QB], scoresT[:, j % 2, off:QB], ACT.Exp,
                                             scale=scale).then_inc(probs_ready, 1)

        @block.vector
        def _(dve):
            lane = Lane(dve, own)
            from_pe = ring.reader(lane)
            dve.sem_inc(w_used, 1)
            dve.sem_inc(out_ready, 1)

            def prepare(b):
                s = slice(b * QB, (b + 1) * QB)
                bank = from_pe.take()
                if causal:
                    from_pe.free(nc.vector.tensor_copy(qs[:, s], bank[:, :]))
                    bank = from_pe.take()
                    from_pe.free(nc.vector.tensor_scalar(ks[:, s], bank[:, :], g.e012[:], None, ALU.add))
                    from_pe.settle()
                    dve.sem_inc(prepared, 1)
                    return
                from_pe.free(nc.vector.tensor_tensor(qT[:, s], bank[:, :], cos[:, s], ALU.mult))
                bank = from_pe.take()
                from_pe.free(nc.vector.tensor_tensor(rotated[:], bank[:, :], sin[:, s], ALU.mult))
                from_pe.settle()
                nc.vector.tensor_tensor(qT[:, s], rotated[:], qT[:, s], ALU.add).then_inc(sum_ready, 1)
                lane.wait(sum_ready)
                bank = from_pe.take()
                from_pe.free(nc.vector.tensor_copy(v[:, 4 * b:4 * b + 4, 0:D],
                                                   bank[:, 0:4 * D].rearrange("p (t d) -> p t d", t=4)))

            def lower_keys(b):
                s = slice(b * QB, (b + 1) * QB)
                lane.wait(k_hi_ready)
                nc.vector.tensor_tensor(k_mm[0:64, s], qT[64:P, s], k_hh[64:P, s], ALU.subtract).then_inc(k_ready, 1)

            def add_projected(b):
                s = slice(b * QB, (b + 1) * QB)
                bank = from_pe.take()
                from_pe.free(nc.vector.tensor_tensor(yT[:, s], bank[:, :], yT[:, s], ALU.add))

            def read_max(qt, c, first, n):
                bank = from_pe.take()
                from_pe.free(nc.vector.reduce_max(chunk_max[:, qt, c:c + 1], bank[:, 0:n], axis=AX.X))

            def finish_max(b):
                from_pe.settle()
                n = len(chunks(b, 0))
                ins = nc.vector.reduce_max(row_max[:], chunk_max[:, :, 0:n], axis=AX.X)
                if causal:
                    lane.seq(ins)
                    lane.seq(nc.vector.tensor_scalar(neg_parts[:, 0, :], row_max[:], -1.0, None, ALU.mult))
                    lane.seq(nc.vector.scalar_tensor_tensor(neg_rest[:], row_max[:], -1.0, neg_parts[:, 0, :],
                                                            ALU.mult, ALU.subtract))
                    lane.seq(nc.vector.tensor_copy(neg_parts[:, 1, :], neg_rest[:]))
                    ins = nc.vector.tensor_tensor(neg_parts[:, 2, :], neg_rest[:], neg_parts[:, 1, :], ALU.subtract)
                ins.then_inc(max_ready, 1)

            def write_max(b):
                s = slice(b * QB, (b + 1) * QB)
                bank = from_pe.take()
                if causal:
                    from_pe.free(nc.vector.tensor_copy(qs[0:3, s], bank[0:3, :]))
                else:
                    from_pe.free(nc.vector.tensor_scalar(qT[64:65, s], bank[0:1, :], -1.0, None, ALU.mult))
                from_pe.settle()
                dve.sem_inc(negmax_ready, 1)

            def normalise(b):
                acc = out[:, b % 2, :]
                lane.wait(out_ready)
                for i in range(4):
                    q = slice(i * P, (i + 1) * P)
                    lane.post(nc.vector.reciprocal(rsum[:, q], acc[S0:M, q]))
                    yield
                lane.settle()
                ins = nc.vector.tensor_tensor(oT[0:D, :], acc[0:D, :], rsum[:], ALU.mult)
                if causal and b == 0:
                    lane.seq(ins)
                    ins = nc.vector.memset(oT[:, 0:1], 0.0)
                ins.then_inc(oT_ready, 1)
                yield

            per = {ring.filled: n_ring, ring.freed: n_ring, out_ready: NB, own: HEAD_STEPS[name]}
            if not causal:
                per |= {sum_ready: NB, k_hi_ready: NB}
                lane.seen[sum_ready] = begun
            with lane.loop(heads, per) as h:
                steps = normalise(NB - 1)
                next(steps)
                next(steps)
                for b in range(NB):
                    prepare(b)
                    if b == 0:
                        for _ in steps:
                            pass
                    if b == 2:
                        add_projected(NB - 1)
                        from_pe.settle()
                        dve.sem_inc(projected, 1)
                    if b > 1:
                        for item in first_maxima(b - 2):
                            read_max(*item)
                    if not causal:
                        lower_keys(b)
                if causal:
                    lane.seq(nc.vector.tensor_copy(v[:, :, 0:D], v_all[:, :, h, :]))
                from_pe.settle()
                dve.sem_inc(v_ready, 1)
                dve.sem_inc(w_used, 1)
                for c in (NB - 2, NB - 1):
                    for item in first_maxima(c):
                        read_max(*item)
                finish_max(0)
                write_max(0)
                for b in range(NB):
                    steps = normalise(b - 1) if b > 0 else iter(())
                    for items in aside(b):
                        next(steps, None)
                        for kind, *item in items:
                            if kind == "max":
                                read_max(*item)
                            else:
                                add_projected(b - 1)
                    if b + 1 < NB:
                        finish_max(b + 1)
                        write_max(b + 1)
            for _ in normalise(NB - 1):
                pass
            add_projected(NB - 1)


E_ = 8
F_ = 512
FT = F_ // P
TOPK = T // E_
EXPERT_COLS = F_ + FT * C + FT + 1


def stage_l0_ffn(nc, g, d, y):
    with ExitStack() as ctx:
        def sb(n, shape, dt=fp32):
            return ctx.enter_context(nc.sbuf_tensor(f"l0f_{n}", shape, dt))
        ws, bs = sb("ws", [P, E_]), sb("bs", [P, NT, E_])
        probsT = sb("probsT", [E_, T])
        left = sb("left", [E_, T])
        gates = sb("gates", [P, T])
        expert_out = sb("expert_out", [C, E_, T])
        select = sb("select", [P, E_, P])
        zero(nc, "l0f_gates", gates)
        zero(nc, "l0f_select", select)
        load(nc, "l0f", [(ws[:], d["L0_ffn_Ws"]), (bs[:], d["h_l0_bs"]), (select[0:E_], d["c_select8"])])
        route(nc, g, ws, bs, probsT, left)
        experts(nc, g, d, probsT, left, gates, expert_out)
        combine(nc, g, select, gates, expert_out)
    layernorm(nc, g, "ln1", feature=g.delta)


def route(nc, g, ws, bs, probsT, left):
    with ExitStack() as ctx:
        def sb(n, shape, dt=fp32):
            return ctx.enter_context(nc.sbuf_tensor(f"rt_{n}", shape, dt))

        def sem(n):
            return nc.alloc_semaphore(f"rt_{n}")
        p = sb("p", [P, NT, E_])
        row = sb("row", [P, NT])
        logits = ctx.enter_context(nc.psum_tensor("rt_logits", [P, NT, E_], fp32))
        turned = ctx.enter_context(nc.psum_tensor("rt_turned", [E_, T], fp32))
        logits_ready, shifted = sem("logits_ready"), sem("shifted")
        exp_ready, p_ready, turned_ready = sem("exp_ready"), sem("p_ready"), sem("turned_ready")
        own = sem("dve_steps")
        block = ctx.enter_context(nc.Block())

        @block.tensor
        def _(pe):
            for t in range(NT):
                last = nc.tensor.matmul(logits[:, t, :], g.xT[:, t * P:(t + 1) * P], ws[:], start=True, stop=True)
            last.then_inc(logits_ready, 1)
            pe.wait_ge(p_ready, 1)
            for t in range(NT):
                last = nc.tensor.transpose(turned[:, t * P:(t + 1) * P], p[:, t, :], g.ident[:])
            last.then_inc(turned_ready, 1)

        @block.vector
        def _(dve):
            lane = Lane(dve, own)
            dve.wait_ge(logits_ready, 1)
            lane.seq(nc.vector.tensor_tensor(p[:], logits[:], bs[:], ALU.add))
            lane.seq(nc.vector.reduce_max(row[:], p[:], axis=AX.X))
            nc.vector.tensor_tensor(p[:], p[:], spread(row[:], E_), ALU.subtract).then_inc(shifted, 1)
            dve.wait_ge(exp_ready, 1)
            lane.seq(nc.vector.reduce_sum(row[:], p[:], axis=AX.X))
            lane.seq(nc.vector.reciprocal(row[:], row[:]))
            nc.vector.tensor_tensor(p[:], p[:], spread(row[:], E_), ALU.mult).then_inc(p_ready, 1)
            dve.wait_ge(turned_ready, 1)
            nc.vector.tensor_copy(probsT[:], turned[:])
            nc.vector.tensor_copy(left[:], turned[:])

        @block.scalar
        def _(act):
            act.wait_ge(shifted, 1)
            nc.scalar.activation(p[:], p[:], ACT.Exp).then_inc(exp_ready, 1)


def spread(ap, n):
    return ap.unsqueeze(2).to_broadcast([ap.shape[0], ap.shape[1], n])


def experts(nc, g, d, probsT, left, gates, expert_out):
    with ExitStack() as ctx:
        def sb(n, shape, dt=fp32):
            return ctx.enter_context(nc.sbuf_tensor(f"ex_{n}", shape, dt))

        def sem(n):
            return nc.alloc_semaphore(f"ex_{n}")
        w = sb("w", [P, 2, EXPERT_COLS])
        hidden = sb("hidden", [P, 2, FT, QB])
        best = sb("best", [E_, 8])
        up = ctx.enter_context(nc.psum_tensor("ex_up", [P, FT, QB], fp32))
        down = ctx.enter_context(nc.psum_tensor("ex_down", [P, 2, QB], fp32))
        loaded = [sem(f"loaded{s}") for s in range(2)]
        w_free = sem("w_free")
        up_ready = sem("up_ready")
        up_done = sem("up_done")
        down_ready = sem("down_ready")
        down_done = sem("down_done")
        own = sem("dve_steps")
        block = ctx.enter_context(nc.Block())
        b1_at, b2_at = F_ + FT * C, F_ + FT * C + FT

        @block.sync
        def _(sp):
            lane = Lane(sp, None)
            with lane.loop(E_ // 2, {w_free: 2}) as i:
                for s in range(2):
                    lane.wait(w_free)
                    sp.dma_start(w[:, s, :], d["h_l0_experts"][2 * i + s]).then_inc(loaded[s], 16)

        @block.tensor
        def _(pe):
            lane = Lane(pe, None)
            with lane.loop(E_ // 2, {loaded[0]: 16, loaded[1]: 16, up_done: 2 * NB * FT,
                                     down_done: 2 * NB}) as i:
                for s in range(2):
                    lane.wait(loaded[s], 16)

                    def make_up(b):
                        for f in range(FT):
                            lane.wait(up_done)
                            nc.tensor.matmul(up[:, f, :], w[:, s, f * P:(f + 1) * P], g.xT[:, b * QB:(b + 1) * QB],
                                             start=True, stop=True).then_inc(up_ready, 1)

                    def make_down(b):
                        lane.wait(down_done)
                        for f in range(FT):
                            last = nc.tensor.matmul(down[:, b % 2, :], w[:, s, F_ + f * C:F_ + (f + 1) * C],
                                                    hidden[:, b % 2, f, :], start=f == 0, stop=f == FT - 1)
                        last.then_inc(down_ready, 1)
                    make_up(0)
                    for b in range(1, NB):
                        make_up(b)
                        make_down(b - 1)
                    pe.wait_ge(up_done, lane.base[up_done] + lane.seen[up_done] + FT)
                    make_down(NB - 1)

        @block.scalar
        def _(act):
            lane = Lane(act, None)
            act.sem_inc(up_done, FT)
            act.sem_inc(down_done, 2)
            act.sem_inc(w_free, 2)
            with lane.loop(E_ // 2, {up_ready: 2 * NB * FT, down_ready: 2 * NB}) as i:
                for s in range(2):
                    def gelu(b):
                        for f in range(FT):
                            lane.wait(up_ready)
                            nc.scalar.activation(hidden[:, b % 2, f, :], up[:, f, :], ACT.Gelu_apprx_tanh,
                                                 bias=w[:, s, b1_at + f:b1_at + f + 1]).then_inc(up_done, 1)

                    def store(b):
                        lane.wait(down_ready)
                        nc.scalar.activation(expert_out[:, 2 * i + s, b * QB:(b + 1) * QB], down[:, b % 2, :],
                                             ACT.Identity, bias=w[:, s, b2_at:b2_at + 1]).then_inc(down_done, 1)
                    gelu(0)
                    for b in range(1, NB):
                        gelu(b)
                        store(b - 1)
                    store(NB - 1)
                    act.wait_ge(down_done, 2 + NB * (2 * i + s + 1))
                    act.sem_inc(w_free, 1)

        @block.vector
        def _(dve):
            lane = Lane(dve, own)
            for _ in range(TOPK // 8):
                lane.seq(nc.vector.max(best[:], left[:]))
                lane.seq(nc.vector.match_replace(left[:], best[:], left[:], -1.0))
            nc.vector.scalar_tensor_tensor(gates[0:E_], left[:], 0.0, probsT[:], ALU.is_lt, ALU.mult)


def combine(nc, g, select, gates, expert_out):
    with ExitStack() as ctx:
        def sem(n):
            return nc.alloc_semaphore(f"cb_{n}")
        part = ctx.enter_context(nc.sbuf_tensor("cb_part", [P, 2, T // 2], fp32))
        spread_gate = ctx.enter_context(nc.psum_tensor("cb_gate", [P, 2, 2, QB], fp32))
        gate_ready, gate_used = sem("gate_ready"), sem("gate_used")
        own = sem("dve_steps")
        block = ctx.enter_context(nc.Block())
        H = T // 2

        @block.tensor
        def _(pe):
            n = 0
            for e in range(E_):
                for half in range(2):
                    if n >= 2:
                        pe.wait_ge(gate_used, n - 1)
                    for b in range(2):
                        at = half * H + b * QB
                        last = nc.tensor.matmul(spread_gate[:, half, b, :], select[:, e, :], gates[:, at:at + QB],
                                                start=True, stop=True)
                    last.then_inc(gate_ready, 1)
                    n += 1

        @block.vector
        def _(dve):
            lane = Lane(dve, own)
            n = 0
            for e in range(E_):
                for half in range(2):
                    n += 1
                    s = slice(half * H, (half + 1) * H)
                    dve.wait_ge(gate_ready, n)
                    weight = spread_gate[:, half].rearrange("p b q -> p (b q)")
                    dst = g.delta[:, s] if e == 0 else part[:, half, :]
                    nc.vector.tensor_tensor(dst, weight, expert_out[:, e, s], ALU.mult).then_inc(gate_used, 1)
                    dve.wait_ge(gate_used, n)
                    if e:
                        lane.seq(nc.vector.tensor_tensor(g.delta[:, s], part[:, half, :], g.delta[:, s], ALU.add))


DEPTH = 6
LH = 16
LD = 64
INNER = LH * LD
WIN = 32
SPAN = WIN + P
GROUP = 3
GROUPS = [list(range(a, min(a + GROUP, LH))) for a in range(0, LH, GROUP)]
FI = int(C * 4 * 2 / 3)
FCH = [(a, min(P, FI - a)) for a in range(0, FI, P)]
LEFT = 64
QK_SCALE = 8.0
PIECES = 6
A_RING, C_RING = PIECES + 4, 3


def hold(eng, sem):
    eng.sem_inc(sem, 1)


def shift_copy(nc, lane, held, dst, src, first, count, ready):
    hold(lane.eng, held)
    lane.seq(nc.gpsimd.tensor_copy(dst[0:C // 2, :], src[0:C // 2, bass.ds(first + LEFT, count)]))
    hold(lane.eng, held)
    nc.gpsimd.tensor_copy(dst[C // 2:C, :], src[C // 2:C, bass.ds(first + LEFT - 1, count)]).then_inc(ready, 1)


def stage_l1_ffn(nc, g, d, y):
    with ExitStack() as ctx:
        def sb(n, shape, dt=fp32):
            return ctx.enter_context(nc.sbuf_tensor(f"lw_{n}", shape, dt))

        def sem(n):
            return nc.alloc_semaphore(f"lw_{n}")
        L = Shared()
        L.sb = sb
        L.xa, L.xb = sb("xa", [C, LEFT + T + P]), sb("xb", [C, LEFT + T + P])
        L.wqkv, L.wo = sb("wqkv", [C, 3 * INNER]), sb("wo", [P, INNER // P, C])
        L.w1, L.w2 = sb("w1", [C, 2 * FI]), sb("w2", [P, len(FCH), C])
        L.scales = sb("scales", [P, 4, LD])
        L.cols = sb("cols", [P, 3 + 2 * len(FCH)])
        L.rope = sb("rope", [P, NT, 4, LD])
        L.band = sb("band", [P, 2, SPAN], bf16)
        L.ident16 = sb("ident16", [P, P], bf16)
        L.halo_scale = sb("halo_scale", [P, 1])
        L.minus_half = sb("minus_half", [P, 2 * LH])
        L.bank = ctx.enter_context(nc.psum_tensor("lw_bank", [P, 8, QB], fp32))
        band32 = sb("band32", [P, 2, SPAN])
        cleared = sem("cleared")
        L.held, L.held_sp = sem("held"), sem("held_sp")
        load(nc, "lw", [(L.rope[:], d["c_rope"]), (band32[:], d["c_band"]), (L.halo_scale[:], d["c_halo_scale"]),
                        (L.wqkv[:], d["h_lw_wqkv"][0]), (L.wo[:], d["h_lw_wo"][0]), (L.scales[:], d["h_lw_scales"][0])])
        with nc.Block() as block:
            @block.vector
            def _(dve):
                nc.vector.memset(L.xa[:], 0.0).then_inc(cleared, 1)
                nc.vector.memset(L.xb[:], 0.0)
                nc.vector.tensor_copy(L.band[:], band32[:])
                nc.vector.tensor_copy(L.ident16[:], g.ident[:])
                dve.wait_ge(cleared, 1)
                nc.vector.tensor_copy(L.xa[:, LEFT:LEFT + T], g.xT[:])

            @block.gpsimd
            def _(pool):
                nc.gpsimd.memset(L.minus_half[:], -0.5)
        A = LocalAttention(nc, g, L, ctx)
        with nc.Block() as block:
            @block.scalar
            def _(act):
                act.sem_inc(A.ring_freed, 2)
        F = LocalFfn(nc, g, L, ctx)
        L.w_loaded, L.wf_loaded = sem("w_loaded"), sem("wf_loaded")
        L.d = d
        with nc.Fori(0, DEPTH) as layer:
            A.run(layer)
            F.run(layer)
        with nc.Block() as block:
            @block.vector
            def _(dve):
                nc.vector.tensor_copy(g.delta[:], L.xa[:, LEFT:LEFT + T])
    layernorm(nc, g, "ln3", feature=g.delta)


class LocalAttention:

    def __init__(self, nc, g, L, ctx):
        self.nc, self.g, self.L = nc, g, L

        def sem(n):
            return nc.alloc_semaphore(f"la_{n}")

        def sb(n, shape, dt=fp32):
            return ctx.enter_context(nc.sbuf_tensor(f"la_{n}", shape, dt))
        self.xs = sb("xs", [C, 2, P])
        self.raw = sb("raw", [P, 2 * LH, LD])
        self.square = sb("square", [P, 2 * LH, LD])
        self.roped = sb("roped", [P, 2 * LH, LD])
        self.turn = sb("turn", [P, 2 * LH, LD])
        self.tab = sb("tab", [P, 4, LD])
        self.sumsq = sb("sumsq", [P, 2 * LH])
        self.rnorm = sb("rnorm", [P, 2, 2 * LH])
        self.qfac = sb("qfac", [P, 2, 2, LH])
        self.v = sb("v", [P, 2, INNER])
        self.vh = sb("vh", [WIN, 2, INNER])
        self.qT = sb("qT", [P, 2, LH // 2, P])
        self.kT = sb("kT", [P, 2, LH, SPAN])
        self.rowmax = sb("rowmax", [P, LH])
        self.bias = sb("bias", [P, LH])
        self.rowsum = sb("rowsum", [P, LH])
        self.rrow = sb("rrow", [P, LH])
        self.p = sb("p", [P, 3, GROUP, SPAN])
        self.pT = sb("pT", [P, 2, GROUP, P])
        self.pTh = sb("pTh", [WIN, 2, GROUP, WIN])
        self.o = sb("o", [P, INNER])
        self.oT = sb("oT", [P, INNER // P, C])
        self.ring_filled = sem("ring_filled")
        self.ring_freed = sem("ring_freed")
        self.scores_ready = sem("scores_ready")
        self.bias_ready = sem("bias_ready")
        self.probs_ready = sem("probs_ready")
        self.pT_ready = sem("pT_ready")
        self.pT_copied = sem("pT_copied")
        self.out_ready = sem("out_ready")
        self.o_ready = sem("o_ready")
        self.vh_ready = sem("vh_ready")
        self.q_roped = sem("q_roped")
        self.xs_ready = sem("xs_ready")
        self.tab_ready = sem("tab_ready")
        self.squares_ready = sem("squares_ready")
        self.q_squares = sem("q_squares")
        self.sums_ready = sem("sums_ready")
        self.rot_ready = sem("rot_ready")
        self.rope_done = sem("rope_done")
        self.qfac_ready = sem("qfac_ready")
        self.halo_ready = sem("halo_ready")
        self.dve_steps = sem("dve_steps")
        self.act_steps = sem("act_steps")
        self.pool_steps = sem("pool_steps")
        with nc.Block() as block:
            @block.vector
            def _(dve):
                nc.vector.memset(self.kT[:], 0.0)
                nc.vector.memset(self.vh[:], 0.0)
        groups = len(GROUPS)
        self.per_tile = {
            self.ring_filled: A_RING + C_RING, self.ring_freed: A_RING + C_RING,
            self.scores_ready: groups, self.bias_ready: groups, self.probs_ready: groups,
            self.pT_ready: groups, self.pT_copied: groups, self.out_ready: 1, self.o_ready: 1,
            self.vh_ready: 1, self.q_roped: 1, self.xs_ready: 1, self.tab_ready: 1,
            self.squares_ready: 1, self.q_squares: 1, self.sums_ready: 1, self.rot_ready: 2, self.rope_done: 1, self.qfac_ready: 1,
            self.halo_ready: 1, self.dve_steps: groups + 1, self.pool_steps: 6}

    def steps(self, lane, body):
        body(0, None, None, 0, False)
        body(1, 0, None, 1, True)
        with lane.loop((NT - 2) // 2, {sem: 2 * by for sem, by in self.per_tile.items()}) as i:
            body(2 * i + 2, 2 * i + 1, 2 * i, 0, False)
            body(2 * i + 3, 2 * i + 2, 2 * i + 1, 1, False)
        body(None, NT - 1, NT - 2, 0, False)
        body(None, None, NT - 1, 1, False)

    def base(self, layer, given=0):
        base = {sem: layer * by * NT for sem, by in self.per_tile.items()}
        base[self.ring_freed] = layer * (A_RING + C_RING) * NT + given
        base[self.xs_ready] = layer * (NT + 1)
        base[self.pool_steps] = layer * (6 * NT + 1)
        return base

    def check(self, lane):
        for sem, by in self.per_tile.items():
            assert lane.seen.get(sem, 0) <= by * NT + 1, (sem.name, lane.seen[sem], by * NT)

    def run(self, layer):
        nc, g, L = self.nc, self.g, self.L
        S = self
        bank = L.bank
        RING, SCORES, PT, OUT = 0, 2, 4, 6
        out = bank[:, OUT:OUT + 2, :].rearrange("p b q -> p (b q)")

        def scores_of(k):
            return bank[:, SCORES + k % 2, 0:GROUP * SPAN].rearrange("p (h s) -> p h s", s=SPAN)
        with nc.Block() as block:
            @block.sync
            def _(sp):
                for dst, src in ((L.w1[:], "L1_ffn_W1"), (L.w2[:], "h_lw_w2"), (L.cols[:], "h_lw_cols")):
                    sp.dma_start(dst, L.d[src][layer]).then_inc(L.wf_loaded, 16)
                sp.wait_ge(L.wf_loaded, 16 * 3 * (layer + 1))
                hold(sp, L.held_sp)

            @block.gpsimd
            def _(pool):
                lane = Lane(pool, S.pool_steps, S.base(layer, given=2))
                one = nc.gpsimd

                def shifted(t, slot):
                    shift_copy(nc, lane, L.held, S.xs[:, slot, :], L.xa, t * P, P, S.xs_ready)
                    lane.wait(S.xs_ready)
                    hold(pool, L.held)

                def body(a, b, c, s, first):
                    if a is None:
                        return
                    one.tensor_tensor(S.tab[:], L.rope[:, a, :, :], L.scales[:], ALU.mult).then_inc(S.tab_ready, 1)
                    lane.wait(S.ring_freed, 4)
                    one.tensor_tensor(S.square[:, LH:, :], S.raw[:, LH:, :], S.raw[:, LH:, :],
                                      ALU.mult).then_inc(S.squares_ready, 1)
                    lane.skip(S.ring_freed, A_RING - 4 + (C_RING if c is not None else 0))
                    lane.wait(S.rot_ready)
                    one.tensor_tensor(S.roped[:, 0:LH, :], S.roped[:, 0:LH, :], S.turn[:, 0:LH, :], ALU.add).then_inc(S.q_roped, 1)
                    lane.wait(S.sums_ready)
                    hold(pool, L.held)
                    lane.seq(one.tensor_scalar(S.sumsq[:], S.sumsq[:], 1e-24, None, ALU.max))
                    lane.post(one.tensor_tensor(S.rnorm[:, s, LH:], S.sumsq[:, LH:], L.minus_half[:, LH:], ALU.pow))
                    lane.wait(S.rot_ready)
                    lane.post(one.tensor_tensor(S.roped[:, LH:, :], S.roped[:, LH:, :], S.turn[:, LH:, :], ALU.add))
                    lane.settle()
                    one.tensor_tensor(S.roped[:, LH:, :], S.roped[:, LH:, :], spread(S.rnorm[:, s, LH:], LD),
                                      ALU.mult).then_inc(S.rope_done, 1)
                    lane.seq(one.tensor_tensor(S.rnorm[:, s, 0:LH], S.sumsq[:, 0:LH], L.minus_half[:, 0:LH], ALU.pow))
                    hold(pool, L.held)
                    lane.post(one.tensor_scalar(S.qfac[:, s, 0, :], S.rnorm[:, s, 0:LH], QK_SCALE, None, ALU.mult))
                    one.tensor_scalar(S.qfac[:, s, 1, :], S.rnorm[:, s, 0:LH], -QK_SCALE, None, ALU.mult).then_inc(S.qfac_ready, 1)
                    lane.wait(S.rope_done)
                    lane.wait(S.qfac_ready)
                    shifted(a + 1, 1 - s)
                shifted(0, 0)
                S.steps(lane, body)
                S.check(lane)

            @block.tensor
            def _(pe):
                lane = Lane(pe, None, S.base(layer))
                place = [0]

                def ring():
                    lane.wait(S.ring_freed)
                    place[0] += 1
                    return bank[:, RING + (place[0] - 1) % 2, :]

                def body(a, b, c, s, first):
                    o = 1 - s

                    def scores(k):
                        dst = scores_of(k)
                        for i, h in enumerate(GROUPS[k]):
                            nc.tensor.matmul(dst[:, i, :], S.qT[:, o, h // 2, :], S.kT[:, o, h, :], start=True, stop=False)
                            last = nc.tensor.matmul(dst[:, i, :], L.ident16[:], L.band[:, 1 if first else 0, :],
                                                    start=False, stop=True)
                        last.then_inc(S.scores_ready, 1)

                    def transpose_probs(k):
                        lane.wait(S.probs_ready)
                        for i, h in enumerate(GROUPS[k]):
                            nc.tensor.transpose(bank[:, PT + k % 2, i * P:(i + 1) * P], S.p[:, k % 3, i, WIN:SPAN], g.ident[:])
                        for i, h in enumerate(GROUPS[k]):
                            at = GROUP * P + i * WIN
                            last = nc.tensor.transpose(bank[0:WIN, PT + k % 2, at:at + WIN], S.p[0:WIN, k % 3, i, 0:WIN],
                                                       g.ident[0:WIN, 0:WIN])
                        last.then_inc(S.pT_ready, 1)

                    def values(k):
                        lane.wait(S.pT_copied)
                        for i, h in enumerate(GROUPS[k]):
                            cols = slice(h * LD, (h + 1) * LD)
                            nc.tensor.matmul(out[:, cols], S.pT[:, k % 2, i, :], S.v[:, o, cols], start=True, stop=True)
                            last = nc.tensor.matmul(out[0:WIN, cols], S.pTh[:, k % 2, i, :], S.vh[:, o, cols],
                                                    start=False, stop=True, skip_group_check=True)
                        return last

                    def project(j):
                        nc.tensor.matmul(ring(), S.xs[:, s, :], L.wqkv[:, j * QB:(j + 1) * QB],
                                         start=True, stop=True).then_inc(S.ring_filled, 1)

                    def turn(src, j):
                        dst = ring()
                        for i in range(4):
                            at = (4 * j + i) * P
                            last = nc.tensor.transpose(dst[:, i * P:(i + 1) * P], src[:, at:at + P], g.ident[:])
                        last.then_inc(S.ring_filled, 1)

                    def output():
                        dst = ring()
                        lane.ahead(S.ring_freed, 1)
                        for i in range(INNER // P):
                            nc.tensor.matmul(dst[:, 0:P], L.wo[:, i, :], S.oT[:, i, :], start=i == 0, stop=False)
                        nc.tensor.matmul(dst[:, 0:P], g.ident[:], L.xa[:, bass.ds(c * P + LEFT, P)],
                                         start=False, stop=True).then_inc(S.ring_filled, 1)
                    flat = S.roped[:].rearrange("p h d -> p (h d)")
                    if a is not None:
                        lane.wait(S.xs_ready)
                        for k in range(4):
                            project(k)
                    if b is not None:
                        lane.ahead(S.ring_freed, 0 if a is not None else 2)
                        lane.wait(S.halo_ready)
                        lane.wait(S.vh_ready)
                        for k in range(2):
                            scores(k)
                    if c is not None:
                        lane.wait(S.o_ready)
                        for j in range(2):
                            turn(S.o[:], j)
                    if b is not None:
                        transpose_probs(0)
                    for k in range(PIECES):
                        if b is not None:
                            if k + 2 < PIECES:
                                scores(k + 2)
                            if k + 1 < PIECES:
                                transpose_probs(k + 1)
                        if a is not None and k in (0, 2):
                            project(4 + k // 2)
                        if c is not None and k == 1:
                            output()
                        if a is not None and k in (3, 4):
                            if k == 3:
                                lane.wait(S.q_roped)
                            turn(flat, k - 3)
                        if a is not None and k == 5:
                            lane.wait(S.rope_done)
                            turn(flat, 2)
                        if b is not None:
                            last = values(k)
                    if b is not None:
                        last.then_inc(S.out_ready, 1)
                    if a is not None:
                        turn(flat, 3)
                S.steps(lane, body)
                S.check(lane)

            @block.scalar
            def _(act):
                lane = Lane(act, S.act_steps, S.base(layer, given=2))
                place = [0]

                def taken():
                    lane.wait(S.ring_filled)
                    lane.skip(S.ring_freed, 1)
                    place[0] += 1
                    return bank[:, RING + (place[0] - 1) % 2, :]

                def copy(dst, shape=None):
                    src = taken()
                    if shape:
                        src = src.rearrange("p (a b) -> p a b", b=shape)
                    nc.scalar.copy(dst, src).then_inc(S.ring_freed, 1)

                def body(a, b, c, s, first):
                    o = 1 - s

                    def weigh(k):
                        lane.wait(S.bias_ready)
                        src = scores_of(k)
                        for i, h in enumerate(GROUPS[k]):
                            last = nc.scalar.activation(S.p[:, k % 3, i, :], src[:, i, :], ACT.Exp,
                                                        bias=S.bias[:, h:h + 1], scale=S.qfac[:, o, 0, h:h + 1],
                                                        accum_out=S.rowsum[:, h:h + 1])
                        last.then_inc(S.probs_ready, 1)
                    if a is not None:
                        for k in range(4):
                            copy(S.raw[:, 8 * k:8 * k + 8, :], shape=LD)
                        lane.ahead(S.ring_freed, 0)
                        nc.scalar.activation(S.square[:, 0:LH, :], S.raw[:, 0:LH, :], ACT.Square).then_inc(S.q_squares, 1)
                    if b is not None:
                        weigh(0)
                        weigh(1)
                    if c is not None:
                        for j in range(2):
                            copy(S.oT[:, 4 * j:4 * j + 4, :], shape=C)
                    for k in range(PIECES):
                        if b is not None and k + 2 < PIECES:
                            weigh(k + 2)
                        if a is not None and k in (0, 2):
                            copy(S.v[:, s, (k // 2) * QB:(k // 2 + 1) * QB])
                        if c is not None and k == 1:
                            copy_y = taken()
                            nc.scalar.copy(L.xb[:, bass.ds(c * P + LEFT, P)], copy_y[:, 0:P]).then_inc(S.ring_freed, 1)
                        if a is not None and k in (3, 4):
                            copy(S.qT[:, s, 4 * (k - 3):4 * (k - 3) + 4, :], shape=P)
                        if a is not None and k == 4:
                            if b is not None:
                                lane.ahead(S.ring_freed, 0)
                                nc.scalar.copy(S.vh[:, s, :], S.v[P - WIN:P, o, :]).then_inc(S.vh_ready, 1)
                            else:
                                act.sem_inc(S.vh_ready, 1)
                    if a is not None:
                        for j in range(2):
                            src = taken().rearrange("p (a b) -> p a b", b=P)
                            nc.scalar.copy(S.kT[0:LD, s, 8 * j:8 * j + 8:2, WIN:SPAN], src[0:LD])
                            nc.scalar.copy(S.kT[LD:P, s, 8 * j + 1:8 * j + 8:2, WIN:SPAN], src[LD:P]).then_inc(S.ring_freed, 1)
                S.steps(lane, body)
                S.check(lane)

            @block.vector
            def _(dve):
                lane = Lane(dve, S.dve_steps, S.base(layer, given=2))

                def body(a, b, c, s, first):
                    o = 1 - s

                    def find_bias(k):
                        lane.wait(S.scores_ready)
                        src = scores_of(k)
                        h0, n = GROUPS[k][0], len(GROUPS[k])
                        hs = slice(h0, h0 + n)
                        lane.seq(nc.vector.reduce_max(S.rowmax[:, hs], src[:, 0:n, :], axis=AX.X))
                        nc.vector.tensor_tensor(S.bias[:, hs], S.rowmax[:, hs], S.qfac[:, o, 1, hs],
                                                ALU.mult).then_inc(S.bias_ready, 1)

                    def copy_probs(k):
                        lane.wait(S.pT_ready)
                        n = len(GROUPS[k])
                        nc.vector.tensor_copy(S.pT[:, k % 2, 0:n, :],
                                              bank[:, PT + k % 2, 0:n * P].rearrange("p (h q) -> p h q", q=P))
                        at = GROUP * P
                        nc.vector.tensor_copy(S.pTh[:, k % 2, 0:n, :],
                                              bank[0:WIN, PT + k % 2, at:at + n * WIN].rearrange("p (h q) -> p h q", q=WIN)
                                              ).then_inc(S.pT_copied, 1)

                    def rotate(half):
                        hs = slice(half * LH, (half + 1) * LH)
                        lane.wait(S.ring_freed, 2)
                        if half == 0:
                            lane.wait(S.tab_ready)
                        tab = S.tab[:, 2 * half:2 * half + 2, :]

                        def heads_of(x):
                            return x.unsqueeze(1).to_broadcast([P, LH, x.shape[-1]])
                        H2 = LD // 2
                        nc.vector.tensor_tensor(S.roped[:, hs, :], S.raw[:, hs, :], heads_of(tab[:, 0, :]), ALU.mult)
                        nc.vector.tensor_tensor(S.turn[:, hs, 0:H2], S.raw[:, hs, H2:LD], heads_of(tab[:, 1, 0:H2]), ALU.mult)
                        nc.vector.tensor_tensor(S.turn[:, hs, H2:LD], S.raw[:, hs, 0:H2], heads_of(tab[:, 1, H2:LD]),
                                                ALU.mult).then_inc(S.rot_ready, 1)
                    if b is not None:
                        if first:
                            nc.vector.memset(S.kT[:, o, :, 0:WIN], 0.0).then_inc(S.halo_ready, 1)
                        else:
                            nc.vector.tensor_scalar(S.kT[:, o, :, 0:WIN], S.kT[:, s, :, P:SPAN], L.halo_scale[:], None,
                                                    ALU.mult).then_inc(S.halo_ready, 1)
                    if a is not None:
                        rotate(0)
                    if b is not None:
                        lane.wait(S.qfac_ready)
                        find_bias(0)
                        find_bias(1)
                    if a is not None:
                        lane.wait(S.squares_ready)
                        lane.wait(S.q_squares)
                        nc.vector.reduce_sum(S.sumsq[:], S.square[:], axis=AX.X).then_inc(S.sums_ready, 1)
                    for k in range(PIECES):
                        if b is not None:
                            copy_probs(k)
                            if k + 2 < PIECES:
                                find_bias(k + 2)
                        if a is not None and k == 0:
                            rotate(1)
                    if b is not None:
                        lane.seq(nc.vector.reciprocal(S.rrow[:], S.rowsum[:]))
                        lane.wait(S.out_ready)
                        nc.vector.tensor_tensor(S.o[:].rearrange("p (h d) -> p h d", d=LD),
                                                out.rearrange("p (h d) -> p h d", d=LD), spread(S.rrow[:], LD),
                                                ALU.mult).then_inc(S.o_ready, 1)
                    lane.skip(S.ring_freed, (A_RING - 4 if a is not None else 0) + (C_RING if c is not None else 0))
                S.steps(lane, body)
                S.check(lane)


class LocalFfn:

    def __init__(self, nc, g, L, ctx):
        self.nc, self.g, self.L = nc, g, L

        def sb(n, shape, dt=fp32):
            return ctx.enter_context(nc.sbuf_tensor(f"lf_{n}", shape, dt))
        self.xs = sb("xs", [C, 2, QB])
        self.stats = sb("stats", [P, 4, 6])
        self.meanvar = sb("meanvar", [P, 2, 4, 2])
        self.rstd = sb("rstd", [P, 2, 4])
        self.xn = sb("xn", [P, 2, 4, C])
        self.xnT = sb("xnT", [C, QB])
        self.gelu = sb("gelu", [P, 2, QB])
        self.h = sb("h", [P, len(FCH), QB])
        self.xs_ready = nc.alloc_semaphore("lf_xs_ready")
        self.turned = nc.alloc_semaphore("lf_turned")
        self.stats_ready = nc.alloc_semaphore("lf_stats_ready")
        self.rstd_ready = nc.alloc_semaphore("lf_rstd_ready")
        self.xn_ready = nc.alloc_semaphore("lf_xn_ready")
        self.xn_turned = nc.alloc_semaphore("lf_xn_turned")
        self.xnT_ready = nc.alloc_semaphore("lf_xnT_ready")
        self.gate_ready = nc.alloc_semaphore("lf_gate_ready")
        self.gelu_ready = nc.alloc_semaphore("lf_gelu_ready")
        self.a_ready = nc.alloc_semaphore("lf_a_ready")
        self.h_ready = nc.alloc_semaphore("lf_h_ready")
        self.y_ready = nc.alloc_semaphore("lf_y_ready")
        self.y_added = nc.alloc_semaphore("lf_y_added")
        self.dve_steps = nc.alloc_semaphore("lf_dve_steps")
        self.pool_steps = nc.alloc_semaphore("lf_pool_steps")

    def run(self, layer):
        nc, g, L, S = self.nc, self.g, self.L, self
        bank = L.bank
        TURN, BACK, GATE, AFACT, Y = 0, 2, 3, 5, 7
        NCH = len(FCH)

        def upto(sem, per_block, n):
            return layer * (per_block * NB) + n

        def tokens(b):
            return slice(LEFT + b * QB, LEFT + (b + 1) * QB)
        with nc.Block() as block:
            @block.sync
            def _(sp):
                for dst, src in ((L.wqkv[:], "h_lw_wqkv"), (L.wo[:], "h_lw_wo"), (L.scales[:], "h_lw_scales")):
                    sp.dma_start(dst, L.d[src][layer + 1]).then_inc(L.w_loaded, 16)
                sp.wait_ge(L.w_loaded, 16 * 3 * (layer + 1))
                hold(sp, L.held_sp)

            @block.gpsimd
            def _(pool):
                lane = Lane(pool, S.pool_steps, {S.pool_steps: layer * 2 * NB})

                def shifted(b):
                    if b >= 2:
                        pool.wait_ge(S.turned, upto(S.turned, 1, b - 1))
                    shift_copy(nc, lane, L.held, S.xs[:, b % 2, :], L.xb, b * QB, QB, S.xs_ready)
                    pool.wait_ge(S.xs_ready, upto(S.xs_ready, 1, b + 1))
                shifted(0)
                for b in range(NB):
                    pool.wait_ge(S.stats_ready, upto(S.stats_ready, 1, b + 1))
                    hold(pool, L.held)
                    lane.seq(nc.gpsimd.tensor_scalar(S.rstd[:, b % 2, :], S.meanvar[:, b % 2, :, 1], LN_EPS, None, ALU.add))
                    nc.gpsimd.tensor_tensor(S.rstd[:, b % 2, :], S.rstd[:, b % 2, :], L.minus_half[:, 0:4],
                                            ALU.pow).then_inc(S.rstd_ready, 1)
                    pool.wait_ge(S.rstd_ready, upto(S.rstd_ready, 1, b + 1))
                    if b + 1 < NB:
                        hold(pool, L.held)
                        shifted(b + 1)

            @block.tensor
            def _(pe):
                def turn(b):
                    pe.wait_ge(S.xs_ready, upto(S.xs_ready, 1, b + 1))
                    if b >= 2:
                        pe.wait_ge(S.xn_ready, upto(S.xn_ready, 1, b - 1))
                    for t in range(4):
                        last = nc.tensor.transpose(bank[:, TURN + b % 2, t * P:(t + 1) * P],
                                                   S.xs[:, b % 2, t * P:(t + 1) * P], g.ident[:])
                    last.then_inc(S.turned, 1)
                turn(0)
                for b in range(NB):
                    pe.wait_ge(S.xn_ready, upto(S.xn_ready, 1, b + 1))
                    for t in range(4):
                        last = nc.tensor.transpose(bank[:, BACK, t * P:(t + 1) * P], S.xn[:, b % 2, t, :], g.ident[:])
                    last.then_inc(S.xn_turned, 1)
                    if b + 1 < NB:
                        turn(b + 1)
                    pe.wait_ge(S.xnT_ready, upto(S.xnT_ready, 1, b + 1))
                    for j, (at, n) in enumerate(FCH):
                        c = NCH * b + j
                        if c >= 2:
                            pe.wait_ge(S.gelu_ready, upto(S.gelu_ready, NCH, c - 1))
                        nc.tensor.matmul(bank[0:n, GATE + c % 2, :], L.w1[:, FI + at:FI + at + n], S.xnT[:],
                                         start=True, stop=True).then_inc(S.gate_ready, 1)
                        if c >= 2:
                            pe.wait_ge(S.h_ready, upto(S.h_ready, NCH, c - 1))
                        nc.tensor.matmul(bank[0:n, AFACT + c % 2, :], L.w1[:, at:at + n], S.xnT[:],
                                         start=True, stop=True).then_inc(S.a_ready, 1)
                    if b:
                        pe.wait_ge(S.y_added, upto(S.y_added, 1, b))
                    for j, (at, n) in enumerate(FCH):
                        pe.wait_ge(S.h_ready, upto(S.h_ready, NCH, NCH * b + j + 1))
                        last = nc.tensor.matmul(bank[:, Y, :], L.w2[0:n, j, :], S.h[0:n, j, :],
                                                start=j == 0, stop=j == NCH - 1)
                    last.then_inc(S.y_ready, 1)

            @block.scalar
            def _(act):
                for b in range(NB):
                    act.wait_ge(S.xn_turned, upto(S.xn_turned, 1, b + 1))
                    if b:
                        act.wait_ge(S.a_ready, upto(S.a_ready, NCH, NCH * b))
                    nc.scalar.activation(S.xnT[:], bank[:, BACK, :], ACT.Identity, bias=L.cols[:, 1:2],
                                         scale=L.cols[:, 0:1]).then_inc(S.xnT_ready, 1)
                    for j, (at, n) in enumerate(FCH):
                        c = NCH * b + j
                        act.wait_ge(S.gate_ready, upto(S.gate_ready, NCH, c + 1))
                        if c >= 2:
                            act.wait_ge(S.h_ready, upto(S.h_ready, NCH, c - 1))
                        nc.scalar.activation(S.gelu[0:n, c % 2, :], bank[0:n, GATE + c % 2, :], ACT.Gelu,
                                             bias=L.cols[0:n, 3 + NCH + j:4 + NCH + j]).then_inc(S.gelu_ready, 1)

            @block.vector
            def _(dve):
                lane = Lane(dve, S.dve_steps, {S.dve_steps: layer * 4 * NB})

                def normalise(b):
                    dve.wait_ge(S.turned, upto(S.turned, 1, b + 1))
                    src = bank[:, TURN + b % 2, :].rearrange("p (t c) -> p t c", c=C)
                    for t in range(4):
                        lane.post(nc.vector.bn_stats(S.stats[:, t, :], src[:, t, :]))
                    lane.settle()
                    hold(dve, L.held)
                    for t in range(4):
                        last = nc.vector.bn_aggr(S.meanvar[:, b % 2, t, :], S.stats[:, t, :])
                    last.then_inc(S.stats_ready, 1)
                    dve.wait_ge(S.stats_ready, upto(S.stats_ready, 1, b + 1))
                    dve.wait_ge(S.rstd_ready, upto(S.rstd_ready, 1, b + 1))
                    if b >= 2:
                        dve.wait_ge(S.xn_turned, upto(S.xn_turned, 1, b - 1))
                    for t in range(4):
                        last = nc.vector.tensor_scalar(S.xn[:, b % 2, t, :], src[:, t, :], S.meanvar[:, b % 2, t, 0:1],
                                                       S.rstd[:, b % 2, t:t + 1], ALU.subtract, ALU.mult)
                    last.then_inc(S.xn_ready, 1)
                normalise(0)
                for b in range(NB):
                    if b + 1 < NB:
                        normalise(b + 1)
                    for j, (at, n) in enumerate(FCH):
                        c = NCH * b + j
                        dve.wait_ge(S.a_ready, upto(S.a_ready, NCH, c + 1))
                        dve.wait_ge(S.gelu_ready, upto(S.gelu_ready, NCH, c + 1))
                        nc.vector.scalar_tensor_tensor(S.h[0:n, j, :], bank[0:n, AFACT + c % 2, :], L.cols[0:n, 3 + j:4 + j],
                                                       S.gelu[0:n, c % 2, :], ALU.add, ALU.mult).then_inc(S.h_ready, 1)
                    dve.wait_ge(S.y_ready, upto(S.y_ready, 1, b + 1))
                    nc.vector.scalar_tensor_tensor(L.xa[:, tokens(b)], bank[:, Y, :], L.cols[:, 2:3], L.xb[:, tokens(b)],
                                                   ALU.add, ALU.add).then_inc(S.y_added, 1)


DI = 256
DT = DI // P
NS = 16
RANK = 8
TAPS = 4
SERIES_BELOW = 0.01


def stage_l2_attn(nc, g, d, y):
    with ExitStack() as ctx:
        def sb(n, shape, dt=fp32):
            return ctx.enter_context(nc.sbuf_tensor(f"l2a_{n}", shape, dt))
        shapes = {"w_in": [C, 4 * P], "w_out": [P, DT, C], "xproj": [P, DT, RANK + 2 * NS], "w_dt": [RANK, DI],
                  "cols": [P, DT, TAPS + 3], "a_log": [P, DT, NS]}
        w = {n: sb(n, s) for n, s in shapes.items()}
        select = sb("select", [P, NS, P])
        bT, cT = sb("bT", [P, T]), sb("cT", [P, T])
        with nc.Block() as block:
            @block.vector
            def _(dve):
                nc.vector.memset(select[:], 0.0)

            @block.gpsimd
            def _(pool):
                nc.gpsimd.memset(bT[:], 0.0)
                nc.gpsimd.memset(cT[:], 0.0)

        load(nc, "l2a", [(t[:], d["h_l2_" + n]) for n, t in w.items()] + [(select[0:NS], d["c_select16"])])
        xc, zs = sb("xc", [P, DT, T]), sb("zs", [P, DT, T])
        step, dx = sb("step", [P, DT, T]), sb("dx", [P, DT, T])
        ysum = sb("ysum", [P, DT, T])
        scan_inputs(nc, g, w, xc, zs)
        scan_steps(nc, g, w, xc, step, dx, bT, cT)
        scan_states(nc, g, w, select, xc, zs, step, dx, bT, cT, ysum)
    layernorm(nc, g, "ln4", feature=g.delta)


def scan_inputs(nc, g, w, xc, zs):
    with ExitStack() as ctx:
        def sb(n, shape, dt=fp32):
            return ctx.enter_context(nc.sbuf_tensor(f"si_{n}", shape, dt))

        def sem(n):
            return nc.alloc_semaphore(f"si_{n}")
        padded = sb("padded", [P, DT, TAPS - 1 + T])
        conv = sb("conv", [P, DT, T])
        acc = [ctx.enter_context(nc.psum_tensor(f"si_acc{i}", [P, NB, QB], fp32)) for i in range(2)]
        made, taken = sem("made"), sem("taken")
        conv_ready = sem("conv_ready")
        z_taken = sem("z_taken")
        own = sem("dve_steps")
        block = ctx.enter_context(nc.Block())

        def flat(i):
            return acc[i][:, :, :].rearrange("p b q -> p (b q)")

        @block.tensor
        def _(pe):
            for m in range(2 * DT):
                if m >= 2:
                    pe.wait_ge(taken, m - 1)
                for b in range(NB):
                    last = nc.tensor.matmul(acc[m % 2][:, b, :], w["w_in"][:, m * P:(m + 1) * P],
                                            g.xT[:, b * QB:(b + 1) * QB], start=True, stop=True)
                last.then_inc(made, 1)

        @block.vector
        def _(dve):
            lane = Lane(dve, own)
            lane.post(nc.vector.memset(padded[:, :, 0:TAPS - 1], 0.0))
            for m in range(DT):
                dve.wait_ge(made, m + 1)
                nc.vector.tensor_copy(padded[:, m, TAPS - 1:], flat(m)).then_inc(taken, 1)
            dve.wait_ge(taken, DT)
            lane.settle()
            for m in range(DT):
                lane.seq(nc.vector.tensor_scalar(conv[:, m, :], padded[:, m, 0:T], w["cols"][:, m, 0:1], None, ALU.mult))
                for j in range(1, TAPS):
                    ins = nc.vector.scalar_tensor_tensor(conv[:, m, :], padded[:, m, j:j + T], w["cols"][:, m, j:j + 1],
                                                         conv[:, m, :], ALU.mult, ALU.add)
                    if j < TAPS - 1:
                        lane.seq(ins)
                ins.then_inc(conv_ready, 1)

        @block.scalar
        def _(act):
            for m in range(DT):
                act.wait_ge(made, DT + m + 1)
                nc.scalar.activation(zs[:, m, :], flat(m), ACT.Silu)
            for m in range(DT):
                act.wait_ge(conv_ready, m + 1)
                nc.scalar.activation(xc[:, m, :], conv[:, m, :], ACT.Silu, bias=w["cols"][:, m, TAPS:TAPS + 1])


def scan_steps(nc, g, w, xc, step, dx, bT, cT):
    with ExitStack() as ctx:
        def sb(n, shape, dt=fp32):
            return ctx.enter_context(nc.sbuf_tensor(f"ss_{n}", shape, dt))

        def sem(n):
            return nc.alloc_semaphore(f"ss_{n}")
        low = sb("low", [RANK, T])
        raw, ex, one_ex = (sb(n, [P, DT, T]) for n in ("raw", "ex", "one_ex"))
        ps = [ctx.enter_context(nc.psum_tensor(f"ss_ps{i}", [P, NB, QB], fp32)) for i in range(2)]
        made, taken = sem("made"), sem("taken")
        low_ready = sem("low_ready")
        raw_ready, abs_ready, ex_ready, one_ready, ln_ready = (sem(n) for n in ("raw_ready", "abs_ready", "ex_ready", "one_ready", "ln_ready"))
        own = sem("dve_steps")
        block = ctx.enter_context(nc.Block())

        def flat(i, rows=P):
            return ps[i][0:rows, :, :].rearrange("p b q -> p (b q)")

        @block.tensor
        def _(pe):
            for n, (at, rows) in enumerate(((0, RANK), (RANK, NS), (RANK + NS, NS))):
                if n >= 2:
                    pe.wait_ge(taken, n - 1)
                for b in range(NB):
                    for m in range(DT):
                        last = nc.tensor.matmul(ps[n % 2][0:rows, b, :], w["xproj"][:, m, at:at + rows],
                                                xc[:, m, b * QB:(b + 1) * QB], start=m == 0, stop=m == DT - 1)
                last.then_inc(made, 1)
            for m in range(DT):
                pe.wait_ge(taken, 2 + m)
                for b in range(NB):
                    last = nc.tensor.matmul(ps[(m + 1) % 2][:, b, :], w["w_dt"][:, m * P:(m + 1) * P],
                                            low[:, b * QB:(b + 1) * QB], start=True, stop=True)
                last.then_inc(made, 1)

        @block.vector
        def _(dve):
            lane = Lane(dve, own)
            for n, (dst, rows) in enumerate(((low, RANK), (bT, NS), (cT, NS))):
                dve.wait_ge(made, n + 1)
                nc.vector.tensor_copy(dst[0:rows], flat(n % 2, rows)).then_inc(taken, 1)
            for m in range(DT):
                dve.wait_ge(made, 4 + m)
                nc.vector.tensor_scalar(raw[:, m, :], flat((m + 1) % 2), w["cols"][:, m, TAPS + 1:TAPS + 2], None,
                                        ALU.add).then_inc(raw_ready, 1)
            dve.wait_ge(ex_ready, 1)
            lane.post(nc.vector.tensor_scalar(dx[:], ex[:], -0.25, 1.0 / 3.0, ALU.mult, ALU.add))
            nc.vector.tensor_scalar(one_ex[:], ex[:], 1.0, None, ALU.add).then_inc(one_ready, 1)
            lane.settle()
            lane.seq(nc.vector.tensor_tensor(dx[:], dx[:], ex[:], ALU.mult))
            lane.seq(nc.vector.scalar_tensor_tensor(dx[:], dx[:], -0.5, ex[:], ALU.add, ALU.mult))
            lane.seq(nc.vector.scalar_tensor_tensor(dx[:], dx[:], 1.0, ex[:], ALU.add, ALU.mult))
            dve.wait_ge(ln_ready, 1)
            lane.seq(nc.vector.tensor_tensor(dx[:], dx[:], step[:], ALU.subtract))
            lane.seq(nc.vector.scalar_tensor_tensor(dx[:], ex[:], SERIES_BELOW, dx[:], ALU.is_lt, ALU.mult))
            lane.seq(nc.vector.scalar_tensor_tensor(step[:], raw[:], 0.0, step[:], ALU.max, ALU.add))
            lane.seq(nc.vector.tensor_tensor(step[:], step[:], dx[:], ALU.add))
            nc.vector.tensor_tensor(dx[:], step[:], xc[:], ALU.mult)

        @block.scalar
        def _(act):
            act.wait_ge(raw_ready, DT)
            nc.scalar.activation(ex[:], raw[:], ACT.Abs).then_inc(abs_ready, 1)
            act.wait_ge(abs_ready, 1)
            nc.scalar.activation(ex[:], ex[:], ACT.Exp, scale=-1.0).then_inc(ex_ready, 1)
            act.wait_ge(one_ready, 1)
            nc.scalar.activation(step[:], one_ex[:], ACT.Ln).then_inc(ln_ready, 1)


def scan_states(nc, g, w, select, xc, zs, step, dx, bT, cT, ysum):
    HB = 3
    with ExitStack() as ctx:
        def sb(n, shape, dt=fp32):
            return ctx.enter_context(nc.sbuf_tensor(f"st_{n}", shape, dt))

        def sem(n):
            return nc.alloc_semaphore(f"st_{n}")
        a = sb("a", [P, DT, NS])
        bn, cn = sb("bn", [P, 2, T]), sb("cn", [P, 2, T])
        decay = sb("decay", [P, 2, T])
        h = g.delta
        hc2 = sb("hc", [P, 2, T])
        hc = (hc2[:, 0, :], hc2[:, 1, :], g.xT[:])
        bps = ctx.enter_context(nc.psum_tensor("st_bps", [P, NB, QB], fp32))
        cps = ctx.enter_context(nc.psum_tensor("st_cps", [P, NB, QB], fp32))
        a_exp, a_ready = sem("a_exp"), sem("a_ready")
        spread_ready = sem("spread_ready")
        spread_copied = sem("spread_copied")
        decay_ready = sem("decay_ready")
        scanned = sem("scanned")
        hc_ready = sem("hc_ready")
        added = sem("added")
        pool_product = sem("pool_product")
        y_ready = sem("y_ready")
        out_ready = sem("out_ready")
        own = sem("dve_steps")
        block = ctx.enter_context(nc.Block())

        def by_pool(k):
            return 0 < k < DT * NS and k % 3 == 2

        @block.tensor
        def _(pe):
            for n in range(NS):
                for i, (ps, src) in enumerate(((bps, bT), (cps, cT))):
                    if n:
                        pe.wait_ge(spread_copied, 2 * n - 1 + i)
                    for b in range(NB):
                        last = nc.tensor.matmul(ps[:, b, :], select[:, n, :], src[:, b * QB:(b + 1) * QB],
                                                start=True, stop=True)
                    last.then_inc(spread_ready, 1)
            pe.wait_ge(y_ready, DT)
            pe.wait_ge(spread_copied, 2 * NS)
            for b in range(NB):
                for m in range(DT):
                    last = nc.tensor.matmul(bps[:, b, :], w["w_out"][:, m, :], ysum[:, m, b * QB:(b + 1) * QB],
                                            start=m == 0, stop=m == DT - 1)
            last.then_inc(out_ready, 1)

        @block.scalar
        def _(act):
            nc.scalar.activation(a[:], w["a_log"][:], ACT.Exp).then_inc(a_exp, 1)
            act.wait_ge(a_ready, 1)
            for n in range(NS):
                for i, (ps, dst) in enumerate(((bps, bn), (cps, cn))):
                    act.wait_ge(spread_ready, 2 * n + i + 1)
                    if n >= 2:
                        act.wait_ge(hc_ready, DT * (n - 1))
                    nc.scalar.copy(dst[:, n % 2, :], ps[:, :, :].rearrange("p b q -> p (b q)")).then_inc(spread_copied, 1)
                for m in range(DT):
                    k = DT * n + m
                    if k >= 2:
                        act.wait_ge(scanned, k - 1)
                    nc.scalar.activation(decay[:, k % 2, :], step[:, m, :], ACT.Exp,
                                         scale=a[:, m, n:n + 1]).then_inc(decay_ready, 1)

        @block.vector
        def _(dve):
            lane = Lane(dve, own)
            dve.wait_ge(a_exp, 1)
            nc.vector.tensor_scalar(a[:], a[:], -1.0, None, ALU.mult).then_inc(a_ready, 1)
            products = 0
            for n in range(NS):
                dve.wait_ge(spread_copied, 2 * n + 2)
                for m in range(DT):
                    k = DT * n + m
                    if by_pool(k):
                        products += 1
                        dve.wait_ge(pool_product, products)
                    else:
                        if k >= HB:
                            dve.wait_ge(added, k - HB + 1)
                        lane.seq(nc.vector.tensor_tensor(hc[k % HB], dx[:, m, :], bn[:, n % 2, :], ALU.mult))
                    dve.wait_ge(decay_ready, k + 1)
                    if k:
                        dve.wait_ge(hc_ready, k)
                    nc.vector.tensor_tensor_scan(h[:], decay[:, k % 2, :], hc[k % HB], 0.0,
                                                 ALU.mult, ALU.add).then_inc(scanned, 1)
                    dve.wait_ge(scanned, k + 1)
                    nc.vector.tensor_tensor(hc[k % HB], h[:], cn[:, n % 2, :], ALU.mult).then_inc(hc_ready, 1)
            dve.wait_ge(added, DT * NS)
            for m in range(DT):
                lane.seq(nc.vector.scalar_tensor_tensor(ysum[:, m, :], xc[:, m, :], w["cols"][:, m, TAPS + 2:TAPS + 3],
                                                        ysum[:, m, :], ALU.mult, ALU.add))
                nc.vector.tensor_tensor(ysum[:, m, :], ysum[:, m, :], zs[:, m, :], ALU.mult).then_inc(y_ready, 1)
            dve.wait_ge(out_ready, 1)
            nc.vector.tensor_copy(g.delta[:], bps[:, :, :].rearrange("p b q -> p (b q)"))

        @block.gpsimd
        def _(pool):
            for k in range(DT * NS):
                m = k % DT
                j = k + 2
                if by_pool(j):
                    pool.wait_ge(spread_copied, 2 * (j // DT) + 1)
                    if j >= HB:
                        pool.wait_ge(added, j - HB + 1)
                    nc.gpsimd.tensor_tensor(hc[j % HB], dx[:, j % DT, :], bn[:, j // DT % 2, :],
                                            ALU.mult).then_inc(pool_product, 1)
                pool.wait_ge(hc_ready, k + 1)
                if k < DT:
                    nc.gpsimd.tensor_copy(ysum[:, m, :], hc[k % HB]).then_inc(added, 1)
                else:
                    pool.wait_ge(added, k - 1)
                    nc.gpsimd.tensor_tensor(ysum[:, m, :], hc[k % HB], ysum[:, m, :], ALU.add).then_inc(added, 1)


def stage_l2_ffn(nc, g, d, y):
    with ExitStack() as ctx:
        def sb(n, shape, dt=fp32):
            return ctx.enter_context(nc.sbuf_tensor(f"l2f_{n}", shape, dt))

        def sem(n):
            return nc.alloc_semaphore(f"l2f_{n}")
        w = {n: sb(n, [P, P]) for n in ("rT", "kT", "vT")}
        mu = sb("mu", [P, 4])
        load(nc, "l2f", [(t[:], d["h_l2f_" + n]) for n, t in w.items()] + [(mu[:, 0:2], d["h_l2f_mu"])])
        mixed = sb("mixed", [P, 2, T])
        r = sb("r", [P, T])
        k = sb("k", [P, NB, QB])
        ps = ctx.enter_context(nc.psum_tensor("l2f_ps", [P, 2, NB, QB], fp32))
        mixed_ready = sem("mixed_ready")
        made, v_made = sem("made"), sem("v_made")
        sig, k_sq = sem("sig"), sem("k_sq")
        own, act_own = sem("dve_steps"), sem("act_steps")
        with nc.Block() as block:
            @block.vector
            def _(dve):
                lane = Lane(dve, own)
                lane.seq(nc.vector.tensor_scalar(mu[:, 2:4], mu[:, 0:2], -1.0, 1.0, ALU.mult, ALU.add))
                for i in range(2):
                    lane.seq(nc.vector.tensor_scalar(mixed[:, i, :], g.xT[:], mu[:, i:i + 1], None, ALU.mult))
                    nc.vector.scalar_tensor_tensor(mixed[:, i, 1:T], g.xT[:, 0:T - 1], mu[:, 2 + i:3 + i],
                                                   mixed[:, i, 1:T], ALU.mult, ALU.add).then_inc(mixed_ready, 1)
                for b in range(NB):
                    dve.wait_ge(v_made, b + 1)
                    s = slice(b * QB, (b + 1) * QB)
                    nc.vector.tensor_tensor(g.delta[:, s], ps[:, 1, b, :], r[:, s], ALU.mult)

            @block.tensor
            def _(pe):
                for i, n in enumerate(("rT", "kT")):
                    pe.wait_ge(mixed_ready, i + 1)
                    for b in range(NB):
                        nc.tensor.matmul(ps[:, i, b, :], w[n][:], mixed[:, i, b * QB:(b + 1) * QB],
                                         start=True, stop=True).then_inc(made, 1)
                for b in range(NB):
                    pe.wait_ge(k_sq, b + 1)
                    nc.tensor.matmul(ps[:, 1, b, :], w["vT"][:], k[:, b, :], start=True, stop=True).then_inc(v_made, 1)

            @block.scalar
            def _(act):
                act.wait_ge(made, NB)
                nc.scalar.activation(r[:], ps[:, 0].rearrange("p b q -> p (b q)"), ACT.Sigmoid).then_inc(act_own, 1)
                for b in range(NB):
                    act.wait_ge(made, NB + b + 1)
                    nc.scalar.activation(k[:, b, :], ps[:, 1, b, :], ACT.Relu).then_inc(act_own, 1)
                    act.wait_ge(act_own, b + 2)
                    nc.scalar.activation(k[:, b, :], k[:, b, :], ACT.Square).then_inc(k_sq, 1)
    layernorm(nc, g, "ln5", feature=g.delta)


HI = 352
HT = 3
FP4_BLOCK = 16


def quantise(nc, lane, x, out, scale, inv, a, hi, absolute, absolute_ready, sign, sign_ready, n):
    lane.eng.wait_ge(absolute_ready, n)
    lane.seq(nc.vector.reduce_max(scale, absolute, axis=AX.X))
    lane.seq(nc.vector.tensor_scalar(scale, scale, 1.0 / 6.0, 1e-12, ALU.mult, ALU.max))
    lane.seq(nc.vector.reciprocal(inv, scale))
    lane.seq(nc.vector.tensor_tensor(a, absolute, spread(inv, FP4_BLOCK), ALU.mult))
    lane.post(nc.vector.tensor_scalar(hi, a, 5.0, 2.0, ALU.is_gt, ALU.mult))
    lane.seq(nc.vector.tensor_scalar(out, a, 0.25, None, ALU.is_gt))
    for high, low in ((3.5, 0.75), (2.5, 1.25)):
        lane.post(nc.vector.scalar_tensor_tensor(hi, a, high, hi, ALU.is_gt, ALU.add))
        lane.seq(nc.vector.scalar_tensor_tensor(out, a, low, out, ALU.is_gt, ALU.add))
    lane.seq(nc.vector.scalar_tensor_tensor(out, a, 1.75, out, ALU.is_gt, ALU.add))
    lane.seq(nc.vector.scalar_tensor_tensor(out, hi, 2.0, out, ALU.mult, ALU.add))
    lane.post(nc.vector.tensor_scalar(scale, scale, 0.5, None, ALU.mult))
    lane.eng.wait_ge(sign_ready, n)
    lane.seq(nc.vector.tensor_tensor(out, out, sign, ALU.mult))
    return nc.vector.tensor_tensor(out, out, spread(scale, FP4_BLOCK), ALU.mult)


def stage_l3_ffn(nc, g, d, y):
    with ExitStack() as ctx:
        def sb(n, shape, dt=fp32):
            return ctx.enter_context(nc.sbuf_tensor(f"l3f_{n}", shape, dt))
        WC = 2 * HT * C + HI
        raw = sb("raw", [P, WC + NT * C])
        out = sb("out", [P, WC + NT * C])
        load(nc, "l3f", [(raw[:, 0:WC], d["h_l3f_w"])])
        wT = sb("wT", [P, 2 * HT, P])
        wdT = sb("wdT", [P, HT, C])
        xqT = sb("xqT", [C, T])
        quantise_inputs(nc, g, raw, out, WC, wT, wdT, xqT)
        gated_ffn(nc, g, wT, wdT, xqT)
    layernorm(nc, g, "ln7", token=g.delta[:].rearrange("p (t c) -> p t c", c=C), out_dram=y)


def quantise_inputs(nc, g, raw, out, WC, wT, wdT, xqT):
    with ExitStack() as ctx:
        def sb(n, shape, dt=fp32):
            return ctx.enter_context(nc.sbuf_tensor(f"qi_{n}", shape, dt))

        def sem(n):
            return nc.alloc_semaphore(f"qi_{n}")
        total = WC + NT * C
        absolute, a, hi, sign = (sb(n, [P, total]) for n in ("absolute", "a", "hi", "sign"))
        scale, inv = sb("scale", [P, total // FP4_BLOCK]), sb("inv", [P, total // FP4_BLOCK])
        wps = ctx.enter_context(nc.psum_tensor("qi_wps", [P, 4, QB], fp32))
        xps = ctx.enter_context(nc.psum_tensor("qi_xps", [P, 4, QB], fp32))
        x_copied, absolute_ready, sign_ready, done = (sem(n) for n in ("x_copied", "absolute_ready", "sign_ready", "done"))
        turned, own, copied = sem("turned"), sem("dve_steps"), sem("copied")
        block = ctx.enter_context(nc.Block())

        def blocks(t):
            return t[:].rearrange("p (b k) -> p b k", k=FP4_BLOCK)

        @block.vector
        def _(dve):
            lane = Lane(dve, own)
            nc.vector.tensor_copy(raw[:, WC:], g.x[:].rearrange("p t c -> p (t c)")).then_inc(x_copied, 1)
            quantise(nc, lane, blocks(raw), blocks(out), scale[:], inv[:], blocks(a), blocks(hi),
                     blocks(absolute), absolute_ready, blocks(sign), sign_ready, 1).then_inc(done, 1)
            dve.wait_ge(turned, 1)
            nc.vector.tensor_copy(wT[:, 0:3, :], wps[:, 0, 0:3 * P].rearrange("p (t c) -> p t c", c=P))
            nc.vector.tensor_copy(wT[:, 3:6, :], wps[:, 1, 0:3 * P].rearrange("p (t c) -> p t c", c=P))
            nc.vector.tensor_copy(wdT[:, 0:2, :], wps[:, 2, 0:2 * P].rearrange("p (t c) -> p t c", c=P))
            nc.vector.tensor_copy(wdT[0:HI - 2 * P, 2, :], wps[0:HI - 2 * P, 2, 2 * P:3 * P])

        @block.scalar
        def _(act):
            act.wait_ge(x_copied, 1)
            nc.scalar.activation(absolute[:], raw[:], ACT.Abs).then_inc(absolute_ready, 1)
            nc.scalar.activation(sign[:], raw[:], ACT.Sign).then_inc(sign_ready, 1)
            act.wait_ge(turned, 2)
            nc.scalar.copy(xqT[:], xps[:, :, :].rearrange("p b q -> p (b q)"))

        @block.tensor
        def _(pe):
            pe.wait_ge(done, 1)
            for i in range(2):
                for t in range(HT):
                    nc.tensor.transpose(wps[:, i, t * P:(t + 1) * P], out[:, (i * HT + t) * C:(i * HT + t + 1) * C], g.ident[:])
            for t in range(HT):
                rows = min(P, HI - t * P)
                at = 2 * HT * C + t * P
                last = nc.tensor.transpose(wps[0:rows, 2, t * P:(t + 1) * P], out[:, at:at + rows], g.ident[:])
            last.then_inc(turned, 1)
            for t in range(NT):
                last = nc.tensor.transpose(xps[:, t // 4, (t % 4) * P:(t % 4 + 1) * P], out[:, WC + t * C:WC + (t + 1) * C], g.ident[:])
            last.then_inc(turned, 1)


def gated_ffn(nc, g, wT, wdT, xqT):
    with ExitStack() as ctx:
        def sb(n, shape, dt=fp32):
            return ctx.enter_context(nc.sbuf_tensor(f"gf_{n}", shape, dt))

        def sem(n):
            return nc.alloc_semaphore(f"gf_{n}")
        G = 4
        W = G * HI
        silu = sb("silu", [P, HI])
        h = sb("h", [P, 2, W])
        out = sb("out", [P, 2, W])
        absolute, sign = sb("absolute", [P, 2, W]), sb("sign", [P, 2, W])
        a, hi = sb("a", [P, W]), sb("hi", [P, W])
        scale, inv = sb("scale", [P, W // FP4_BLOCK]), sb("inv", [P, W // FP4_BLOCK])
        hT = sb("hT", [P, 2, HT, P])
        gate_ps = ctx.enter_context(nc.psum_tensor("gf_gate", [P, 2, QB], fp32))
        up_ps = ctx.enter_context(nc.psum_tensor("gf_up", [P, 2, QB], fp32))
        hT_ps = ctx.enter_context(nc.psum_tensor("gf_hT_bank", [P, 2, QB], fp32))
        y_ps = ctx.enter_context(nc.psum_tensor("gf_y", [P, 2, QB], fp32))
        made = sem("made")
        silu_ready = sem("silu_ready")
        h_ready = sem("h_ready")
        absolute_ready, sign_ready = sem("absolute_ready"), sem("sign_ready")
        quantised = sem("quantised")
        turned = sem("turned")
        hT_copied = sem("hT_copied")
        y_made = sem("y_made")
        y_copied = sem("y_copied")
        own, own_act = sem("dve_steps"), sem("act_steps")
        block = ctx.enter_context(nc.Block())
        groups = NT // G

        def blocks(t):
            return t.rearrange("p (b k) -> p b k", k=FP4_BLOCK)

        @block.tensor
        def _(pe):
            def up(k):
                for t in range(k * G, (k + 1) * G):
                    if t >= 2:
                        pe.wait_ge(h_ready, t - 1)
                    s = slice(t * P, (t + 1) * P)
                    nc.tensor.matmul(gate_ps[:, t % 2, 0:HI], xqT[:, s], wT[:, 0:3, :].rearrange("p t c -> p (t c)")[:, 0:HI],
                                     start=True, stop=True)
                    nc.tensor.matmul(up_ps[:, t % 2, 0:HI], xqT[:, s], wT[:, 3:6, :].rearrange("p t c -> p (t c)")[:, 0:HI],
                                     start=True, stop=True).then_inc(made, 1)

            def down(k):
                pe.wait_ge(quantised, k + 1)
                for t in range(k * G, (k + 1) * G):
                    at = (t % G) * HI
                    if t >= 2:
                        pe.wait_ge(hT_copied, t - 1)
                    for j in range(HT):
                        rows = min(P, HI - j * P)
                        last = nc.tensor.transpose(hT_ps[0:rows, t % 2, j * P:(j + 1) * P],
                                                   out[:, k % 2, at + j * P:at + j * P + rows], g.ident[:])
                    last.then_inc(turned, 1)
                    pe.wait_ge(hT_copied, t + 1)
                    if t >= 2:
                        pe.wait_ge(y_copied, t - 1)
                    for j in range(HT):
                        rows = min(P, HI - j * P)
                        last = nc.tensor.matmul(y_ps[:, t % 2, 0:C], hT[0:rows, t % 2, j, :], wdT[0:rows, j, :],
                                                start=j == 0, stop=j == HT - 1)
                    last.then_inc(y_made, 1)
            up(0)
            for k in range(groups):
                if k + 1 < groups:
                    up(k + 1)
                down(k)

        @block.scalar
        def _(act):
            def silus(k):
                for t in range(k * G, (k + 1) * G):
                    act.wait_ge(made, t + 1)
                    if t >= 1:
                        act.wait_ge(h_ready, t)
                    nc.scalar.activation(silu[:], gate_ps[:, t % 2, 0:HI], ACT.Silu).then_inc(silu_ready, 1)
                act.wait_ge(h_ready, (k + 1) * G)
                if k >= 2:
                    act.wait_ge(quantised, k - 1)
                nc.scalar.activation(absolute[:, k % 2, :], h[:, k % 2, :], ACT.Abs).then_inc(absolute_ready, 1)
                nc.scalar.activation(sign[:, k % 2, :], h[:, k % 2, :], ACT.Sign).then_inc(sign_ready, 1)

            def copies(k):
                for t in range(k * G, (k + 1) * G):
                    act.wait_ge(turned, t + 1)
                    nc.scalar.copy(hT[:, t % 2, 0:2, :], hT_ps[:, t % 2, 0:2 * P].rearrange("p (t c) -> p t c", c=P)).then_inc(own_act, 1)
                    nc.scalar.copy(hT[0:HI - 2 * P, t % 2, 2, :], hT_ps[0:HI - 2 * P, t % 2, 2 * P:3 * P]).then_inc(hT_copied, 1)
                    act.wait_ge(y_made, t + 1)
                    nc.scalar.copy(g.delta[:, t * C:(t + 1) * C], y_ps[:, t % 2, 0:C]).then_inc(y_copied, 1)
            silus(0)
            for k in range(groups):
                if k + 1 < groups:
                    silus(k + 1)
                copies(k)

        @block.vector
        def _(dve):
            lane = Lane(dve, own)

            def products(k):
                for t in range(k * G, (k + 1) * G):
                    dve.wait_ge(silu_ready, t + 1)
                    at = (t % G) * HI
                    nc.vector.tensor_tensor(h[:, k % 2, at:at + HI], up_ps[:, t % 2, 0:HI], silu[:], ALU.mult).then_inc(h_ready, 1)

            def quantised_group(k):
                quantise(nc, lane, None, blocks(out[:, k % 2, :]), scale[:], inv[:], blocks(a[:]), blocks(hi[:]),
                         blocks(absolute[:, k % 2, :]), absolute_ready, blocks(sign[:, k % 2, :]), sign_ready,
                         k + 1).then_inc(quantised, 1)
                dve.wait_ge(quantised, k + 1)
            products(0)
            for k in range(groups):
                if k + 1 < groups:
                    products(k + 1)
                if k >= 2:
                    dve.wait_ge(turned, G * (k - 1))
                quantised_group(k)


KEY_SCALE_MAX = float(np.log(2 ** 16 - 1))
HEAD_STEPS = {"l0": 34, "l1": 16}


class Shared:
    pass


def load(nc, name, pairs):
    loaded = nc.alloc_semaphore(f"{name}_loaded")
    with nc.Block() as block:
        half = (len(pairs) + 1) // 2

        @block.sync
        def _(sp):
            for dst, src in pairs[:half]:
                sp.dma_start(dst, src).then_inc(loaded, 16)
            sp.wait_ge(loaded, 16 * len(pairs))

        @block.scalar
        def _(act):
            for dst, src in pairs[half:]:
                act.dma_start(dst, src).then_inc(loaded, 16)


def build(nc, d, y, dbg=None, upto=99, only=None):
    ctx = ExitStack()
    with ctx:
        g = Shared()
        def keep(n, shape, dt=fp32):
            return ctx.enter_context(nc.sbuf_tensor(n, shape, dt))
        g.x = keep("x", [P, NT, C])
        g.xT = keep("xT", [C, T])
        g.delta = keep("delta", [P, T])
        consts = {"ident": [P, P], "ones": [P, P], "e012": [P, 1], "head_ones": [P, P],
                  "mask_strict_q": [P, P], "mask_strict_k": [P, P], "mask_q": [P, P], "mask_k": [P, P]}
        consts = {n: keep(n, shape) for n, shape in consts.items()}
        g.ident, g.ones, g.e012, g.head_ones = (consts[n] for n in ("ident", "ones", "e012", "head_ones"))
        g.mask_strict_q, g.mask_strict_k = consts["mask_strict_q"], consts["mask_strict_k"]
        g.mask_q, g.mask_k = consts["mask_q"], consts["mask_k"]
        load(nc, "consts", [(t[:], d["c_" + n]) for n, t in consts.items()]
             + [(g.x[:], d["L0_attn_x"].rearrange("b (t p) c -> p (b t) c", p=P)),
                (g.xT[:], d["h_xT"])])
        stages = [stage_l0_attn, stage_l0_ffn, stage_l1_attn, stage_l1_ffn,
                  stage_l2_attn, stage_l2_ffn, stage_l3_attn, stage_l3_ffn]
        for n, s in enumerate(stages):
            if n > upto or (only is not None and n != only):
                continue
            with nc.cleanup_on_exit():
                s(nc, g, d, y if n == 7 else None)
            nc.all_engine_barrier()
            if dbg is not None and (n == upto or n == only) and n < 7:
                load(nc, "debug", [(dbg.rearrange("(t p) c -> p t c", p=P), g.x[:])])


def stage_l0_attn(nc, g, d, y):
    with ExitStack() as ctx:
        def sb(n, shape, dt=fp32):
            return ctx.enter_context(nc.sbuf_tensor(f"l0a_{n}", shape, dt))
        names = {"kT": [P, P], "vT": [P, P], "beta": [P, 1], "key_scale": [P, 1], "v_coef": [P, 1], "val_scale": [P, 1]}
        w = {n: sb(n, shape) for n, shape in names.items()}
        wo = sb("wo", [8, 16, C])
        groups, head_mask = sb("groups", [P, 6, P]), sb("head_mask", [P, 16, 1])
        load(nc, "l0a", [(t[:], d["h_l0_" + n]) for n, t in w.items()]
             + [(wo[:], d["h_l0_wo"]), (groups[:], d["c_groups"]), (head_mask[:, :, 0], d["c_head_mask"])])
        hi, mid, lo = (sb(n, [P, T], bf16) for n in ("hi", "mid", "lo"))
        v_all = sb("v_all", [P, NT, 16, 8])
        zero(nc, "l0a", g.delta)
        with ExitStack() as ctx2:
            keys = ctx2.enter_context(nc.sbuf_tensor("l0a_keys", [C, T], fp32))
            values = ctx2.enter_context(nc.sbuf_tensor("l0a_values", [C, T], fp32))
            decayed_keys(nc, g, {n: t[:] for n, t in w.items()}, keys, values)
            split_keys(nc, g, "l0s", keys, values, hi, mid, lo, v_all[:, :, :, :].rearrange("p t h d -> p t (h d)"))
        head_attention(nc, g, "l0", 16, 8, 1.0, g.delta, wo, picked=(hi, mid, lo, v_all, groups, head_mask))
    layernorm(nc, g, "ln0", feature=g.delta)


def zero(nc, name, t):
    with nc.Block() as block:
        @block.vector
        def _(dve):
            nc.vector.memset(t[:], 0.0)


def stage_l1_attn(nc, g, d, y):
    with ExitStack() as ctx:
        def sb(n, shape, dt=fp32):
            return ctx.enter_context(nc.sbuf_tensor(f"l1a_{n}", shape, dt))
        w = sb("w", [P, 16, 320])
        wo = sb("wo", [64, 16, C])
        bias = sb("bias", [P, 1])
        cos, sin = sb("cos", [P, T]), sb("sin", [P, T])
        load(nc, "l1a", [(w[:], d["h_l1_w"]), (wo[:], d["h_l1_wo"]), (bias[:], d["h_l1_bo"]),
                         (cos[:], d["c_cos"]), (sin[:], d["c_sin"])])
        with nc.Block() as block:
            @block.vector
            def _(dve):
                nc.vector.tensor_copy(g.delta[:], bias[:, 0:1].to_broadcast([P, T]))
        head_attention(nc, g, "l1", 16, 64, 64 ** -0.5, g.delta, wo, rotary=(w, cos, sin))
    layernorm(nc, g, "ln2", feature=g.delta)


def stage_l3_attn(nc, g, d, y):
    with ExitStack() as ctx:
        w = ctx.enter_context(nc.sbuf_tensor("l3a_w", [P, 3 * C], fp32))
        load(nc, "l3a", [(w[:], d["h_l3_w"])])
        causal_attention(nc, g, "l3", w, 128 ** -0.5, g.delta)
    layernorm(nc, g, "ln6", feature=g.delta)




def constants():
    f = np.float32
    c = {}
    i = np.arange(P)
    c["ident"] = np.eye(P, dtype=f)
    c["ones"] = np.ones((P, P), f)
    c["e012"] = (i[:, None] < 3).astype(f)
    c["head_ones"] = (i[:, None] // 8 == i[None, :] // 8).astype(f)
    c["mask_strict_q"] = np.where(i[None, :] >= i[:, None], MASKED, 0).astype(f)
    c["mask_strict_k"] = np.ascontiguousarray(c["mask_strict_q"].T)
    c["mask_q"] = np.where(i[None, :] > i[:, None], MASKED, 0).astype(f)
    c["mask_k"] = np.ascontiguousarray(c["mask_q"].T)
    groups = np.zeros((P, 6, P), f)
    for n, (q, k) in enumerate(((0, 0), (0, 1), (1, 0), (1, 1), (0, 2), (2, 0))):
        for p in range(P):
            groups[p, q, 32 + 8 * n + p % 8] = 1
            groups[p, 3 + k, 32 + 8 * n + p % 8] = 1
    c["groups"] = groups
    c["head_mask"] = (i[:, None] // 8 == np.arange(16)[None, :]).astype(f)
    c["select16"] = np.repeat(np.eye(16, dtype=f)[:, :, None], P, axis=2)
    c["select8"] = np.repeat(np.eye(8, dtype=f)[:, :, None], P, axis=2)
    half = np.arange(32, dtype=f)
    theta = (f(1.0) / f(10000.0) ** (half / f(32))).astype(f)
    ang = (np.arange(T, dtype=f)[:, None] * theta[None, :]).astype(f)
    cos, sin = np.cos(ang).T.astype(f), np.sin(ang).T.astype(f)
    c["cos"] = np.concatenate([cos, cos, cos, cos])
    c["sin"] = np.concatenate([-sin, sin, -sin, sin])
    even = np.arange(0, LD, 2, dtype=f)
    ang = np.arange(T, dtype=f)[:, None] * (f(1.0) / f(10000.0) ** (even / f(LD)))[None, :]
    cos, sin = np.cos(ang.astype(f)).astype(np.float64), np.sin(ang.astype(f)).astype(np.float64)
    base = (even.astype(np.float64) + 0.4 * LD) / (1.4 * LD)
    power = (np.arange(T) % P)[:, None] / (WIN // 2)
    up, down = base[None, :] ** power, base[None, :] ** -power
    tabs = np.stack([np.concatenate([cos * up, cos * up], 1), np.concatenate([-sin * up, sin * up], 1),
                     np.concatenate([cos * down, cos * down], 1), np.concatenate([-sin * down, sin * down], 1)], axis=1)
    c["rope"] = tabs.reshape(NT, P, 4, LD).transpose(1, 0, 2, 3).astype(f)
    c["halo_scale"] = np.tile(base ** (P / (WIN // 2)), 4)[:, None].astype(f)
    key = np.arange(SPAN)
    seen = (key[None, :] >= i[:, None]) & (key[None, :] <= i[:, None] + WIN)
    c["band"] = np.stack([np.where(seen, 0, MASKED), np.where(seen & (key[None, :] >= WIN), 0, MASKED)], axis=1).astype(f)
    return c


def layouts(a):
    h = {}
    def col(v):
        return np.ascontiguousarray(v.reshape(-1, 1))
    x = a["L0_attn_x"]
    h["xT"] = np.ascontiguousarray(x[0].T)
    h["l0_kT"] = np.ascontiguousarray(a["L0_attn_W_k"].T)
    h["l0_vT"] = np.ascontiguousarray(a["L0_attn_W_v"].T)
    for n, k in (("beta", "leaky_key_beta"), ("key_scale", "key_scale"), ("v_coef", "v_coef"), ("val_scale", "val_scale")):
        h["l0_" + n] = col(np.repeat(a["L0_attn_" + k].reshape(16), 8))
    h["l0_wo"] = a["L0_attn_W_c"].T.reshape(16, 8, C).transpose(1, 0, 2)
    h["l0_bs"] = np.broadcast_to(a["L0_ffn_bs"], (P, NT, E_))
    h["l0_experts"] = np.concatenate([
        a["L0_ffn_W1"],
        a["L0_ffn_W2"].reshape(E_, FT, P, C).transpose(0, 2, 1, 3).reshape(E_, P, FT * C),
        a["L0_ffn_b1"].reshape(E_, FT, P).transpose(0, 2, 1),
        a["L0_ffn_b2"][:, :, None]], axis=2)
    swap = np.concatenate([np.arange(32, 64), np.arange(32)])
    def feature_tiles(v):
        return v.reshape(DT, P, -1).transpose(1, 0, 2)
    h["l2_w_in"] = a["L2_attn_W_in"]
    h["l2_w_out"] = feature_tiles(a["L2_attn_W_out"])
    h["l2_xproj"] = feature_tiles(a["L2_attn_W_xproj"])
    h["l2_w_dt"] = a["L2_attn_W_dt"]
    h["l2_a_log"] = feature_tiles(a["L2_attn_A_log"])
    h["l2_cols"] = np.concatenate([feature_tiles(a["L2_attn_W_conv"]), feature_tiles(a["L2_attn_b_conv"]),
                                   feature_tiles(a["L2_attn_b_dt"]), feature_tiles(a["L2_attn_D"])], axis=2)
    for n in "rkv":
        h[f"l2f_{n}T"] = a["L2_ffn_W_" + n].T
    h["l2f_mu"] = np.stack([a["L2_ffn_mu_r"], a["L2_ffn_mu_k"]], axis=1)
    def spare(v):
        return np.concatenate([v, np.zeros_like(v[:1])])
    h["lw_wqkv"] = spare(a["L1_ffn_Wqkv"])
    h["lw_wo"] = spare(a["L1_ffn_Wo"].reshape(DEPTH, INNER // P, P, C).transpose(0, 2, 1, 3))
    w2 = a["L1_ffn_W2"]
    w2 = np.concatenate([w2, np.zeros((DEPTH, len(FCH) * P - FI, C), w2.dtype)], axis=1)
    h["lw_w2"] = w2.reshape(DEPTH, len(FCH), P, C).transpose(0, 2, 1, 3)
    qs, ks = a["L1_ffn_q_scale"], a["L1_ffn_k_scale"]
    s4 = np.stack([qs, qs[:, swap], ks, ks[:, swap]], axis=1)
    h["lw_scales"] = spare(np.broadcast_to(s4[:, None], (DEPTH, P, 4, LD)))
    b1 = a["L1_ffn_b1"]
    pad = np.zeros((DEPTH, len(FCH) * P - FI), b1.dtype)
    b1 = np.concatenate([b1[:, :FI], pad, b1[:, FI:], pad], axis=1).reshape(DEPTH, 2 * len(FCH), P).transpose(0, 2, 1)
    h["lw_cols"] = np.concatenate([a["L1_ffn_ln_g"][:, :, None], a["L1_ffn_ln_b"][:, :, None],
                                   a["L1_ffn_b2"][:, :, None], b1], axis=2)
    rows = []
    for n in ("w_gate", "w_up"):
        v = a["L3_ffn_" + n]
        v = np.concatenate([v, np.zeros((HT * P - HI, C), v.dtype)])
        rows.append(v.reshape(HT, P, C).transpose(1, 0, 2).reshape(P, HT * C))
    h["l3f_w"] = np.concatenate(rows + [a["L3_ffn_w_down"]], axis=1)
    w = a["L1_attn_w_qkv"].reshape(C, 3, 16, 64)
    q, k, v = w[:, 0], w[:, 1], w[:, 2]
    h["l1_w"] = np.concatenate([q, k, q[:, :, swap], k[:, :, swap], v], axis=2)
    h["l1_wo"] = a["L1_attn_w_out"].reshape(16, 64, C).transpose(1, 0, 2)
    h["l1_bo"] = col(a["L1_attn_b_out"])
    h["l3_w"] = np.concatenate([a["L3_attn_W_Q"], a["L3_attn_W_K"], a["L3_attn_W_V"]], axis=1)
    return h




def kernel(**inputs):
    import concourse.bacc as bacc
    from concourse.bass_utils import run_bass_kernel_spmd

    a = {n: np.asarray(v) for n, v in inputs.items()}
    arrays = {"h_" + n: v for n, v in layouts(a).items()}
    arrays |= {"c_" + n: v for n, v in constants().items()}
    arrays |= {n: a[n] for n in ("L0_attn_x", "L0_ffn_Ws", "L1_ffn_W1")}
    arrays = {n: np.ascontiguousarray(v) for n, v in arrays.items()}
    nc = bacc.Bacc("TRN2", target_bir_lowering=False, num_devices=1)
    d = {n: nc.dram_tensor(n, v.shape, mybir.dt.from_np(v.dtype), kind="ExternalInput").ap() for n, v in arrays.items()}
    y = nc.dram_tensor("y", (T, C), fp32, kind="ExternalOutput").ap()
    build(nc, d, y)
    got = run_bass_kernel_spmd(nc, [arrays], core_ids=[0])
    return got.results[0]["y"].reshape(1, T, C)
```
